# Optimizing a Trainium2 kernel written in Bass

```python
import numpy as np
import jax
import jax.numpy as jnp

def _softmax(x, axis=-1):
    return jax.nn.softmax(x, axis=axis)

def _gelu(x):
    return jax.nn.gelu(x, approximate=True)

def _silu(x):
    return jax.nn.silu(x)

def _sigmoid(x):
    return jax.nn.sigmoid(x)

def _layernorm(x, axis=-1, eps=1e-05):
    m = jnp.mean(x, axis=axis, keepdims=True)
    v = jnp.var(x, axis=axis, keepdims=True)
    return (x - m) / jnp.sqrt(v + eps)

def _scatter_add(tgt, idx, src, axis=0):
    return tgt.at[idx].add(src)

def _segment_sum(src, seg, n):
    return jax.ops.segment_sum(src, seg, n)
kernel_name = 'mk_sandwich_d1_jaxref_r8_ffecd0'

def setup_inputs(seed: int=0):
    np.random.seed(seed)
    _w = jnp.asarray

    def _L0_attn_setup():
        import jax, jax.numpy as jnp
        import numpy as np
        HIDDEN = 256
        INTER = 512
        HEADS = 32
        HEAD_DIM = INTER // HEADS
        STATE = 128
        GROUPS = 1
        CONV_K = 4
        CHUNK = 32
        EPS = 1e-05
        CONV_DIM = INTER + 2 * GROUPS * STATE
        DT_MIN, DT_MAX = (0.0, 100.0)
        BATCH, SEQ = (2, 512)

        def _segment_sum(x):
            T = x.shape[-1]
            xx = jnp.broadcast_to(x[..., None], x.shape + (T,))
            mask_lower = jnp.tril(jnp.ones((T, T), bool), -1)
            xx = jnp.where(mask_lower, xx, 0.0)
            seg = jnp.cumsum(xx, axis=-2)
            mask_incl = jnp.tril(jnp.ones((T, T), bool), 0)
            return jnp.where(mask_incl, seg, -jnp.inf)
        key = jax.random.key(seed)
        ks = jax.random.split(key, 8)
        std = 0.02
        return {'hidden_states': jax.random.normal(ks[0], (BATCH, SEQ, HIDDEN), jnp.float32), 'in_proj_w': jax.random.normal(ks[1], (INTER + CONV_DIM + HEADS, HIDDEN), jnp.float32) * std, 'conv_w': jax.random.normal(ks[2], (CONV_DIM, 1, CONV_K), jnp.float32) * std, 'conv_b': jnp.zeros((CONV_DIM,), jnp.float32), 'A_log': jnp.log(jax.random.uniform(ks[3], (HEADS,), jnp.float32, 1.0, 16.0)), 'dt_bias': jax.random.normal(ks[4], (HEADS,), jnp.float32) * 0.1, 'D': jnp.ones((HEADS,), jnp.float32), 'norm_w': jnp.ones((INTER,), jnp.float32), 'out_proj_w': jax.random.normal(ks[5], (HIDDEN, INTER), jnp.float32) * (std / np.sqrt(48.0))}
    _L0_attn_in = _L0_attn_setup()

    def _L0_ffn_setup():
        import jax, jax.numpy as jnp
        import numpy as np
        H = 256
        HQ = 16
        HKV = 4
        D = 128
        E = 32
        K = 4
        I = 128
        ISH = 128
        EPS = 1e-06
        THETA = 10000.0
        NORM_MIN = 1e-12

        def rmsnorm(x, w):
            xf = x.astype(jnp.float32)
            var = jnp.mean(xf * xf, axis=-1, keepdims=True)
            return w * (xf * jax.lax.rsqrt(var + EPS))

        def rotate_half(x):
            x1 = x[..., 0::2]
            x2 = x[..., 1::2]
            return jnp.stack((-x2, x1), axis=-1).reshape(x.shape)
        key = jax.random.key(seed)
        ks = jax.random.split(key, 14)
        s = 0.02
        B, S = (1, 128)
        return {'hidden_states': jax.random.normal(ks[0], (B, S, H), jnp.float32), 'ln1_w': jnp.ones((H,), jnp.float32), 'ln2_w': jnp.ones((H,), jnp.float32), 'wq': jax.random.normal(ks[1], (H, HQ * D), jnp.float32) * s, 'wk': jax.random.normal(ks[2], (H, HKV * D), jnp.float32) * s, 'wv': jax.random.normal(ks[3], (H, HKV * D), jnp.float32) * s, 'wo': jax.random.normal(ks[4], (HQ * D, H), jnp.float32) * s, 'gate_w': jax.random.normal(ks[5], (E, H), jnp.float32) * s, 'bias_e': jnp.zeros((E,), jnp.float32), 'weg': jax.random.normal(ks[6], (E, H, I), jnp.float32) * s, 'weu': jax.random.normal(ks[7], (E, H, I), jnp.float32) * s, 'wed': jax.random.normal(ks[8], (E, I, H), jnp.float32) * s, 'wsg': jax.random.normal(ks[9], (H, ISH), jnp.float32) * s, 'wsu': jax.random.normal(ks[10], (H, ISH), jnp.float32) * s, 'wsd': jax.random.normal(ks[11], (ISH, H), jnp.float32) * s}
    _L0_ffn_in = _L0_ffn_setup()
    _d = {'L0_attn_hidden_states': _L0_attn_in['hidden_states'], 'L0_attn_in_proj_w': _L0_attn_in['in_proj_w'], 'L0_attn_conv_w': _L0_attn_in['conv_w'], 'L0_attn_conv_b': _L0_attn_in['conv_b'], 'L0_attn_A_log': _L0_attn_in['A_log'], 'L0_attn_dt_bias': _L0_attn_in['dt_bias'], 'L0_attn_D': _L0_attn_in['D'], 'L0_attn_norm_w': _L0_attn_in['norm_w'], 'L0_attn_out_proj_w': _L0_attn_in['out_proj_w'], 'L0_ffn_ln1_w': _L0_ffn_in['ln1_w'], 'L0_ffn_ln2_w': _L0_ffn_in['ln2_w'], 'L0_ffn_wq': _L0_ffn_in['wq'], 'L0_ffn_wk': _L0_ffn_in['wk'], 'L0_ffn_wv': _L0_ffn_in['wv'], 'L0_ffn_wo': _L0_ffn_in['wo'], 'L0_ffn_gate_w': _L0_ffn_in['gate_w'], 'L0_ffn_bias_e': _L0_ffn_in['bias_e'], 'L0_ffn_weg': _L0_ffn_in['weg'], 'L0_ffn_weu': _L0_ffn_in['weu'], 'L0_ffn_wed': _L0_ffn_in['wed'], 'L0_ffn_wsg': _L0_ffn_in['wsg'], 'L0_ffn_wsu': _L0_ffn_in['wsu'], 'L0_ffn_wsd': _L0_ffn_in['wsd']}
    _x0 = _d['L0_attn_hidden_states']
    _d['L0_attn_hidden_states'] = jax.random.normal(jax.random.fold_in(jax.random.key(seed), 1), (4, 512, 256), dtype=_x0.dtype)
    del _x0
    return _d

def reference(L0_attn_hidden_states, L0_attn_in_proj_w, L0_attn_conv_w, L0_attn_conv_b, L0_attn_A_log, L0_attn_dt_bias, L0_attn_D, L0_attn_norm_w, L0_attn_out_proj_w, L0_ffn_ln1_w, L0_ffn_ln2_w, L0_ffn_wq, L0_ffn_wk, L0_ffn_wv, L0_ffn_wo, L0_ffn_gate_w, L0_ffn_bias_e, L0_ffn_weg, L0_ffn_weu, L0_ffn_wed, L0_ffn_wsg, L0_ffn_wsu, L0_ffn_wsd):

    def _L0_attn_ref(hidden_states, in_proj_w, conv_w, conv_b, A_log, dt_bias, D, norm_w, out_proj_w):
        import jax, jax.numpy as jnp
        import numpy as np
        HIDDEN = 256
        INTER = 512
        HEADS = 32
        HEAD_DIM = INTER // HEADS
        STATE = 128
        GROUPS = 1
        CONV_K = 4
        CHUNK = 32
        EPS = 1e-05
        CONV_DIM = INTER + 2 * GROUPS * STATE
        DT_MIN, DT_MAX = (0.0, 100.0)
        BATCH, SEQ = (2, 512)

        def _segment_sum(x):
            T = x.shape[-1]
            xx = jnp.broadcast_to(x[..., None], x.shape + (T,))
            mask_lower = jnp.tril(jnp.ones((T, T), bool), -1)
            xx = jnp.where(mask_lower, xx, 0.0)
            seg = jnp.cumsum(xx, axis=-2)
            mask_incl = jnp.tril(jnp.ones((T, T), bool), 0)
            return jnp.where(mask_incl, seg, -jnp.inf)
        b, s, _ = hidden_states.shape
        proj = hidden_states @ in_proj_w.T
        gate, hBC, dt = jnp.split(proj, [INTER, INTER + CONV_DIM], axis=-1)
        x = jnp.transpose(hBC, (0, 2, 1))
        x = jax.lax.conv_general_dilated(x, conv_w, window_strides=(1,), padding=[(CONV_K - 1, 0)], dimension_numbers=('NCH', 'OIH', 'NCH'), feature_group_count=CONV_DIM)
        x = x + conv_b[None, :, None]
        hBC = jax.nn.silu(jnp.transpose(x, (0, 2, 1)))
        xs, B, C = jnp.split(hBC, [INTER, INTER + GROUPS * STATE], axis=-1)
        A = -jnp.exp(A_log)
        dt = jnp.clip(jax.nn.softplus(dt + dt_bias), DT_MIN, DT_MAX)
        xs = xs.reshape(b, s, HEADS, HEAD_DIM)
        rep = HEADS // GROUPS
        Bm = jnp.repeat(B.reshape(b, s, GROUPS, STATE), rep, axis=2)
        Cm = jnp.repeat(C.reshape(b, s, GROUPS, STATE), rep, axis=2)
        pad = -s % CHUNK

        def padseq(t):
            return jnp.pad(t, ((0, 0), (0, pad)) + ((0, 0),) * (t.ndim - 2))
        D_res = D[None, None, :, None] * padseq(xs)
        xdt = padseq(xs * dt[..., None])
        Ad = padseq(A[None, None, :] * dt)
        Bm, Cm = (padseq(Bm), padseq(Cm))
        nc = (s + pad) // CHUNK
        xdt = xdt.reshape(b, nc, CHUNK, HEADS, HEAD_DIM)
        Ad = jnp.transpose(Ad.reshape(b, nc, CHUNK, HEADS), (0, 3, 1, 2))
        Bm = Bm.reshape(b, nc, CHUNK, HEADS, STATE)
        Cm = Cm.reshape(b, nc, CHUNK, HEADS, STATE)
        A_cum = jnp.cumsum(Ad, axis=-1)
        L = jnp.exp(_segment_sum(Ad))
        G = jnp.einsum('bclhn,bcshn->bclsh', Cm, Bm)
        M = G * jnp.transpose(L, (0, 2, 3, 4, 1))
        Y_diag = jnp.einsum('bclsh,bcshp->bclhp', M, xdt)
        decay_states = jnp.exp(A_cum[:, :, :, -1:] - A_cum)
        B_decay = Bm * jnp.transpose(decay_states, (0, 2, 3, 1))[..., None]
        states = jnp.einsum('bclhn,bclhp->bchpn', B_decay, xdt)
        states = jnp.concatenate([jnp.zeros_like(states[:, :1]), states], axis=1)
        chunk_sums = jnp.pad(A_cum[:, :, :, -1], ((0, 0), (0, 0), (1, 0)))
        decay_chunk = jnp.exp(_segment_sum(chunk_sums))
        decay_chunk = jnp.transpose(decay_chunk, (0, 2, 3, 1))
        new_states = jnp.einsum('bczh,bchpn->bzhpn', decay_chunk, states)
        states = new_states[:, :-1]
        state_decay = jnp.exp(A_cum)
        Y_off = jnp.einsum('bclhn,bchpn->bclhp', Cm, states) * jnp.transpose(state_decay, (0, 2, 3, 1))[..., None]
        y = (Y_diag + Y_off).reshape(b, nc * CHUNK, HEADS, HEAD_DIM) + D_res
        y = y[:, :s].reshape(b, s, INTER)
        y = y * jax.nn.silu(gate)
        var = jnp.mean(y * y, axis=-1, keepdims=True)
        y = y * jax.lax.rsqrt(var + EPS) * norm_w
        return y @ out_proj_w.T

    def _L0_ffn_ref(hidden_states, ln1_w, ln2_w, wq, wk, wv, wo, gate_w, bias_e, weg, weu, wed, wsg, wsu, wsd):
        import jax, jax.numpy as jnp
        import numpy as np
        H = 256
        HQ = 16
        HKV = 4
        D = 128
        E = 32
        K = 4
        I = 128
        ISH = 128
        EPS = 1e-06
        THETA = 10000.0
        NORM_MIN = 1e-12

        def rmsnorm(x, w):
            xf = x.astype(jnp.float32)
            var = jnp.mean(xf * xf, axis=-1, keepdims=True)
            return w * (xf * jax.lax.rsqrt(var + EPS))

        def rotate_half(x):
            x1 = x[..., 0::2]
            x2 = x[..., 1::2]
            return jnp.stack((-x2, x1), axis=-1).reshape(x.shape)
        B, S, _ = hidden_states.shape
        resid = hidden_states
        x = rmsnorm(hidden_states, ln1_w)
        q = (x @ wq).reshape(B, S, HQ, D).transpose(0, 2, 1, 3)
        k = (x @ wk).reshape(B, S, HKV, D).transpose(0, 2, 1, 3)
        v = (x @ wv).reshape(B, S, HKV, D).transpose(0, 2, 1, 3)
        pos = jnp.arange(S, dtype=jnp.float32)
        inv_freq = 1.0 / THETA ** (jnp.arange(0, D, 2, dtype=jnp.float32) / D)
        ang = pos[:, None] * inv_freq[None, :]
        cos = jnp.repeat(jnp.cos(ang), 2, axis=-1)[None, None]
        sin = jnp.repeat(jnp.sin(ang), 2, axis=-1)[None, None]
        q = q * cos + rotate_half(q) * sin
        k = k * cos + rotate_half(k) * sin
        k = jnp.repeat(k, HQ // HKV, axis=1)
        v = jnp.repeat(v, HQ // HKV, axis=1)
        scores = jnp.einsum('bhqd,bhkd->bhqk', q, k) / jnp.sqrt(jnp.float32(D))
        causal = jnp.tril(jnp.ones((S, S), dtype=bool))
        scores = jnp.where(causal, scores, jnp.float32(-1000000000.0))
        attn = jax.nn.softmax(scores, axis=-1)
        o = jnp.einsum('bhqk,bhkd->bhqd', attn, v).transpose(0, 2, 1, 3).reshape(B, S, HQ * D)
        x = resid + o @ wo
        resid2 = x
        xn = rmsnorm(x, ln2_w)
        T = B * S
        xf = xn.reshape(T, H).astype(jnp.float32)
        router_logits = xf @ gate_w.T
        probs = jax.nn.softmax(router_logits, axis=-1)
        _, sel = jax.lax.top_k(probs + bias_e, K)
        rw = jnp.take_along_axis(probs, sel, axis=-1)
        rw = rw / jnp.maximum(jnp.sum(rw, axis=-1, keepdims=True), NORM_MIN)
        cw = jnp.zeros((T, E), jnp.float32).at[jnp.arange(T)[:, None], sel].set(rw)
        g = jnp.einsum('th,ehi->tei', xf, weg)
        u = jnp.einsum('th,ehi->tei', xf, weu)
        hmid = jax.nn.silu(g) * u * cw[:, :, None]
        moe_y = jnp.einsum('tei,eih->th', hmid, wed).reshape(B, S, H)
        shared = jax.nn.silu(xn @ wsg) * (xn @ wsu) @ wsd
        return resid2 + moe_y + shared
    x = L0_attn_hidden_states
    x = x + _layernorm(_L0_attn_ref(_layernorm(x, axis=-1), L0_attn_in_proj_w, L0_attn_conv_w, L0_attn_conv_b, L0_attn_A_log, L0_attn_dt_bias, L0_attn_D, L0_attn_norm_w, L0_attn_out_proj_w), axis=-1)
    x = x + _layernorm(_L0_ffn_ref(_layernorm(x, axis=-1), L0_ffn_ln1_w, L0_ffn_ln2_w, L0_ffn_wq, L0_ffn_wk, L0_ffn_wv, L0_ffn_wo, L0_ffn_gate_w, L0_ffn_bias_e, L0_ffn_weg, L0_ffn_weu, L0_ffn_wed, L0_ffn_wsg, L0_ffn_wsu, L0_ffn_wsd), axis=-1)
    return x

_drawn_inputs = setup_inputs


def setup_inputs(seed=0):
    import zlib

    import numpy as np

    out = dict(_drawn_inputs(seed))
    spreads = {'L0_attn_conv_b': (0.0, 0.1),
     'L0_attn_D': (1.0, 0.2),
     'L0_attn_norm_w': (1.0, 0.2),
     'L0_ffn_ln1_w': (1.0, 0.6),
     'L0_ffn_ln2_w': (1.0, 0.6),
     'L0_ffn_bias_e': (0.0, 0.8)}
    factors = {'L0_attn_A_log': 8.0,
     'L0_attn_dt_bias': 8.0,
     'L0_ffn_wq': 8.0,
     'L0_ffn_wk': 8.0,
     'L0_ffn_wv': 2.807,
     'L0_ffn_wo': 2.895,
     'L0_ffn_gate_w': 8.0,
     'L0_ffn_weg': 8.0,
     'L0_ffn_weu': 8.0,
     'L0_ffn_wed': 8.0,
     'L0_ffn_wsg': 8.0,
     'L0_ffn_wsu': 8.0,
     'L0_ffn_wsd': 8.0}
    for name, (base, spread) in spreads.items():
        noise = np.random.default_rng([zlib.crc32(name.encode()), seed]).standard_normal(out[name].shape)
        drawn = base * np.exp(spread * noise) if base else spread * noise
        out[name] = jnp.asarray(drawn.astype(out[name].dtype))
    for name, factor in factors.items():
        out[name] = (out[name] * factor).astype(out[name].dtype)
    return out
```

```python
from contextlib import ExitStack, contextmanager

import concourse.bass as bass
from concourse import mybir

F32 = mybir.dt.float32
BF16 = mybir.dt.bfloat16
ALU = mybir.AluOpType
ACT = mybir.ActivationFunctionType
AX_X = mybir.AxisListType.X
P = 128

BATCH, SEQ, HID = 4, 512, 256
NT = SEQ // P
NK = HID // P
INTER, STATE, HEADS = 512, 128, 32
HD = INTER // HEADS
CONV = INTER + 2 * STATE
TAPS = 4
CH = 64
NCH = SEQ // CH
HG = HEADS // 2
DT0 = INTER + CONV
LN_EPS = 1e-5
RMS_EPS = 1e-6


def open_tools(nc, ctx):
    def sb(name, shape, dt=F32):
        return ctx.enter_context(nc.sbuf_tensor(name, shape, dt))

    def ps(name, shape, dt=F32):
        return ctx.enter_context(nc.psum_tensor(name, shape, dt))

    def sem(name):
        return ctx.enter_context(nc.semaphore(name))

    return sb, ps, sem


def spread(ap, n):
    return ap.rearrange("p (a o) -> p a o", o=1).broadcast_to((ap.shape[0], ap.shape[1], n))


class Sems:

    def __init__(self, sem):
        self.sem, self.all = sem, []

    def __call__(self, name):
        s = self.sem(name)
        self.all.append(s)
        return s


def clear(nc, sems):
    for s in sems.all:
        nc.sync.sem_clear(s)
    nc.all_engine_barrier()


@contextmanager
def turn(nc, sems):
    with nc.Block() as block:
        yield block
    clear(nc, sems)


def mamba_phase(nc, x, winT, conv_w, conv_b, a_log, dt_bias, d_skip, norm_w, woutT, ident, x1, dbg=None):
    with ExitStack() as ctx:
        sb, ps, sem = open_tools(nc, ctx)
        w_in = sb("w_in", [P, NK, DT0 + HEADS])
        w_out = sb("w_out", [P, INTER // P, HID])
        nw = sb("nw", [P, INTER // P])
        cw = sb("cw", [P, CONV // P, TAPS])
        cb = sb("cb", [P, CONV // P])
        neg_a = sb("neg_a", [P, HEADS])
        dtb = sb("dtb", [P, HEADS])
        dsk = sb("dsk", [P, HEADS])
        tri = sb("tri", [P, P])
        suf = sb("suf", [P, P])
        half = sb("half", [P, 2, P])
        causal = sb("causal", [P, CH])
        segm = sb("segm", [P, CH, P], BF16)

        x_sb = sb("x_sb", [P, NT, HID])
        xn = sb("xn", [P, NT, HID])
        lnv = sb("lnv", [P, NT])
        eps_col = sb("eps_col", [P, 1])
        st6 = sb("st6", [P, NT, 6])
        mv = sb("mv", [P, NT, 2])
        rstd = sb("rstd", [P, NT])
        xnT = sb("xnT", [P, NK, SEQ])
        xc = sb("xc", [P, CONV // P, SEQ])
        bdup = sb("bdup", [P, NCH, 2, CH])
        sg = sb("sg", [P, NT, INTER])
        dt = sb("dt", [P, NT, HEADS])
        z = sb("z", [P, NT, HEADS])
        az = sb("az", [P, NT, HEADS])
        et = sb("et", [P, NT, HEADS])
        u = sb("u", [P, NT, HEADS])
        lu = sb("lu", [P, NT, HEADS])
        ad = sb("ad", [P, NT, HEADS])
        dsuf = sb("dsuf", [P, NT, HEADS])
        dec = sb("dec", [P, 4, NT, HEADS])
        adl = sb("adl", [P, NT, 2, HG])
        adr = sb("adr", [P, NT, 2, HG])
        adp = sb("adp", [P, 3, NCH * HG], BF16)
        es = sb("es", [P, 2, 4, NCH * HG])
        mt = sb("mt", [P, NCH * HG, CH])
        gm = sb("gm", [P, NCH, CH])
        xtok = sb("xtok", [P, NT, INTER])
        btok = sb("btok", [P, NT, STATE])
        xbd = sb("xbd", [P, NCH, HG, 2 * HD])
        xds = sb("xds", [P, NT, INTER])
        xd = sb("xd", [P, NT, INTER])
        stt = sb("stt", [P, NCH, INTER])
        y = sb("y", [P, NT, INTER])
        sq = sb("sq", [P, INTER])
        ssq = sb("ssq", [P, NT])
        yT = xc
        o_sb = xn
        bank = [ps(f"bank{i}", [P, 512]) for i in range(8)]

        su = Sems(sem)
        loaded, masks, folded, a_ready = su("m_loaded"), su("m_masks"), su("m_folded"), su("m_a_ready")

        with nc.Block() as block:
            @block.sync
            def _(sp):
                sp.dma_start(w_in[:], winT.rearrange("(k p) n -> p k n", p=P)).then_inc(loaded, 16)
                sp.dma_start(w_out[:], woutT.rearrange("(k p) n -> p k n", p=P)).then_inc(loaded, 16)
                sp.dma_start(nw[:], norm_w).then_inc(loaded, 16)
                sp.dma_start(cw[:], conv_w).then_inc(loaded, 16)
                sp.dma_start(cb[:], conv_b).then_inc(loaded, 16)
                for dst, src in ((neg_a, a_log), (dtb, dt_bias), (dsk, d_skip)):
                    sp.dma_start(dst[:], src.rearrange("(o h) -> o h", o=1).broadcast_to((P, HEADS))).then_inc(loaded, 16)
                sp.wait_ge(loaded, 8 * 16)

            @block.gpsimd
            def _(pool):
                pool.memset(ident[:], 0.0)
                pool.memset(tri[:], 1.0)
                pool.memset(suf[:], 1.0)
                pool.memset(segm[:], 1.0)
                pool.memset(stt[:, 0, :], 0.0)
                pool.memset(xbd[:], 0.0)
                pool.memset(eps_col[:], LN_EPS)
                pool.memset(half[:, 0, :], 1.0)
                pool.memset(half[:, 1, :], 1.0).then_inc(masks, 1)
                pool.wait_ge(masks, 1)
                pool.affine_select(out=ident[:], in_=ident[:], compare_op=ALU.not_equal, fill=1.0, base=0,
                                   pattern=[[-1, P]], channel_multiplier=1)
                pool.affine_select(out=tri[:], in_=tri[:], compare_op=ALU.is_ge, fill=0.0, base=0,
                                   pattern=[[1, P]], channel_multiplier=-1)
                pool.affine_select(out=suf[:], in_=suf[:], compare_op=ALU.is_ge, fill=0.0, base=-1,
                                   pattern=[[-1, P]], channel_multiplier=1).then_inc(masks, 1)
                pool.wait_ge(masks, 2)
                pool.memset(half[0:CH, 1, :], 0.0)
                pool.memset(tri[0:CH, CH:P], 0.0).then_inc(masks, 1)
                pool.wait_ge(masks, 3)
                pool.memset(half[CH:P, 0, :], 0.0)
                pool.memset(suf[CH:P, 0:CH], 0.0).then_inc(masks, 1)
                pool.wait_ge(masks, 4)
                for hh in range(2):
                    v = segm[:, :, hh * CH:(hh + 1) * CH]
                    pool.affine_select(out=v, in_=v, compare_op=ALU.is_ge, fill=0.0, base=-1 - CH * hh,
                                       pattern=[[0, CH], [-1, CH]], channel_multiplier=1).then_inc(masks, 1)
                pool.wait_ge(masks, 6)
                for hh in range(2):
                    v = segm[:, :, hh * CH:(hh + 1) * CH]
                    pool.affine_select(out=v, in_=v, compare_op=ALU.is_ge, fill=0.0, base=CH * hh,
                                       pattern=[[1, CH], [0, CH]], channel_multiplier=-1).then_inc(masks, 1)
                for hh in range(2):
                    h = slice(hh * CH, (hh + 1) * CH)
                    pool.wait_ge(masks, 8 + hh)
                    pool.tensor_copy(causal[h, :], tri[h, h]).then_inc(masks, 1)

            @block.scalar
            def _(act):
                act.wait_ge(loaded, 8 * 16)
                act.activation(az[:, 0, :], neg_a[:], ACT.Exp).then_inc(a_ready, 1)

            @block.vector
            def _(dve):
                dve.wait_ge(loaded, 8 * 16)
                for k in range(INTER // P):
                    dve.tensor_scalar(w_out[:, k, :], w_out[:, k, :], nw[:, k:k + 1], None, ALU.mult)
                dve.wait_ge(a_ready, 1)
                dve.tensor_scalar(neg_a[:], az[:, 0, :], -1.0, None, ALU.mult).then_inc(folded, 1)
        clear(nc, su)

        s = Sems(sem)
        x_in = s("x_in")
        stat, mv_ok, rstd_ok, xn_ok = s("stat"), s("mv_ok"), s("rstd_ok"), s("xn_ok")
        pe = s("pe_banks")
        act_free, dve_free = s("act_free"), s("dve_free")
        tap, conv_ok = s("tap"), s("conv_ok")
        bdup_ok = s("bdup_ok")
        cid, lnv_ok = s("cid"), s("lnv_ok")
        gate_ok = s("gate_ok")
        dts, dts_a, ad_ok, adp_ok = s("dts"), s("dts_a"), s("ad_ok"), s("adp_ok")
        dec_ok, es_ok, es_used, mt_ok, gm_ok = s("dec_ok"), s("es_ok"), s("es_used"), s("mt_ok"), s("gm_ok")
        tok_ok, xbd_ok, xds_ok, xd_ok, dsuf_ok = s("tok_ok"), s("xbd_ok"), s("xds_ok"), s("xd_ok"), s("dsuf_ok")
        carried, state_ok = s("carried"), s("state_ok")
        ych, y_ok, sq_ok = s("ych"), s("y_ok"), s("sq_ok")
        out_ok, och, x1_ok = s("out_ok"), s("och"), s("x1_ok")

        A, V = (act_free, 1), (dve_free, 1)
        jobs = [("xnT", 0, A), ("xnT", 1, V), ("dt", 0, V)]
        jobs += [("conv", c, (tap, TAPS - 1)) for c in (4, 5, 0, 1, 2, 3)]
        jobs += [("gate", t, A) for t in range(NT)]
        jobs += [("bT", 0, A), ("g", 0, V)]
        jobs += [("xT", t, A) for t in range(NT)]
        jobs += [("dec", 0, A)]
        jobs += [("seg", i, A) for i in range(CH // 4)]
        jobs += [("st", c, (state_ok, 1)) for c in range(NCH - 1)]
        for t in range(NT):
            jobs += [("off", t, V), ("diag", t, V)]
        jobs += [("yT", c, A) for c in range(INTER // P)]
        jobs += [("out", i, (out_ok, 2)) for i in range(NT // 2)]
        at = {(n, i): k for k, (n, i, _) in enumerate(jobs)}

        def read_by(k):
            return sum(j[2][1] for j in jobs[:k + 1] if j[2][0] is jobs[k][2][0])

        def where(name, i=0):
            return bank[at[name, i] % 8]

        def fill(eng, name, i=0):
            k = at[name, i] - 8
            if k >= 0:
                eng.wait_ge(jobs[k][2][0], read_by(k))

        def full(eng, name, i=0):
            eng.wait_ge(pe, at[name, i] + 1)

        def free_no(name, i=0):
            return read_by(at[name, i])

        CONV_ORDER = [i for n, i, _ in jobs if n == "conv"]
        with nc.Fori(0, BATCH) as b, turn(nc, s) as block:
            @block.sync
            def _(sp):
                sp.dma_start(x_sb[:], x[bass.ts(b, SEQ), :].rearrange("(t p) h -> p t h", p=P)).then_inc(x_in, 16)

            @block.tensor
            def _(te):
                for k in range(NK):
                    for t in range(NT):
                        te.wait_ge(xn_ok, t + 1)
                        i = te.transpose(where("xnT", k)[:, t * P:(t + 1) * P], xn[:, t, k * P:(k + 1) * P], ident[:])
                    i.then_inc(pe, 1)
                te.wait_ge(act_free, 1)
                te.wait_ge(dve_free, 1)
                for t in range(NT):
                    for k in range(NK):
                        i = te.matmul(where("dt")[:, t * HEADS:(t + 1) * HEADS], xnT[:, k, t * P:(t + 1) * P],
                                      w_in[:, k, DT0:DT0 + HEADS], start=k == 0, stop=k == NK - 1)
                i.then_inc(pe, 1)
                for c in CONV_ORDER:
                    fill(te, "conv", c)
                    for k in range(NK):
                        i = te.matmul(where("conv", c)[:], w_in[:, k, INTER + c * P:INTER + (c + 1) * P],
                                      xnT[:, k, :], start=k == 0, stop=k == NK - 1)
                    i.then_inc(pe, 1)
                for t in range(NT):
                    fill(te, "gate", t)
                    for k in range(NK):
                        i = te.matmul(where("gate", t)[:], xnT[:, k, t * P:(t + 1) * P], w_in[:, k, 0:INTER],
                                      start=k == 0, stop=k == NK - 1)
                    i.then_inc(pe, 1)
                te.wait_ge(conv_ok, 2)
                fill(te, "bT")
                for t in range(NT):
                    i = te.transpose(where("bT")[:, t * P:(t + 1) * P], xc[:, 4, t * P:(t + 1) * P], ident[:])
                i.then_inc(pe, 1)
                fill(te, "g")
                for c in range(NCH):
                    i = te.matmul(where("g")[:, c * CH:(c + 1) * CH],
                                  bdup[:, c, :, :].rearrange("p a s -> p (a s)"),
                                  xc[:, 5, c * CH:(c + 1) * CH], start=True, stop=True)
                i.then_inc(pe, 1)
                te.wait_ge(conv_ok, 6)
                for t in range(NT):
                    fill(te, "xT", t)
                    for c in range(NT):
                        i = te.transpose(where("xT", t)[:, c * P:(c + 1) * P], xc[:, c, t * P:(t + 1) * P], ident[:])
                    i.then_inc(pe, 1)
                te.wait_ge(ad_ok, 1)
                fill(te, "dec")
                rhs = ad[:].rearrange("p t h -> p (t h)")
                te.matmul(where("dec")[:, 0:P], tri[:], rhs, start=True, stop=True)
                te.matmul(where("dec")[:, P:2 * P], suf[:], rhs, start=True, stop=True)
                for q in range(2):
                    i = te.matmul(where("dec")[:, (2 + q) * P:(3 + q) * P], half[:, q, :], rhs,
                                  start=True, stop=True)
                i.then_inc(pe, 1)
                te.wait_ge(adp_ok, 3)
                for g in range(CH // 4):
                    fill(te, "seg", g)
                    for j in range(4):
                        for part in range(3):
                            i = te.matmul(where("seg", g)[:, j * P:(j + 1) * P], segm[:, 4 * g + j, :],
                                          adp[:, part, :], start=part == 0, stop=part == 2)
                    i.then_inc(pe, 1)
                te.wait_ge(xds_ok, 1)
                te.wait_ge(act_free, free_no("bT"))
                for c in range(NCH - 1):
                    fill(te, "st", c)
                    h = slice(c % 2 * CH, (c % 2 + 1) * CH)
                    te.matmul(where("st", c)[:], btok[h, c // 2, :], xds[h, c // 2, :],
                              start=True, stop=True).then_inc(pe, 1)
                te.wait_ge(xbd_ok, 4)
                te.wait_ge(mt_ok, CH // 4)
                for t in range(NT):
                    fill(te, "off", t)
                    for q in range(2):
                        c = 2 * t + q
                        if c:
                            te.wait_ge(state_ok, c)
                        i = te.matmul(where("off", t)[q * CH:(q + 1) * CH, :], xc[:, 5, c * CH:(c + 1) * CH],
                                      stt[:, c, :], start=True, stop=True)
                    i.then_inc(pe, 1)
                    fill(te, "diag", t)
                    for q in range(2):
                        for g in range(HG):
                            out = where("diag", t)[q * CH:(q + 1) * CH, :].rearrange(
                                "p (a g d) -> p g a d", a=2, g=HG)[:, g, :, :]
                            i = te.matmul(out, mt[:, (2 * t + q) * HG + g, :], xbd[:, 2 * t + q, g, :],
                                          start=True, stop=True)
                    i.then_inc(pe, 1)
                for c in range(INTER // P):
                    fill(te, "yT", c)
                    for t in range(NT):
                        te.wait_ge(y_ok, t + 1)
                        i = te.transpose(where("yT", c)[:, t * P:(t + 1) * P], y[:, t, c * P:(c + 1) * P], ident[:])
                    i.then_inc(pe, 1)
                te.wait_ge(act_free, free_no("yT", INTER // P - 1))
                for j in range(NT // 2):
                    fill(te, "out", j)
                    for t in (2 * j, 2 * j + 1):
                        for c in range(INTER // P):
                            i = te.matmul(where("out", j)[:, t % 2 * HID:(t % 2 + 1) * HID],
                                          yT[:, c, t * P:(t + 1) * P], w_out[:, c, :],
                                          start=c == 0, stop=c == INTER // P - 1)
                    i.then_inc(pe, 1)

            @block.scalar
            def _(act):
                def rsqrt(out, v, eps, n):
                    act.activation(lnv[:], v, ACT.Ln, bias=eps_col[:, 0:1]).then_inc(lnv_ok, 1)
                    act.wait_ge(lnv_ok, n)
                    act.activation(out, lnv[:], ACT.Exp, scale=-0.5).then_inc(rstd_ok, 1)

                act.wait_ge(mv_ok, NT)
                rsqrt(rstd[:], mv[:, :, 1], LN_EPS, 1)

                def silu_conv(n):
                    c = CONV_ORDER[n]
                    act.wait_ge(tap, 3 * (n + 1))
                    if c == 4:
                        act.activation(bdup[:], xc[:, c, :].rearrange("p (c o s) -> p c o s", c=NCH, o=1).broadcast_to(
                            (P, NCH, 2, CH)), ACT.Silu).then_inc(bdup_ok, 1)
                        act.wait_ge(bdup_ok, 1)
                    act.activation(xc[:, c, :], xc[:, c, :], ACT.Silu).then_inc(conv_ok, 1)

                full(act, "xnT", 0)
                act.activation(xnT[:, 0, :], where("xnT", 0)[:], ACT.Copy).then_inc(act_free, 1)
                for n, c in enumerate(CONV_ORDER):
                    full(act, "conv", c)
                    act.activation(xc[:, c, :], where("conv", c)[:], ACT.Identity, bias=cb[:, c:c + 1],
                                   scale=cw[:, c, TAPS - 1:TAPS]).then_inc(cid, 1)
                    if n:
                        silu_conv(n - 1)
                silu_conv(5)
                for t in range(NT):
                    full(act, "gate", t)
                    act.activation(sg[:, t, :], where("gate", t)[:], ACT.Silu).then_inc(act_free, 1)
                full(act, "bT")
                act.activation(btok[:].rearrange("p t n -> p (t n)"), where("bT")[:], ACT.Copy).then_inc(act_free, 1)
                for t in range(NT):
                    full(act, "xT", t)
                    act.activation(xtok[:, t, :], where("xT", t)[:], ACT.Copy).then_inc(act_free, 1)
                act.wait_ge(dts, 1)
                act.activation(et[:], az[:], ACT.Exp, scale=-1.0).then_inc(dts_a, 1)
                act.wait_ge(dts, 2)
                act.activation(lu[:], u[:], ACT.Ln).then_inc(dts_a, 1)
                full(act, "dec")
                act.activation(dec[:].rearrange("p k t h -> p (k t h)"), where("dec")[:], ACT.Exp).then_inc(act_free, 1)
                for g in range(CH // 4):
                    full(act, "seg", g)
                    if g >= 2:
                        act.wait_ge(mt_ok, g - 1)
                    act.activation(es[:, g % 2, :, :].rearrange("p l c -> p (l c)"), where("seg", g)[:],
                                   ACT.Exp).then_inc(act_free, 1)
                for t in range(NT):
                    act.wait_ge(y_ok, t + 1)
                    if t:
                        act.wait_ge(sq_ok, t)
                    act.activation(sq[:], y[:, t, :], ACT.Square, scale=INTER ** -0.5, accum_out=ssq[:, t:t + 1]).then_inc(sq_ok, 1)
                act.wait_ge(sq_ok, NT)
                rsqrt(ssq[:], ssq[:], LN_EPS, 2)
                for c in range(INTER // P):
                    full(act, "yT", c)
                    act.activation(yT[:, c, :], where("yT", c)[:], ACT.Copy).then_inc(act_free, 1)
                act.wait_ge(mv_ok, 2 * NT)
                rsqrt(rstd[:], mv[:, :, 1], LN_EPS, 3)

            @block.vector
            def _(dve):
                def stats(t, src, first):
                    dve.bn_stats(st6[:, t, :], src).then_inc(stat, 1)
                    dve.wait_ge(stat, first + t + 1)
                    dve.bn_aggr(mv[:, t, :], st6[:, t, :]).then_inc(mv_ok, 1)

                dve.wait_ge(x_in, 16)
                for t in range(NT):
                    stats(t, x_sb[:, t, :], 0)
                dve.wait_ge(rstd_ok, 1)
                for t in range(NT):
                    dve.tensor_scalar(xn[:, t, :], x_sb[:, t, :], mv[:, t, 0:1], rstd[:, t:t + 1],
                                      ALU.subtract, ALU.mult).then_inc(xn_ok, 1)
                full(dve, "xnT", 1)
                dve.tensor_copy(xnT[:, 1, :], where("xnT", 1)[:]).then_inc(dve_free, 1)
                full(dve, "dt")
                dve.tensor_tensor(z[:], where("dt")[:, 0:NT * HEADS].rearrange("p (t h) -> p t h", t=NT),
                                  dtb[:].rearrange("p (o h) -> p o h", o=1).broadcast_to((P, NT, HEADS)),
                                  ALU.add).then_inc(dve_free, 1)
                dve.wait_ge(dve_free, 2)
                dve.scalar_tensor_tensor(out=az[:], in0=z[:], scalar=-1.0, in1=z[:], op0=ALU.mult,
                                         op1=ALU.max).then_inc(dts, 1)
                for n, c in enumerate(CONV_ORDER):
                    full(dve, "conv", c)
                    dve.wait_ge(cid, n + 1)
                    for j in range(1, TAPS):
                        if j > 1:
                            dve.wait_ge(tap, 3 * n + j - 1)
                        i = dve.scalar_tensor_tensor(out=xc[:, c, j:SEQ], in0=where("conv", c)[:, 0:SEQ - j],
                                                     scalar=cw[:, c, TAPS - 1 - j:TAPS - j], in1=xc[:, c, j:SEQ],
                                                     op0=ALU.mult, op1=ALU.add)
                        i.then_inc(tap, 1)
                full(dve, "g")
                dve.tensor_tensor(gm[:], where("g")[:].rearrange("p (c l) -> p c l", c=NCH),
                                  causal[:].rearrange("p (o l) -> p o l", o=1).broadcast_to((P, NCH, CH)),
                                  ALU.mult).then_inc(dve_free, 1)
                dve.wait_ge(dts_a, 1)
                dve.tensor_scalar(u[:], et[:], 1.0, None, ALU.add).then_inc(dts, 1)
                dve.wait_ge(dts, 2)
                dve.scalar_tensor_tensor(out=et[:], in0=u[:], scalar=1.0, in1=et[:], op0=ALU.subtract,
                                         op1=ALU.subtract)
                dve.reciprocal(az[:], u[:]).then_inc(dts, 1)
                dve.wait_ge(dts, 3)
                dve.tensor_tensor(et[:], et[:], az[:], ALU.mult)
                dve.wait_ge(dts_a, 2)
                dve.scalar_tensor_tensor(out=dt[:], in0=z[:], scalar=0.0, in1=lu[:], op0=ALU.max,
                                         op1=ALU.add).then_inc(dts, 1)
                dve.wait_ge(dts, 4)
                dve.tensor_tensor(dt[:], dt[:], et[:], ALU.subtract).then_inc(dts, 1)
                dve.wait_ge(dts, 5)
                dve.tensor_scalar(dt[:], dt[:], 0.0, 100.0, ALU.max, ALU.min).then_inc(dts, 1)
                dve.wait_ge(dts, 6)
                dve.tensor_tensor(ad[:], dt[:], neg_a[:].rearrange("p (o h) -> p o h", o=1).broadcast_to(
                    (P, NT, HEADS)), ALU.mult).then_inc(ad_ok, 1)
                dve.wait_ge(ad_ok, 1)
                for hh in range(2):
                    for q in range(2):
                        i = dve.tensor_copy(adl[hh * CH:(hh + 1) * CH, :, q, :],
                                            ad[q * CH:(q + 1) * CH, :, hh * HG:(hh + 1) * HG])
                i.then_inc(dts, 1)
                dve.wait_ge(dts, 7)
                flat = "p t q g -> p (t q g)"
                dve.tensor_copy(adp[:, 0, :], adl[:].rearrange(flat)).then_inc(adp_ok, 1)
                dve.wait_ge(adp_ok, 1)
                dve.tensor_tensor(adr[:].rearrange(flat), adl[:].rearrange(flat), adp[:, 0, :],
                                  ALU.subtract).then_inc(dts, 1)
                dve.wait_ge(dts, 8)
                dve.tensor_copy(adp[:, 1, :], adr[:].rearrange(flat)).then_inc(adp_ok, 1)
                dve.wait_ge(adp_ok, 2)
                dve.tensor_tensor(adp[:, 2, :], adr[:].rearrange(flat), adp[:, 1, :], ALU.subtract).then_inc(adp_ok, 1)
                dve.wait_ge(act_free, free_no("dec"))
                dve.tensor_tensor(dsuf[:], dt[:], dec[:, 1, :, :], ALU.mult).then_inc(dsuf_ok, 1)
                dve.wait_ge(dsuf_ok, 1)
                dve.wait_ge(act_free, free_no("xT", NT - 1))
                dve.tensor_tensor(xds[:].rearrange("p t (h d) -> p (t h) d", d=HD),
                                  xtok[:].rearrange("p t (h d) -> p (t h) d", d=HD),
                                  spread(dsuf[:].rearrange("p t h -> p (t h)"), HD), ALU.mult).then_inc(xds_ok, 1)
                dve.wait_ge(dve_free, free_no("g"))
                for g in range(CH // 4):
                    dve.wait_ge(act_free, free_no("seg", g))
                    out = mt[:, :, 4 * g:4 * g + 4].rearrange("p (c g) l -> p c g l", c=NCH)
                    e_ap = es[:, g % 2, :, :].rearrange("p l (c g) -> p c g l", c=NCH)
                    g_ap = gm[:, :, 4 * g:4 * g + 4].rearrange("p c (o l) -> p c o l", o=1).broadcast_to(
                        (P, NCH, HG, 4))
                    dve.tensor_tensor(out, e_ap, g_ap, ALU.mult).then_inc(mt_ok, 1)
                for c in range(NCH - 1):
                    full(dve, "st", c)
                    if c == 0:
                        dve.tensor_copy(stt[:, 1, :], where("st", 0)[:]).then_inc(state_ok, 1)
                    else:
                        dve.wait_ge(state_ok, c)
                        dve.tensor_tensor(stt[:, c + 1, :].rearrange("p (h d) -> p h d", d=HD),
                                          stt[:, c, :].rearrange("p (h d) -> p h d", d=HD),
                                          spread(dec[:, 2 + c % 2, c // 2, :], HD), ALU.mult).then_inc(carried, 1)
                        dve.wait_ge(carried, c)
                        dve.tensor_tensor(stt[:, c + 1, :], stt[:, c + 1, :], where("st", c)[:],
                                          ALU.add).then_inc(state_ok, 1)
                dve.wait_ge(xd_ok, 1)
                for t in range(NT):
                    full(dve, "off", t)
                    dve.tensor_tensor(y[:, t, :].rearrange("p (h d) -> p h d", d=HD),
                                      where("off", t)[:].rearrange("p (h d) -> p h d", d=HD),
                                      spread(dec[:, 0, t, :], HD), ALU.mult).then_inc(dve_free, 1)
                    full(dve, "diag", t)
                    dve.wait_ge(dve_free, free_no("off", t))
                    dve.tensor_tensor(y[:, t, :], y[:, t, :], where("diag", t)[:], ALU.add).then_inc(dve_free, 1)
                    dve.wait_ge(dve_free, free_no("diag", t))
                    dve.tensor_tensor(y[:, t, :], y[:, t, :], xd[:, t, :], ALU.add).then_inc(ych, 1)
                    dve.wait_ge(ych, t + 1)
                    dve.tensor_tensor(y[:, t, :], y[:, t, :], sg[:, t, :], ALU.mult).then_inc(y_ok, 1)
                dve.wait_ge(rstd_ok, 2)
                for t in range(NT):
                    full(dve, "out", t // 2)
                    dve.tensor_scalar(o_sb[:, t, :], where("out", t // 2)[:, t % 2 * HID:(t % 2 + 1) * HID],
                                      ssq[:, t:t + 1], None, ALU.mult).then_inc(out_ok, 1)
                    dve.wait_ge(out_ok, t + 1)
                    stats(t, o_sb[:, t, :], NT)
                dve.wait_ge(rstd_ok, 3)
                for t in range(NT):
                    dve.tensor_scalar(o_sb[:, t, :], o_sb[:, t, :], mv[:, t, 0:1], rstd[:, t:t + 1],
                                      ALU.subtract, ALU.mult).then_inc(och, 1)
                    dve.wait_ge(och, t + 1)
                    dve.tensor_tensor(x1[:, bass.ds(b * (NT * HID) + t * HID, HID)], o_sb[:, t, :], x_sb[:, t, :],
                                      ALU.add).then_inc(x1_ok, 1)

            @block.gpsimd
            def _(pool):
                pool.wait_ge(act_free, free_no("xT", NT - 1))
                pool.tensor_tensor(xd[:].rearrange("p t (h d) -> p t h d", d=HD),
                                   xtok[:].rearrange("p t (h d) -> p t h d", d=HD),
                                   dsk[:].rearrange("p (o h u) -> p o h u", o=1, u=1).broadcast_to((P, NT, HEADS, HD)),
                                   ALU.mult).then_inc(xd_ok, 1)
                pool.wait_ge(dts, 6)
                pool.wait_ge(xd_ok, 1)
                for q in range(2):
                    for hh in range(2):
                        src = slice(q * CH, (q + 1) * CH)
                        out = xbd[hh * CH:(hh + 1) * CH, :, :, hh * HD:(hh + 1) * HD].rearrange(
                            "p (t q) g d -> p q t g d", q=2)[:, q]
                        xin = xtok[src, :, hh * 256:(hh + 1) * 256].rearrange("p t (g d) -> p t g d", d=HD)
                        din = dt[src, :, hh * HG:(hh + 1) * HG].rearrange("p t (g o) -> p t g o", o=1).broadcast_to(
                            (CH, NT, HG, HD))
                        if q or hh:
                            pool.wait_ge(xbd_ok, 2 * q + hh)
                        pool.tensor_tensor(out, xin, din, ALU.mult).then_inc(xbd_ok, 1)


QH, KVH, D = 16, 4, 128
GRP = QH // KVH
NE, TOPK, EI = 32, 4, 128
NORM_MIN = 1e-12
NEG = -1e30
PAIRS = NT * (NT + 1) // 2


def attention_phase(nc, wq, wk, wv, wo, ln1, ln2, cos, sin, gateT, bias_e, ident, x1, x2, xfT, cw):
    with ExitStack() as ctx:
        sb, ps, sem = open_tools(nc, ctx)
        wq_sb = sb("wq_sb", [P, NK, QH * D])
        wk_sb = sb("wk_sb", [P, NK, KVH * D])
        wv_sb = sb("wv_sb", [P, NK, KVH * D])
        wo_sb = sb("wo_sb", [P, QH, HID])
        ln1_sb = sb("ln1_sb", [P, NK])
        ln2_sb = sb("ln2_sb", [P, NK])
        cos_sb = sb("cos_sb", [P, SEQ])
        sin_sb = sb("sin_sb", [P, SEQ])
        gate_sb = sb("gate_sb", [P, NK, NE])
        be_sb = sb("be_sb", [P, NE])
        eps_ln = sb("eps_ln", [P, 1])
        eps_rms = sb("eps_rms", [P, 1])
        identb = sb("identb", [P, P], BF16)
        future = sb("future", [P, P], BF16)
        col_no = sb("col_no", [P, NE])
        scol_i = sb("scol_i", [P, NE], mybir.dt.int32)

        st6 = sb("a_st6", [P, NT, 6])
        mv = sb("a_mv", [P, NT, 2])
        lnv = sb("a_lnv", [P, NT])
        r1 = sb("r1", [P, NT])
        m2 = sb("m2", [P, NT])
        r2 = sb("r2", [P, NT])
        h = sb("h", [P, NT, HID])
        xr = sb("xr", [P, NT, HID])
        xT = sb("xT", [P, NK, SEQ])
        v = sb("v", [P, NT, KVH * D])
        kT = sb("kT", [P, KVH, SEQ])
        rc = sb("rc", [P, 2, SEQ])
        rs = sb("rs", [P, 2, SEQ])
        qT = sb("qT", [P, 2, SEQ])
        nmax_r = sb("nmax_r", [P, 2, NT])
        nmax = sb("nmax", [P, 2, NT])
        rsum = sb("rsum", [P, 2, NT])
        rrec = sb("rrec", [P, 2, NT])
        pr = sb("pr", [P, 2, PAIRS * P])
        pt = sb("pt", [P, 2, PAIRS * P])
        oT = sb("oT", [P, QH, SEQ])
        sq = sb("a_sq", [P, HID])
        ssq = sb("a_ssq", [P, NT])
        x2s = sb("x2s", [P, NT, HID])
        xfs = sb("xfs", [P, NK, SEQ])
        lmax = sb("lmax", [P, NT])
        lsum = sb("lsum", [P, NT])
        lrec = sb("lrec", [P, NT])
        pb = sb("pb", [P, NT, NE])
        pbb = sb("pbb", [P, NT, NE])
        top = sb("top", [P, NT, 8])
        topi = sb("topi", [P, NT, 8], mybir.dt.uint32)
        topf = sb("topf", [P, NT, TOPK])
        sel = sb("sel", [P, NT, NE])
        one = sb("one", [P, NT, NE])
        bank = [ps(f"a_bank{i}", [P, 512]) for i in range(8)]

        su = Sems(sem)
        loaded, masks = su("a_loaded"), su("a_masks")
        with nc.Block() as block:
            @block.sync
            def _(sp):
                n = 0
                for dst, src in ((wq_sb, wq), (wk_sb, wk), (wv_sb, wv), (gate_sb, gateT)):
                    sp.dma_start(dst[:], src.rearrange("(k p) n -> p k n", p=P)).then_inc(loaded, 16)
                    n += 16
                sp.dma_start(wo_sb[:], wo.rearrange("(h p) n -> p h n", p=P)).then_inc(loaded, 16)
                for dst, src in ((ln1_sb, ln1), (ln2_sb, ln2), (cos_sb, cos), (sin_sb, sin)):
                    sp.dma_start(dst[:], src).then_inc(loaded, 16)
                    n += 16
                sp.dma_start(be_sb[:], bias_e.rearrange("(o h) -> o h", o=1).broadcast_to((P, NE))).then_inc(loaded, 16)
                sp.wait_ge(loaded, n + 32)

            @block.gpsimd
            def _(pool):
                pool.memset(eps_ln[:], LN_EPS)
                pool.memset(eps_rms[:], RMS_EPS)
                pool.memset(future[:], 0.0)
                pool.memset(identb[:], 0.0)
                pool.iota(scol_i[:], pattern=[[1, NE]], base=0, channel_multiplier=0).then_inc(masks, 1)
                pool.wait_ge(masks, 1)
                pool.affine_select(out=identb[:], in_=identb[:], compare_op=ALU.not_equal, fill=1.0, base=0,
                                   pattern=[[-1, P]], channel_multiplier=1)
                pool.affine_select(out=future[:], in_=future[:], compare_op=ALU.is_ge, fill=NEG, base=0,
                                   pattern=[[-1, P]], channel_multiplier=1)
                pool.tensor_copy(col_no[:], scol_i[:]).then_inc(masks, 1)
                pool.wait_ge(masks, 2)
        clear(nc, su)

        s = Sems(sem)
        pe, act_free, dve_free = s("a_pe"), s("a_act_free"), s("a_dve_free")
        stat, mv_ok, lnv_ok, r_ok, m2_ok = s("a_stat"), s("a_mv_ok"), s("a_lnv_ok"), s("r_ok"), s("m2_ok")
        h_ok, xr_ok, xT_ok = s("h_ok"), s("xr_ok"), s("xT_ok")
        rot, qk_ok = s("rot"), s("qk_ok")
        mxr = s("mxr")
        mx_ok, e_ok, rec_ok, p_ok = s("mx_ok"), s("e_ok"), s("rec_ok"), s("p_ok")
        pt_a, pt_v, oT_ok = s("pt_a"), s("pt_v"), s("oT_ok")
        x2_ok, sq_ok, xf_ok, xfT_ok = s("x2_ok"), s("a_sq_ok"), s("xf_ok"), s("xfT_ok")
        rt, rt_a, cw_ok, kept = s("rt"), s("rt_a"), s("cw_ok"), s("kept")

        A, V = (act_free, 1), (dve_free, 1)
        jobs = [("xT", 0, A), ("xT", 1, A)]
        jobs += [("v", t, A) for t in range(NT)]
        jobs += [("k", g, (rot, 3)) for g in range(KVH)]
        steps = []
        for n in range(-2, QH + 1):
            if 0 <= n + 2 < QH:
                steps.append(("q", n + 2))
            if 0 <= n + 1 < QH:
                steps.append(("s", n + 1))
            if 0 <= n < QH:
                steps.append(("p", n))
            if 0 <= n - 1 < QH:
                steps.append(("o", n - 1))
        for what, n in steps:
            if what == "q":
                jobs += [("q", n, (rot, 3))]
            elif what == "s":
                jobs += [("s", (n, g), (e_ok, m)) for g, m in ((3, 1), (2, 2), (1, 1))]
            elif what == "p":
                jobs += [("p", (n, 0), (pt_a, 1)), ("p", (n, 1), (pt_v, 1)), ("p", (n, 2), (pt_a, 1))]
            else:
                jobs += [("o", n, (oT_ok, 1))]
        jobs += [("wo", i, (x2_ok, 2)) for i in range(NT // 2)]
        jobs += [("xf", k, A) for k in range(NK)]
        jobs += [("rt", 0, V)]
        at = {(n, i): k for k, (n, i, _) in enumerate(jobs)}

        def read_by(k):
            return sum(j[2][1] for j in jobs[:k + 1] if j[2][0] is jobs[k][2][0])

        def where(name, i=0):
            return bank[at[name, i] % 8]

        def fill(eng, name, i=0):
            k = at[name, i] - 8
            if k >= 0:
                eng.wait_ge(jobs[k][2][0], read_by(k))

        def full(eng, name, i=0):
            eng.wait_ge(pe, at[name, i] + 1)

        TILES = (3, 2, 0, 1)

        def score_place(n, i):
            b_ = where("s", (n, i if i else 2))
            c0 = 3 * P if i == 0 else 0
            return b_[:, c0:c0 + (i + 1) * P]

        P_AT = {3: 0, 2: 4 * P, 0: 7 * P, 1: 8 * P}
        T_JOB = {0: (0, 0), 1: (1, 0), 3: (1, 3 * P), 2: (2, 0)}
        T_AT = {0: 0, 1: 4 * P, 3: 7 * P, 2: 8 * P}

        with nc.Fori(0, BATCH) as b, turn(nc, s) as block:
            @block.tensor
            def _(te):
                for k in range(NK):
                    for t in range(NT):
                        te.wait_ge(xr_ok, t + 1)
                        i = te.transpose(where("xT", k)[:, t * P:(t + 1) * P], xr[:, t, k * P:(k + 1) * P], ident[:])
                    i.then_inc(pe, 1)
                te.wait_ge(act_free, 2)
                for t in range(NT):
                    for k in range(NK):
                        i = te.matmul(where("v", t)[:], xT[:, k, t * P:(t + 1) * P], wv_sb[:, k, :],
                                      start=k == 0, stop=k == NK - 1)
                    i.then_inc(pe, 1)

                def project(name, n, w):
                    fill(te, name, n)
                    for k in range(NK):
                        i = te.matmul(where(name, n)[:], w[:, k, n * D:(n + 1) * D], xT[:, k, :],
                                      start=k == 0, stop=k == NK - 1)
                    i.then_inc(pe, 1)

                for g in range(KVH):
                    project("k", g, wk_sb)
                for what, n in steps:
                    if what == "q":
                        project("q", n, wq_sb)
                    elif what == "s":
                        te.wait_ge(qk_ok, KVH + n + 1)
                        for i in TILES:
                            if i:
                                fill(te, "s", (n, i))
                            out = score_place(n, i)
                            te.matmul(out, qT[:, n % 2, i * P:(i + 1) * P], kT[:, n // GRP, 0:(i + 1) * P],
                                      start=True, stop=False)
                            m = te.matmul(out[:, i * P:(i + 1) * P], identb[:], future[:], start=False, stop=True)
                            if i != 2:
                                m.then_inc(pe, 1)
                    elif what == "p":
                        te.wait_ge(p_ok, NT * (n + 1))
                        for job, js in ((0, (0,)), (1, (1, 3)), (2, (2,))):
                            fill(te, "p", (n, job))
                            for j in js:
                                for i in range(j, NT):
                                    c = T_JOB[j][1] + (i - j) * P
                                    m = te.transpose(where("p", (n, job))[:, c:c + P],
                                                     pr[:, n % 2, P_AT[i] + j * P:P_AT[i] + (j + 1) * P], ident[:])
                            m.then_inc(pe, 1)
                    else:
                        fill(te, "o", n)
                        te.wait_ge(pt_a, 2 * (n + 1))
                        te.wait_ge(pt_v, n + 1)
                        for j in range(NT):
                            m = te.matmul(where("o", n)[:, j * P:SEQ], v[:, j, n // GRP * D:(n // GRP + 1) * D],
                                          pt[:, n % 2, T_AT[j]:T_AT[j] + (NT - j) * P],
                                          start=j == 0, stop=j == NT - 1)
                        m.then_inc(pe, 1)
                te.wait_ge(oT_ok, QH)
                for q in range(NT // 2):
                    fill(te, "wo", q)
                    for t in (2 * q, 2 * q + 1):
                        for n in range(QH):
                            m = te.matmul(where("wo", q)[:, t % 2 * HID:(t % 2 + 1) * HID],
                                          oT[:, n, t * P:(t + 1) * P], wo_sb[:, n, :],
                                          start=n == 0, stop=n == QH - 1)
                    m.then_inc(pe, 1)
                for k in range(NK):
                    fill(te, "xf", k)
                    for t in range(NT):
                        te.wait_ge(xf_ok, t + 1)
                        i = te.transpose(where("xf", k)[:, t * P:(t + 1) * P], xr[:, t, k * P:(k + 1) * P], ident[:])
                    i.then_inc(pe, 1)
                te.wait_ge(act_free, read_by(at["xf", 1]))
                fill(te, "rt")
                for t in range(NT):
                    for k in range(NK):
                        i = te.matmul(where("rt")[:, t * NE:(t + 1) * NE], xfs[:, k, t * P:(t + 1) * P],
                                      gate_sb[:, k, :], start=k == 0, stop=k == NK - 1)
                i.then_inc(pe, 1)

            @block.scalar
            def _(act):
                logs = [0]

                def rsqrt(out, val, eps):
                    logs[0] += 1
                    act.activation(lnv[:], val, ACT.Ln, bias=eps[:, 0:1]).then_inc(lnv_ok, 1)
                    act.wait_ge(lnv_ok, logs[0])
                    act.activation(out, lnv[:], ACT.Exp, scale=-0.5).then_inc(r_ok, 1)

                act.wait_ge(mv_ok, NT)
                rsqrt(r1[:], mv[:, :, 1], eps_ln)
                act.wait_ge(m2_ok, 2)
                rsqrt(r2[:], m2[:], eps_rms)
                for k in range(NK):
                    full(act, "xT", k)
                    act.activation(xT[:, k, :], where("xT", k)[:], ACT.Copy, scale=ln1_sb[:, k:k + 1]).then_inc(act_free, 1)
                for t in range(NT):
                    full(act, "v", t)
                    act.activation(v[:, t, :], where("v", t)[:], ACT.Copy).then_inc(act_free, 1)

                for what, n in steps:
                    if what == "s":
                        for m, i in enumerate(TILES):
                            act.wait_ge(mx_ok, NT * n + (3 if m == 1 else m + 1))
                            if n >= 2 and m == 0:
                                full(act, "p", (n - 2, 2))
                            act.activation(pr[:, n % 2, P_AT[i]:P_AT[i] + (i + 1) * P], score_place(n, i), ACT.Exp,
                                           bias=nmax[:, n % 2, i:i + 1], scale=D ** -0.5,
                                           accum_out=rsum[:, n % 2, i:i + 1]).then_inc(e_ok, 1)
                    elif what == "p":
                        for job, c in ((0, 4 * P), (2, 2 * P)):
                            full(act, "p", (n, job))
                            if n >= 2 and job == 0:
                                full(act, "o", n - 2)
                            c0 = T_AT[job]
                            act.activation(pt[:, n % 2, c0:c0 + c], where("p", (n, job))[:, 0:c],
                                           ACT.Copy).then_inc(pt_a, 1)
                    elif what == "o":
                        full(act, "o", n)
                        act.activation(oT[:, n, :], where("o", n)[:], ACT.Copy).then_inc(oT_ok, 1)
                for t in range(NT):
                    act.wait_ge(x2_ok, t + 1)
                    if t:
                        act.wait_ge(sq_ok, t)
                    act.activation(sq[:], x2s[:, t, :], ACT.Square, scale=HID ** -0.5,
                                   accum_out=ssq[:, t:t + 1]).then_inc(sq_ok, 1)
                act.wait_ge(sq_ok, NT)
                rsqrt(ssq[:], ssq[:], eps_rms)
                for k in range(NK):
                    full(act, "xf", k)
                    act.activation(xfs[:, k, :], where("xf", k)[:], ACT.Copy, scale=ln2_sb[:, k:k + 1]).then_inc(act_free, 1)
                act.wait_ge(rt, NT)
                for t in range(NT):
                    act.activation(pb[:, t, :], where("rt")[:, t * NE:(t + 1) * NE], ACT.Exp,
                                   bias=lmax[:, t:t + 1], accum_out=lsum[:, t:t + 1]).then_inc(rt_a, 1)

            @block.vector
            def _(dve):
                for t in range(NT):
                    src = x1[:, bass.ds(b * (NT * HID) + t * HID, HID)]
                    dve.bn_stats(st6[:, t, :], src).then_inc(stat, 1)
                    dve.wait_ge(stat, t + 1)
                    dve.bn_aggr(mv[:, t, :], st6[:, t, :]).then_inc(mv_ok, 1)
                dve.wait_ge(r_ok, 1)
                dve.tensor_tensor(m2[:], mv[:, :, 1], r1[:], ALU.mult).then_inc(m2_ok, 1)
                dve.wait_ge(m2_ok, 1)
                dve.tensor_tensor(m2[:], m2[:], r1[:], ALU.mult).then_inc(m2_ok, 1)
                for t in range(NT):
                    src = x1[:, bass.ds(b * (NT * HID) + t * HID, HID)]
                    dve.tensor_scalar(h[:, t, :], src, mv[:, t, 0:1], r1[:, t:t + 1],
                                      ALU.subtract, ALU.mult).then_inc(h_ok, 1)
                dve.wait_ge(r_ok, 2)
                for t in range(NT):
                    dve.wait_ge(h_ok, t + 1)
                    dve.tensor_scalar(xr[:, t, :], h[:, t, :], r2[:, t:t + 1], None, ALU.mult).then_inc(xr_ok, 1)

                def rotate(name, n, m):
                    full(dve, name, n)
                    if m >= 2:
                        dve.wait_ge(qk_ok, m - 1)
                    src = where(name, n)
                    half = P // 2
                    dve.tensor_tensor(rc[:, m % 2, :], src[:], cos_sb[:], ALU.mult).then_inc(rot, 1)
                    dve.tensor_tensor(rs[0:half, m % 2, :], src[half:P, :], sin_sb[0:half, :], ALU.mult).then_inc(rot, 1)
                    dve.tensor_tensor(rs[half:P, m % 2, :], src[0:half, :], sin_sb[half:P, :], ALU.mult).then_inc(rot, 1)

                for g in range(KVH):
                    rotate("k", g, g)
                for what, n in steps:
                    if what == "q":
                        rotate("q", n, KVH + n)
                    elif what == "s":
                        for m, i in enumerate(TILES):
                            full(dve, "s", (n, i if i else 2))
                            if n >= 2 and m == 0:
                                dve.wait_ge(e_ok, NT * (n - 1))
                            dve.tensor_reduce(nmax_r[:, n % 2, i:i + 1], score_place(n, i), AX_X, ALU.max,
                                              negate=True).then_inc(mxr, 1)
                            dve.wait_ge(mxr, NT * n + m + 1)
                            dve.tensor_scalar(nmax[:, n % 2, i:i + 1], nmax_r[:, n % 2, i:i + 1], D ** -0.5, None,
                                              ALU.mult).then_inc(mx_ok, 1)
                        for m, i in enumerate(TILES):
                            dve.wait_ge(e_ok, NT * n + m + 1)
                            dve.reciprocal(rrec[:, n % 2, i:i + 1], rsum[:, n % 2, i:i + 1]).then_inc(rec_ok, 1)
                            dve.wait_ge(rec_ok, NT * n + m + 1)
                            a = pr[:, n % 2, P_AT[i]:P_AT[i] + (i + 1) * P]
                            dve.tensor_scalar(a, a, rrec[:, n % 2, i:i + 1], None, ALU.mult).then_inc(p_ok, 1)
                    elif what == "p":
                        full(dve, "p", (n, 1))
                        if n >= 2:
                            full(dve, "o", n - 2)
                        dve.tensor_copy(pt[:, n % 2, T_AT[1]:T_AT[1] + 4 * P], where("p", (n, 1))[:]).then_inc(pt_v, 1)
                for t in range(NT):
                    full(dve, "wo", t // 2)
                    dve.tensor_tensor(x2s[:, t, :], where("wo", t // 2)[:, t % 2 * HID:(t % 2 + 1) * HID], h[:, t, :],
                                      ALU.add).then_inc(x2_ok, 1)
                dve.wait_ge(r_ok, 3)
                for t in range(NT):
                    dve.tensor_scalar(xr[:, t, :], x2s[:, t, :], ssq[:, t:t + 1], None, ALU.mult).then_inc(xf_ok, 1)
                full(dve, "rt")
                for t in range(NT):
                    dve.tensor_reduce(lmax[:, t:t + 1], where("rt")[:, t * NE:(t + 1) * NE], AX_X, ALU.max,
                                      negate=True).then_inc(rt, 1)
                dve.wait_ge(rt_a, NT)
                dve.reciprocal(lrec[:], lsum[:]).then_inc(rt, 1)
                dve.wait_ge(rt, NT + 1)
                dve.tensor_tensor(pb[:], pb[:], spread(lrec[:], NE), ALU.mult).then_inc(rt, 1)
                dve.wait_ge(rt, NT + 2)
                dve.tensor_tensor(pbb[:], pb[:], be_sb[:].rearrange("p (o e) -> p o e", o=1).broadcast_to(
                    (P, NT, NE)), ALU.add).then_inc(rt, 1)
                dve.wait_ge(rt, NT + 3)
                for t in range(NT):
                    dve.max(top[:, t, :], pbb[:, t, :]).then_inc(rt, 1)
                    dve.wait_ge(rt, NT + 4 + 2 * t)
                    dve.max_index(topi[:, t, :], top[:, t, :], pbb[:, t, :]).then_inc(rt, 1)
                dve.wait_ge(rt, 3 * NT + 3)
                dve.tensor_copy(topf[:], topi[:, :, 0:TOPK]).then_inc(rt, 1)
                dve.wait_ge(rt, 3 * NT + 4)
                m = 3 * NT + 4
                for k in range(TOPK):
                    dst = sel if k == 0 else one
                    dve.tensor_tensor(dst[:], col_no[:].rearrange("p (o e) -> p o e", o=1).broadcast_to((P, NT, NE)),
                                      topf[:, :, k:k + 1].broadcast_to((P, NT, NE)), ALU.is_equal).then_inc(rt, 1)
                    m += 1
                    dve.wait_ge(rt, m)
                    if k:
                        dve.tensor_tensor(sel[:], sel[:], one[:], ALU.add).then_inc(rt, 1)
                        m += 1
                        dve.wait_ge(rt, m)
                dve.tensor_tensor(sel[:], sel[:], pb[:], ALU.mult).then_inc(rt, 1)
                dve.wait_ge(rt, m + 1)
                dve.tensor_reduce(lsum[:], sel[:], AX_X, ALU.add).then_inc(rt, 1)
                dve.wait_ge(rt, m + 2)
                dve.tensor_scalar(lsum[:], lsum[:], NORM_MIN, None, ALU.max).then_inc(rt, 1)
                dve.wait_ge(rt, m + 3)
                dve.reciprocal(lrec[:], lsum[:]).then_inc(rt, 1)
                dve.wait_ge(rt, m + 4)
                dve.tensor_tensor(sel[:], sel[:], spread(lrec[:], NE), ALU.mult).then_inc(cw_ok, 1)

            @block.gpsimd
            def _(pool):
                for m in range(KVH + QH):
                    pool.wait_ge(rot, 3 * (m + 1))
                    n = m - KVH
                    if n >= 2:
                        full(pool, "s", (n - 2, 1))
                    dst = kT[:, m, :] if n < 0 else qT[:, n % 2, :]
                    pool.tensor_tensor(dst, rc[:, m % 2, :], rs[:, m % 2, :], ALU.add).then_inc(qk_ok, 1)

            @block.sync
            def _(sp):
                sp.wait_ge(x2_ok, NT)
                sp.dma_start(x2[:, bass.ds(b * (NT * HID), NT * HID)].rearrange("p (t h) -> p t h", h=HID),
                             x2s[:]).then_inc(kept, 16)
                sp.wait_ge(act_free, read_by(at["xf", 1]))
                sp.dma_start(xfT[:, :, bass.ds(b * SEQ, SEQ)], xfs[:]).then_inc(kept, 16)
                sp.wait_ge(cw_ok, 1)
                sp.dma_start(cw[:, bass.ds(b * (NT * NE), NT * NE)].rearrange("p (t e) -> p t e", e=NE),
                             sel[:]).then_inc(kept, 16)
                sp.wait_ge(kept, 48)


SLOTS = 4
NB = BATCH


def moe_phase(nc, weg, weu, wed, wsg, wsu, wsd, x1, x2, xfT, cw, out):
    with ExitStack() as ctx:
        sb, ps, sem = open_tools(nc, ctx)
        wg = sb("wg", [P, SLOTS, NK, EI])
        wu = sb("wu", [P, SLOTS, NK, EI])
        wd = sb("wd", [P, SLOTS, HID])
        sgl = sb("sgl", [P, 2, SEQ])
        hT = sb("hT", [P, 2, SEQ])
        eps_ln = sb("f_eps_ln", [P, 1])
        st6 = sb("f_st6", [P, NB * NT, 6])
        mv = sb("f_mv", [P, NB * NT, 2])
        lnv = sb("f_lnv", [P, NB * NT])
        r1 = sb("f_r1", [P, NB * NT])
        bank = [ps(f"f_bank{i}", [P, 512]) for i in range(8)]

        def experts(block, s, slots, load, weight):
            w_in = [s(f"w_in{i}_{slots}") for i in range(slots)]
            pe, silu_ok, h_ok, added = s(f"f_pe{slots}"), s(f"silu_ok{slots}"), s(f"fh_ok{slots}"), s(f"added{slots}")
            work = [(e, n) for e in range(slots) for n in range(NB)]
            jobs = []
            for i in range(len(work) + 1):
                if i < len(work):
                    jobs += [("g", i, (silu_ok, 1)), ("u", i, (h_ok, 1))]
                if i:
                    jobs += [("y", (i - 1, q), (added, 2)) for q in range(NT // 2)]
            at = {(n, i): k for k, (n, i, _) in enumerate(jobs)}

            def read_by(k):
                return sum(j[2][1] for j in jobs[:k + 1] if j[2][0] is jobs[k][2][0])

            def where(name, i=0):
                return bank[at[name, i] % 8]

            def fill(eng, name, i=0):
                k = at[name, i] - 8
                if k >= 0:
                    eng.wait_ge(jobs[k][2][0], read_by(k))

            def full(eng, name, i=0):
                eng.wait_ge(pe, at[name, i] + 1)

            @block.sync
            def _(sp):
                for e in range(slots):
                    load(sp, e, w_in[e])

            @block.tensor
            def _(te):
                for i in range(len(work) + 1):
                    if i < len(work):
                        e, n = work[i]
                        if n == 0:
                            te.wait_ge(w_in[e], 3 * 16)
                        for name, w in (("g", wg), ("u", wu)):
                            fill(te, name, i)
                            for k in range(NK):
                                m = te.matmul(where(name, i)[:], w[:, e, k, :], xfT[:, k, n * SEQ:(n + 1) * SEQ],
                                              start=k == 0, stop=k == NK - 1)
                            m.then_inc(pe, 1)
                    if i:
                        e, n = work[i - 1]
                        te.wait_ge(h_ok, i)
                        for q in range(NT // 2):
                            fill(te, "y", (i - 1, q))
                            for t in range(2):
                                c = (2 * q + t) * P
                                m = te.matmul(where("y", (i - 1, q))[:, t * HID:(t + 1) * HID],
                                              hT[:, (i - 1) % 2, c:c + P], wd[:, e, :], start=True, stop=True)
                            m.then_inc(pe, 1)

            @block.scalar
            def _(act):
                for i in range(len(work)):
                    full(act, "g", i)
                    if i >= 2:
                        act.wait_ge(h_ok, i - 1)
                    act.activation(sgl[:, i % 2, :], where("g", i)[:], ACT.Silu).then_inc(silu_ok, 1)

            @block.vector
            def _(dve):
                for i in range(len(work) + 1):
                    if i < len(work):
                        full(dve, "u", i)
                        dve.wait_ge(silu_ok, i + 1)
                        if i >= 2:
                            full(dve, "y", (i - 2, NT // 2 - 1))
                        dve.tensor_tensor(hT[:, i % 2, :], sgl[:, i % 2, :], where("u", i)[:],
                                          ALU.mult).then_inc(h_ok, 1)
                    if i:
                        e, n = work[i - 1]
                        for t in range(NT):
                            full(dve, "y", (i - 1, t // 2))
                            if i - 1 >= NB:
                                dve.wait_ge(added, (i - 1 - NB) * NT + t + 1)
                            acc = x2[:, (n * NT + t) * HID:(n * NT + t + 1) * HID]
                            dve.scalar_tensor_tensor(
                                out=acc, in0=where("y", (i - 1, t // 2))[:, t % 2 * HID:(t % 2 + 1) * HID],
                                scalar=weight(n * NT + t, e), in1=acc, op0=ALU.mult, op1=ALU.add).then_inc(added, 1)

        s = Sems(sem)

        def load_shared(sp, e, ready):
            sp.dma_start(wg[:, e, :, :], wsg.rearrange("(k p) i -> p k i", p=P)).then_inc(ready, 16)
            sp.dma_start(wu[:, e, :, :], wsu.rearrange("(k p) i -> p k i", p=P)).then_inc(ready, 16)
            sp.dma_start(wd[:, e, :], wsd).then_inc(ready, 16)

        with turn(nc, s) as block:
            experts(block, s, 1, load_shared, lambda t, e: 1.0)

        s = Sems(sem)
        with nc.Fori(0, NE // SLOTS) as r, turn(nc, s) as block:
            def load(sp, e, ready):
                rows = bass.ds(r * (SLOTS * HID) + e * HID, HID)
                sp.dma_start(wg[:, e, :, :], weg[rows, :].rearrange("(k p) i -> p k i", p=P)).then_inc(ready, 16)
                sp.dma_start(wu[:, e, :, :], weu[rows, :].rearrange("(k p) i -> p k i", p=P)).then_inc(ready, 16)
                sp.dma_start(wd[:, e, :], wed[bass.ds(r * (SLOTS * EI) + e * EI, EI), :]).then_inc(ready, 16)

            experts(block, s, SLOTS, load, lambda t, e: cw[:, bass.ds(r * SLOTS + (t * NE + e), 1)])

        s = Sems(sem)
        stat, mv_ok, eps_ok, lnv_ok, r_ok, n_ok, fin_ok, stored = (
            s("f_stat"), s("f_mv_ok"), s("f_eps_ok"), s("f_lnv_ok"), s("f_r_ok"), s("f_n_ok"), s("f_fin"), s("f_stored"))
        N = NB * NT
        with nc.Block() as block:
            @block.vector
            def _(dve):
                dve.memset(eps_ln[:], LN_EPS).then_inc(eps_ok, 1)
                for t in range(N):
                    dve.bn_stats(st6[:, t, :], x2[:, t * HID:(t + 1) * HID]).then_inc(stat, 1)
                    dve.wait_ge(stat, t + 1)
                    dve.bn_aggr(mv[:, t, :], st6[:, t, :]).then_inc(mv_ok, 1)
                dve.wait_ge(r_ok, 1)
                for t in range(N):
                    a = x2[:, t * HID:(t + 1) * HID]
                    dve.tensor_scalar(a, a, mv[:, t, 0:1], r1[:, t:t + 1], ALU.subtract, ALU.mult).then_inc(n_ok, 1)
                    dve.wait_ge(n_ok, t + 1)
                    dve.tensor_tensor(a, a, x1[:, t * HID:(t + 1) * HID], ALU.add).then_inc(fin_ok, 1)

            @block.scalar
            def _(act):
                act.wait_ge(eps_ok, 1)
                act.wait_ge(mv_ok, N)
                act.activation(lnv[:], mv[:, :, 1], ACT.Ln, bias=eps_ln[:, 0:1]).then_inc(lnv_ok, 1)
                act.wait_ge(lnv_ok, 1)
                act.activation(r1[:], lnv[:], ACT.Exp, scale=-0.5).then_inc(r_ok, 1)

            @block.sync
            def _(sp):
                for n in range(NB):
                    sp.wait_ge(fin_ok, NT * (n + 1))
                    sp.dma_start(out[n * SEQ:(n + 1) * SEQ, :].rearrange("(t p) h -> p t h", p=P),
                                 x2[:, n * NT * HID:(n + 1) * NT * HID].rearrange("p (t h) -> p t h", h=HID)
                                 ).then_inc(stored, 16)
                sp.wait_ge(stored, 16 * NB)




def mamba_attention_moe(nc, x, winT, conv_w, conv_b, a_log, dt_bias, d_skip, norm_w, woutT, ln1, ln2, wq, wk, wv, wo,
                        cos, sin, gateT, bias_e, weg, weu, wed, wsg, wsu, wsd, out):
    with ExitStack() as ctx:
        sb, _, _ = open_tools(nc, ctx)
        ident = sb("ident", [P, P])
        x1 = sb("x1", [P, BATCH * NT * HID])
        mamba_phase(nc, x, winT, conv_w, conv_b, a_log, dt_bias, d_skip, norm_w, woutT, ident, x1)
        x2 = sb("x2", [P, BATCH * NT * HID])
        xfT = sb("xfT", [P, NK, BATCH * SEQ])
        cw = sb("cw_all", [P, BATCH * NT * NE])
        attention_phase(nc, wq, wk, wv, wo, ln1, ln2, cos, sin, gateT, bias_e, ident, x1, x2, xfT, cw)
        moe_phase(nc, weg, weu, wed, wsg, wsu, wsd, x1, x2, xfT, cw, out)


def rope_tables(seq, width):
    import numpy as np

    one, theta = np.float32(1.0), np.float32(10000.0)
    freq = one / theta ** (np.arange(0, width, 2, dtype=np.float32) / np.float32(width))
    angle = (np.arange(seq, dtype=np.float32)[:, None] * freq[None, :]).astype(np.float64).T
    c, s = np.cos(angle).astype(np.float32), np.sin(angle).astype(np.float32)
    return np.concatenate([c, c]), np.concatenate([-s, s])


def kernel(**inputs):
    import numpy as np
    import concourse.bacc as bacc
    from concourse.bass_utils import run_bass_kernel_spmd

    a = {k: np.asarray(v) for k, v in inputs.items()}

    def columns(w, n):
        return w.reshape(n, P).T

    def halves(w, heads):
        return w.reshape(HID, heads, D // 2, 2).transpose(0, 1, 3, 2).reshape(HID, heads * D)

    cos, sin = rope_tables(SEQ, D)
    arrays = {
        "x_in": a["L0_attn_hidden_states"].reshape(BATCH * SEQ, HID),
        "winT": a["L0_attn_in_proj_w"].T,
        "conv_w": a["L0_attn_conv_w"].reshape(CONV // P, P, TAPS).transpose(1, 0, 2),
        "conv_b": columns(a["L0_attn_conv_b"], CONV // P),
        "a_log": a["L0_attn_A_log"],
        "dt_bias": a["L0_attn_dt_bias"],
        "d_skip": a["L0_attn_D"],
        "norm_w": columns(a["L0_attn_norm_w"], INTER // P),
        "woutT": a["L0_attn_out_proj_w"].T,
        "ln1": columns(a["L0_ffn_ln1_w"], NK),
        "ln2": columns(a["L0_ffn_ln2_w"], NK),
        "wq": halves(a["L0_ffn_wq"], QH),
        "wk": halves(a["L0_ffn_wk"], KVH),
        "wv": a["L0_ffn_wv"],
        "wo": a["L0_ffn_wo"],
        "cos": cos,
        "sin": sin,
        "gateT": a["L0_ffn_gate_w"].T,
        "bias_e": a["L0_ffn_bias_e"],
        "weg": a["L0_ffn_weg"].reshape(NE * HID, EI),
        "weu": a["L0_ffn_weu"].reshape(NE * HID, EI),
        "wed": a["L0_ffn_wed"].reshape(NE * EI, HID),
        "wsg": a["L0_ffn_wsg"],
        "wsu": a["L0_ffn_wsu"],
        "wsd": a["L0_ffn_wsd"],
    }
    arrays = {f"in_{k}": np.ascontiguousarray(v) for k, v in arrays.items()}
    nc = bacc.Bacc("TRN2", target_bir_lowering=False, num_devices=1)
    args = [nc.dram_tensor(k, v.shape, mybir.dt.from_np(v.dtype), kind="ExternalInput").ap()
            for k, v in arrays.items()]
    args.append(nc.dram_tensor("out", (BATCH * SEQ, HID), F32, kind="ExternalOutput").ap())
    mamba_attention_moe(nc, *args)
    r = run_bass_kernel_spmd(nc, [arrays], core_ids=[0])
    return r.results[0]["out"].reshape(BATCH, SEQ, HID)
```

```python
from contextlib import ExitStack, contextmanager

import concourse.bass as bass
from concourse import mybir

F32 = mybir.dt.float32
BF16 = mybir.dt.bfloat16
ALU = mybir.AluOpType
ACT = mybir.ActivationFunctionType
AX_X = mybir.AxisListType.X
P = 128

BATCH, SEQ, HID = 4, 512, 256
NT = SEQ // P
NK = HID // P
INTER, STATE, HEADS = 512, 128, 32
HD = INTER // HEADS
CONV = INTER + 2 * STATE
TAPS = 4
CH = 64
NCH = SEQ // CH
HG = HEADS // 2
DT0 = INTER + CONV
LN_EPS = 1e-5
RMS_EPS = 1e-6


def open_tools(nc, ctx):
    def sb(name, shape, dt=F32):
        return ctx.enter_context(nc.sbuf_tensor(name, shape, dt))

    def ps(name, shape, dt=F32):
        return ctx.enter_context(nc.psum_tensor(name, shape, dt))

    def sem(name):
        return ctx.enter_context(nc.semaphore(name))

    return sb, ps, sem


def spread(ap, n):
    return ap.rearrange("p (a o) -> p a o", o=1).broadcast_to((ap.shape[0], ap.shape[1], n))


class Sems:

    def __init__(self, sem):
        self.sem, self.all = sem, []

    def __call__(self, name):
        s = self.sem(name)
        self.all.append(s)
        return s


def clear(nc, sems):
    for s in sems.all:
        nc.sync.sem_clear(s)
    nc.all_engine_barrier()


@contextmanager
def turn(nc, sems):
    with nc.Block() as block:
        yield block
    clear(nc, sems)


def mamba_phase(nc, x, winT, conv_w, conv_b, a_log, dt_bias, d_skip, norm_w, woutT, ident, x1, dbg=None):
    with ExitStack() as ctx:
        sb, ps, sem = open_tools(nc, ctx)
        w_in = sb("w_in", [P, NK, DT0 + HEADS])
        w_out = sb("w_out", [P, INTER // P, HID])
        nw = sb("nw", [P, INTER // P])
        cw = sb("cw", [P, CONV // P, TAPS])
        cb = sb("cb", [P, CONV // P])
        neg_a = sb("neg_a", [P, HEADS])
        dtb = sb("dtb", [P, HEADS])
        dsk = sb("dsk", [P, HEADS])
        tri = sb("tri", [P, P])
        suf = sb("suf", [P, P])
        half = sb("half", [P, 2, P])
        causal = sb("causal", [P, CH])
        segm = sb("segm", [P, CH, P], BF16)

        x_sb = sb("x_sb", [P, NT, HID])
        xn = sb("xn", [P, NT, HID])
        lnv = sb("lnv", [P, NT])
        eps_col = sb("eps_col", [P, 1])
        st6 = sb("st6", [P, NT, 6])
        mv = sb("mv", [P, NT, 2])
        rstd = sb("rstd", [P, NT])
        xnT = sb("xnT", [P, NK, SEQ])
        xc = sb("xc", [P, CONV // P, SEQ])
        bdup = sb("bdup", [P, NCH, 2, CH])
        sg = sb("sg", [P, NT, INTER])
        dt = sb("dt", [P, NT, HEADS])
        z = sb("z", [P, NT, HEADS])
        az = sb("az", [P, NT, HEADS])
        et = sb("et", [P, NT, HEADS])
        u = sb("u", [P, NT, HEADS])
        lu = sb("lu", [P, NT, HEADS])
        ad = sb("ad", [P, NT, HEADS])
        dsuf = sb("dsuf", [P, NT, HEADS])
        dec = sb("dec", [P, 4, NT, HEADS])
        adl = sb("adl", [P, NT, 2, HG])
        adr = sb("adr", [P, NT, 2, HG])
        adp = sb("adp", [P, 3, NCH * HG], BF16)
        es = sb("es", [P, 2, 4, NCH * HG])
        mt = sb("mt", [P, NCH * HG, CH])
        gm = sb("gm", [P, NCH, CH])
        xtok = sb("xtok", [P, NT, INTER])
        btok = sb("btok", [P, NT, STATE])
        xbd = sb("xbd", [P, NCH, HG, 2 * HD])
        xds = sb("xds", [P, NT, INTER])
        xd = sb("xd", [P, NT, INTER])
        stt = sb("stt", [P, NCH, INTER])
        y = sb("y", [P, NT, INTER])
        sq = sb("sq", [P, INTER])
        ssq = sb("ssq", [P, NT])
        yT = xc
        o_sb = xn
        bank = [ps(f"bank{i}", [P, 512]) for i in range(8)]

        su = Sems(sem)
        loaded, masks, folded, a_ready = su("m_loaded"), su("m_masks"), su("m_folded"), su("m_a_ready")

        with nc.Block() as block:
            @block.sync
            def _(sp):
                sp.dma_start(w_in[:], winT.rearrange("(k p) n -> p k n", p=P)).then_inc(loaded, 16)
                sp.dma_start(w_out[:], woutT.rearrange("(k p) n -> p k n", p=P)).then_inc(loaded, 16)
                sp.dma_start(nw[:], norm_w).then_inc(loaded, 16)
                sp.dma_start(cw[:], conv_w).then_inc(loaded, 16)
                sp.dma_start(cb[:], conv_b).then_inc(loaded, 16)
                for dst, src in ((neg_a, a_log), (dtb, dt_bias), (dsk, d_skip)):
                    sp.dma_start(dst[:], src.rearrange("(o h) -> o h", o=1).broadcast_to((P, HEADS))).then_inc(loaded, 16)
                sp.wait_ge(loaded, 8 * 16)

            @block.gpsimd
            def _(pool):
                pool.memset(ident[:], 0.0)
                pool.memset(tri[:], 1.0)
                pool.memset(suf[:], 1.0)
                pool.memset(segm[:], 1.0)
                pool.memset(stt[:, 0, :], 0.0)
                pool.memset(xbd[:], 0.0)
                pool.memset(eps_col[:], LN_EPS)
                pool.memset(half[:, 0, :], 1.0)
                pool.memset(half[:, 1, :], 1.0).then_inc(masks, 1)
                pool.wait_ge(masks, 1)
                pool.affine_select(out=ident[:], in_=ident[:], compare_op=ALU.not_equal, fill=1.0, base=0,
                                   pattern=[[-1, P]], channel_multiplier=1)
                pool.affine_select(out=tri[:], in_=tri[:], compare_op=ALU.is_ge, fill=0.0, base=0,
                                   pattern=[[1, P]], channel_multiplier=-1)
                pool.affine_select(out=suf[:], in_=suf[:], compare_op=ALU.is_ge, fill=0.0, base=-1,
                                   pattern=[[-1, P]], channel_multiplier=1).then_inc(masks, 1)
                pool.wait_ge(masks, 2)
                pool.memset(half[0:CH, 1, :], 0.0)
                pool.memset(tri[0:CH, CH:P], 0.0).then_inc(masks, 1)
                pool.wait_ge(masks, 3)
                pool.memset(half[CH:P, 0, :], 0.0)
                pool.memset(suf[CH:P, 0:CH], 0.0).then_inc(masks, 1)
                pool.wait_ge(masks, 4)
                for hh in range(2):
                    v = segm[:, :, hh * CH:(hh + 1) * CH]
                    pool.affine_select(out=v, in_=v, compare_op=ALU.is_ge, fill=0.0, base=-1 - CH * hh,
                                       pattern=[[0, CH], [-1, CH]], channel_multiplier=1).then_inc(masks, 1)
                pool.wait_ge(masks, 6)
                for hh in range(2):
                    v = segm[:, :, hh * CH:(hh + 1) * CH]
                    pool.affine_select(out=v, in_=v, compare_op=ALU.is_ge, fill=0.0, base=CH * hh,
                                       pattern=[[1, CH], [0, CH]], channel_multiplier=-1).then_inc(masks, 1)
                for hh in range(2):
                    h = slice(hh * CH, (hh + 1) * CH)
                    pool.wait_ge(masks, 8 + hh)
                    pool.tensor_copy(causal[h, :], tri[h, h]).then_inc(masks, 1)

            @block.scalar
            def _(act):
                act.wait_ge(loaded, 8 * 16)
                act.activation(az[:, 0, :], neg_a[:], ACT.Exp).then_inc(a_ready, 1)

            @block.vector
            def _(dve):
                dve.wait_ge(loaded, 8 * 16)
                for k in range(INTER // P):
                    dve.tensor_scalar(w_out[:, k, :], w_out[:, k, :], nw[:, k:k + 1], None, ALU.mult)
                dve.wait_ge(a_ready, 1)
                dve.tensor_scalar(neg_a[:], az[:, 0, :], -1.0, None, ALU.mult).then_inc(folded, 1)
        clear(nc, su)

        s = Sems(sem)
        x_in = s("x_in")
        stat, mv_ok, rstd_ok, xn_ok = s("stat"), s("mv_ok"), s("rstd_ok"), s("xn_ok")
        pe = s("pe_banks")
        act_free, dve_free = s("act_free"), s("dve_free")
        tap, conv_ok = s("tap"), s("conv_ok")
        bdup_ok = s("bdup_ok")
        cid, lnv_ok = s("cid"), s("lnv_ok")
        gate_ok = s("gate_ok")
        dts, dts_a, ad_ok, adp_ok = s("dts"), s("dts_a"), s("ad_ok"), s("adp_ok")
        dec_ok, es_ok, es_used, mt_ok, gm_ok = s("dec_ok"), s("es_ok"), s("es_used"), s("mt_ok"), s("gm_ok")
        tok_ok, xbd_ok, xds_ok, xd_ok, dsuf_ok = s("tok_ok"), s("xbd_ok"), s("xds_ok"), s("xd_ok"), s("dsuf_ok")
        carried, state_ok = s("carried"), s("state_ok")
        ych, y_ok, sq_ok = s("ych"), s("y_ok"), s("sq_ok")
        out_ok, och, x1_ok = s("out_ok"), s("och"), s("x1_ok")

        A, V = (act_free, 1), (dve_free, 1)
        jobs = [("xnT", 0, A), ("xnT", 1, V), ("dt", 0, V)]
        jobs += [("conv", c, (tap, TAPS - 1)) for c in (4, 5, 0, 1, 2, 3)]
        jobs += [("gate", t, A) for t in range(NT)]
        jobs += [("bT", 0, A), ("g", 0, V)]
        jobs += [("xT", t, A) for t in range(NT)]
        jobs += [("dec", 0, A)]
        jobs += [("seg", i, A) for i in range(CH // 4)]
        jobs += [("st", c, (state_ok, 1)) for c in range(NCH - 1)]
        for t in range(NT):
            jobs += [("off", t, V), ("diag", t, V)]
        jobs += [("yT", c, A) for c in range(INTER // P)]
        jobs += [("out", i, (out_ok, 2)) for i in range(NT // 2)]
        at = {(n, i): k for k, (n, i, _) in enumerate(jobs)}

        def read_by(k):
            return sum(j[2][1] for j in jobs[:k + 1] if j[2][0] is jobs[k][2][0])

        def where(name, i=0):
            return bank[at[name, i] % 8]

        def fill(eng, name, i=0):
            k = at[name, i] - 8
            if k >= 0:
                eng.wait_ge(jobs[k][2][0], read_by(k))

        def full(eng, name, i=0):
            eng.wait_ge(pe, at[name, i] + 1)

        def free_no(name, i=0):
            return read_by(at[name, i])

        CONV_ORDER = [i for n, i, _ in jobs if n == "conv"]
        with nc.Fori(0, BATCH) as b, turn(nc, s) as block:
            @block.sync
            def _(sp):
                sp.dma_start(x_sb[:], x[bass.ts(b, SEQ), :].rearrange("(t p) h -> p t h", p=P)).then_inc(x_in, 16)

            @block.tensor
            def _(te):
                for k in range(NK):
                    for t in range(NT):
                        te.wait_ge(xn_ok, t + 1)
                        i = te.transpose(where("xnT", k)[:, t * P:(t + 1) * P], xn[:, t, k * P:(k + 1) * P], ident[:])
                    i.then_inc(pe, 1)
                te.wait_ge(act_free, 1)
                te.wait_ge(dve_free, 1)
                for t in range(NT):
                    for k in range(NK):
                        i = te.matmul(where("dt")[:, t * HEADS:(t + 1) * HEADS], xnT[:, k, t * P:(t + 1) * P],
                                      w_in[:, k, DT0:DT0 + HEADS], start=k == 0, stop=k == NK - 1)
                i.then_inc(pe, 1)
                for c in CONV_ORDER:
                    fill(te, "conv", c)
                    for k in range(NK):
                        i = te.matmul(where("conv", c)[:], w_in[:, k, INTER + c * P:INTER + (c + 1) * P],
                                      xnT[:, k, :], start=k == 0, stop=k == NK - 1)
                    i.then_inc(pe, 1)
                for t in range(NT):
                    fill(te, "gate", t)
                    for k in range(NK):
                        i = te.matmul(where("gate", t)[:], xnT[:, k, t * P:(t + 1) * P], w_in[:, k, 0:INTER],
                                      start=k == 0, stop=k == NK - 1)
                    i.then_inc(pe, 1)
                te.wait_ge(conv_ok, 2)
                fill(te, "bT")
                for t in range(NT):
                    i = te.transpose(where("bT")[:, t * P:(t + 1) * P], xc[:, 4, t * P:(t + 1) * P], ident[:])
                i.then_inc(pe, 1)
                fill(te, "g")
                for c in range(NCH):
                    i = te.matmul(where("g")[:, c * CH:(c + 1) * CH],
                                  bdup[:, c, :, :].rearrange("p a s -> p (a s)"),
                                  xc[:, 5, c * CH:(c + 1) * CH], start=True, stop=True)
                i.then_inc(pe, 1)
                te.wait_ge(conv_ok, 6)
                for t in range(NT):
                    fill(te, "xT", t)
                    for c in range(NT):
                        i = te.transpose(where("xT", t)[:, c * P:(c + 1) * P], xc[:, c, t * P:(t + 1) * P], ident[:])
                    i.then_inc(pe, 1)
                te.wait_ge(ad_ok, 1)
                fill(te, "dec")
                rhs = ad[:].rearrange("p t h -> p (t h)")
                te.matmul(where("dec")[:, 0:P], tri[:], rhs, start=True, stop=True)
                te.matmul(where("dec")[:, P:2 * P], suf[:], rhs, start=True, stop=True)
                for q in range(2):
                    i = te.matmul(where("dec")[:, (2 + q) * P:(3 + q) * P], half[:, q, :], rhs,
                                  start=True, stop=True)
                i.then_inc(pe, 1)
                te.wait_ge(adp_ok, 3)
                for g in range(CH // 4):
                    fill(te, "seg", g)
                    for j in range(4):
                        for part in range(3):
                            i = te.matmul(where("seg", g)[:, j * P:(j + 1) * P], segm[:, 4 * g + j, :],
                                          adp[:, part, :], start=part == 0, stop=part == 2)
                    i.then_inc(pe, 1)
                te.wait_ge(xds_ok, 1)
                te.wait_ge(act_free, free_no("bT"))
                for c in range(NCH - 1):
                    fill(te, "st", c)
                    h = slice(c % 2 * CH, (c % 2 + 1) * CH)
                    te.matmul(where("st", c)[:], btok[h, c // 2, :], xds[h, c // 2, :],
                              start=True, stop=True).then_inc(pe, 1)
                te.wait_ge(xbd_ok, 4)
                te.wait_ge(mt_ok, CH // 4)
                for t in range(NT):
                    fill(te, "off", t)
                    for q in range(2):
                        c = 2 * t + q
                        if c:
                            te.wait_ge(state_ok, c)
                        i = te.matmul(where("off", t)[q * CH:(q + 1) * CH, :], xc[:, 5, c * CH:(c + 1) * CH],
                                      stt[:, c, :], start=True, stop=True)
                    i.then_inc(pe, 1)
                    fill(te, "diag", t)
                    for q in range(2):
                        for g in range(HG):
                            out = where("diag", t)[q * CH:(q + 1) * CH, :].rearrange(
                                "p (a g d) -> p g a d", a=2, g=HG)[:, g, :, :]
                            i = te.matmul(out, mt[:, (2 * t + q) * HG + g, :], xbd[:, 2 * t + q, g, :],
                                          start=True, stop=True)
                    i.then_inc(pe, 1)
                for c in range(INTER // P):
                    fill(te, "yT", c)
                    for t in range(NT):
                        te.wait_ge(y_ok, t + 1)
                        i = te.transpose(where("yT", c)[:, t * P:(t + 1) * P], y[:, t, c * P:(c + 1) * P], ident[:])
                    i.then_inc(pe, 1)
                te.wait_ge(act_free, free_no("yT", INTER // P - 1))
                for j in range(NT // 2):
                    fill(te, "out", j)
                    for t in (2 * j, 2 * j + 1):
                        for c in range(INTER // P):
                            i = te.matmul(where("out", j)[:, t % 2 * HID:(t % 2 + 1) * HID],
                                          yT[:, c, t * P:(t + 1) * P], w_out[:, c, :],
                                          start=c == 0, stop=c == INTER // P - 1)
                    i.then_inc(pe, 1)

            @block.scalar
            def _(act):
                def rsqrt(out, v, eps, n):
                    act.activation(lnv[:], v, ACT.Ln, bias=eps_col[:, 0:1]).then_inc(lnv_ok, 1)
                    act.wait_ge(lnv_ok, n)
                    act.activation(out, lnv[:], ACT.Exp, scale=-0.5).then_inc(rstd_ok, 1)

                act.wait_ge(mv_ok, NT)
                rsqrt(rstd[:], mv[:, :, 1], LN_EPS, 1)

                def silu_conv(n):
                    c = CONV_ORDER[n]
                    act.wait_ge(tap, 3 * (n + 1))
                    if c == 4:
                        act.activation(bdup[:], xc[:, c, :].rearrange("p (c o s) -> p c o s", c=NCH, o=1).broadcast_to(
                            (P, NCH, 2, CH)), ACT.Silu).then_inc(bdup_ok, 1)
                        act.wait_ge(bdup_ok, 1)
                    act.activation(xc[:, c, :], xc[:, c, :], ACT.Silu).then_inc(conv_ok, 1)

                full(act, "xnT", 0)
                act.activation(xnT[:, 0, :], where("xnT", 0)[:], ACT.Copy).then_inc(act_free, 1)
                for n, c in enumerate(CONV_ORDER):
                    full(act, "conv", c)
                    act.activation(xc[:, c, :], where("conv", c)[:], ACT.Identity, bias=cb[:, c:c + 1],
                                   scale=cw[:, c, TAPS - 1:TAPS]).then_inc(cid, 1)
                    if n:
                        silu_conv(n - 1)
                silu_conv(5)
                for t in range(NT):
                    full(act, "gate", t)
                    act.activation(sg[:, t, :], where("gate", t)[:], ACT.Silu).then_inc(act_free, 1)
                full(act, "bT")
                act.activation(btok[:].rearrange("p t n -> p (t n)"), where("bT")[:], ACT.Copy).then_inc(act_free, 1)
                for t in range(NT):
                    full(act, "xT", t)
                    act.activation(xtok[:, t, :], where("xT", t)[:], ACT.Copy).then_inc(act_free, 1)
                act.wait_ge(dts, 1)
                act.activation(et[:], az[:], ACT.Exp, scale=-1.0).then_inc(dts_a, 1)
                act.wait_ge(dts, 2)
                act.activation(lu[:], u[:], ACT.Ln).then_inc(dts_a, 1)
                full(act, "dec")
                act.activation(dec[:].rearrange("p k t h -> p (k t h)"), where("dec")[:], ACT.Exp).then_inc(act_free, 1)
                for g in range(CH // 4):
                    full(act, "seg", g)
                    if g >= 2:
                        act.wait_ge(mt_ok, g - 1)
                    act.activation(es[:, g % 2, :, :].rearrange("p l c -> p (l c)"), where("seg", g)[:],
                                   ACT.Exp).then_inc(act_free, 1)
                for t in range(NT):
                    act.wait_ge(y_ok, t + 1)
                    if t:
                        act.wait_ge(sq_ok, t)
                    act.activation(sq[:], y[:, t, :], ACT.Square, scale=INTER ** -0.5, accum_out=ssq[:, t:t + 1]).then_inc(sq_ok, 1)
                act.wait_ge(sq_ok, NT)
                rsqrt(ssq[:], ssq[:], LN_EPS, 2)
                for c in range(INTER // P):
                    full(act, "yT", c)
                    act.activation(yT[:, c, :], where("yT", c)[:], ACT.Copy).then_inc(act_free, 1)
                act.wait_ge(mv_ok, 2 * NT)
                rsqrt(rstd[:], mv[:, :, 1], LN_EPS, 3)

            @block.vector
            def _(dve):
                def stats(t, src, first):
                    dve.bn_stats(st6[:, t, :], src).then_inc(stat, 1)
                    dve.wait_ge(stat, first + t + 1)
                    dve.bn_aggr(mv[:, t, :], st6[:, t, :]).then_inc(mv_ok, 1)

                dve.wait_ge(x_in, 16)
                for t in range(NT):
                    stats(t, x_sb[:, t, :], 0)
                dve.wait_ge(rstd_ok, 1)
                for t in range(NT):
                    dve.tensor_scalar(xn[:, t, :], x_sb[:, t, :], mv[:, t, 0:1], rstd[:, t:t + 1],
                                      ALU.subtract, ALU.mult).then_inc(xn_ok, 1)
                full(dve, "xnT", 1)
                dve.tensor_copy(xnT[:, 1, :], where("xnT", 1)[:]).then_inc(dve_free, 1)
                full(dve, "dt")
                dve.tensor_tensor(z[:], where("dt")[:, 0:NT * HEADS].rearrange("p (t h) -> p t h", t=NT),
                                  dtb[:].rearrange("p (o h) -> p o h", o=1).broadcast_to((P, NT, HEADS)),
                                  ALU.add).then_inc(dve_free, 1)
                dve.wait_ge(dve_free, 2)
                dve.scalar_tensor_tensor(out=az[:], in0=z[:], scalar=-1.0, in1=z[:], op0=ALU.mult,
                                         op1=ALU.max).then_inc(dts, 1)
                for n, c in enumerate(CONV_ORDER):
                    full(dve, "conv", c)
                    dve.wait_ge(cid, n + 1)
                    for j in range(1, TAPS):
                        if j > 1:
                            dve.wait_ge(tap, 3 * n + j - 1)
                        i = dve.scalar_tensor_tensor(out=xc[:, c, j:SEQ], in0=where("conv", c)[:, 0:SEQ - j],
                                                     scalar=cw[:, c, TAPS - 1 - j:TAPS - j], in1=xc[:, c, j:SEQ],
                                                     op0=ALU.mult, op1=ALU.add)
                        i.then_inc(tap, 1)
                full(dve, "g")
                dve.tensor_tensor(gm[:], where("g")[:].rearrange("p (c l) -> p c l", c=NCH),
                                  causal[:].rearrange("p (o l) -> p o l", o=1).broadcast_to((P, NCH, CH)),
                                  ALU.mult).then_inc(dve_free, 1)
                dve.wait_ge(dts_a, 1)
                dve.tensor_scalar(u[:], et[:], 1.0, None, ALU.add).then_inc(dts, 1)
                dve.wait_ge(dts, 2)
                dve.scalar_tensor_tensor(out=et[:], in0=u[:], scalar=1.0, in1=et[:], op0=ALU.subtract,
                                         op1=ALU.subtract)
                dve.reciprocal(az[:], u[:]).then_inc(dts, 1)
                dve.wait_ge(dts, 3)
                dve.tensor_tensor(et[:], et[:], az[:], ALU.mult)
                dve.wait_ge(dts_a, 2)
                dve.scalar_tensor_tensor(out=dt[:], in0=z[:], scalar=0.0, in1=lu[:], op0=ALU.max,
                                         op1=ALU.add).then_inc(dts, 1)
                dve.wait_ge(dts, 4)
                dve.tensor_tensor(dt[:], dt[:], et[:], ALU.subtract).then_inc(dts, 1)
                dve.wait_ge(dts, 5)
                dve.tensor_scalar(dt[:], dt[:], 0.0, 100.0, ALU.max, ALU.min).then_inc(dts, 1)
                dve.wait_ge(dts, 6)
                dve.tensor_tensor(ad[:], dt[:], neg_a[:].rearrange("p (o h) -> p o h", o=1).broadcast_to(
                    (P, NT, HEADS)), ALU.mult).then_inc(ad_ok, 1)
                dve.wait_ge(ad_ok, 1)
                for hh in range(2):
                    for q in range(2):
                        i = dve.tensor_copy(adl[hh * CH:(hh + 1) * CH, :, q, :],
                                            ad[q * CH:(q + 1) * CH, :, hh * HG:(hh + 1) * HG])
                i.then_inc(dts, 1)
                dve.wait_ge(dts, 7)
                flat = "p t q g -> p (t q g)"
                dve.tensor_copy(adp[:, 0, :], adl[:].rearrange(flat)).then_inc(adp_ok, 1)
                dve.wait_ge(adp_ok, 1)
                dve.tensor_tensor(adr[:].rearrange(flat), adl[:].rearrange(flat), adp[:, 0, :],
                                  ALU.subtract).then_inc(dts, 1)
                dve.wait_ge(dts, 8)
                dve.tensor_copy(adp[:, 1, :], adr[:].rearrange(flat)).then_inc(adp_ok, 1)
                dve.wait_ge(adp_ok, 2)
                dve.tensor_tensor(adp[:, 2, :], adr[:].rearrange(flat), adp[:, 1, :], ALU.subtract).then_inc(adp_ok, 1)
                dve.wait_ge(act_free, free_no("dec"))
                dve.tensor_tensor(dsuf[:], dt[:], dec[:, 1, :, :], ALU.mult).then_inc(dsuf_ok, 1)
                dve.wait_ge(dsuf_ok, 1)
                dve.wait_ge(act_free, free_no("xT", NT - 1))
                dve.tensor_tensor(xds[:].rearrange("p t (h d) -> p (t h) d", d=HD),
                                  xtok[:].rearrange("p t (h d) -> p (t h) d", d=HD),
                                  spread(dsuf[:].rearrange("p t h -> p (t h)"), HD), ALU.mult).then_inc(xds_ok, 1)
                dve.wait_ge(dve_free, free_no("g"))
                for g in range(CH // 4):
                    dve.wait_ge(act_free, free_no("seg", g))
                    out = mt[:, :, 4 * g:4 * g + 4].rearrange("p (c g) l -> p c g l", c=NCH)
                    e_ap = es[:, g % 2, :, :].rearrange("p l (c g) -> p c g l", c=NCH)
                    g_ap = gm[:, :, 4 * g:4 * g + 4].rearrange("p c (o l) -> p c o l", o=1).broadcast_to(
                        (P, NCH, HG, 4))
                    dve.tensor_tensor(out, e_ap, g_ap, ALU.mult).then_inc(mt_ok, 1)
                for c in range(NCH - 1):
                    full(dve, "st", c)
                    if c == 0:
                        dve.tensor_copy(stt[:, 1, :], where("st", 0)[:]).then_inc(state_ok, 1)
                    else:
                        dve.wait_ge(state_ok, c)
                        dve.tensor_tensor(stt[:, c + 1, :].rearrange("p (h d) -> p h d", d=HD),
                                          stt[:, c, :].rearrange("p (h d) -> p h d", d=HD),
                                          spread(dec[:, 2 + c % 2, c // 2, :], HD), ALU.mult).then_inc(carried, 1)
                        dve.wait_ge(carried, c)
                        dve.tensor_tensor(stt[:, c + 1, :], stt[:, c + 1, :], where("st", c)[:],
                                          ALU.add).then_inc(state_ok, 1)
                dve.wait_ge(xd_ok, 1)
                for t in range(NT):
                    full(dve, "off", t)
                    dve.tensor_tensor(y[:, t, :].rearrange("p (h d) -> p h d", d=HD),
                                      where("off", t)[:].rearrange("p (h d) -> p h d", d=HD),
                                      spread(dec[:, 0, t, :], HD), ALU.mult).then_inc(dve_free, 1)
                    full(dve, "diag", t)
                    dve.wait_ge(dve_free, free_no("off", t))
                    dve.tensor_tensor(y[:, t, :], y[:, t, :], where("diag", t)[:], ALU.add).then_inc(dve_free, 1)
                    dve.wait_ge(dve_free, free_no("diag", t))
                    dve.tensor_tensor(y[:, t, :], y[:, t, :], xd[:, t, :], ALU.add).then_inc(ych, 1)
                    dve.wait_ge(ych, t + 1)
                    dve.tensor_tensor(y[:, t, :], y[:, t, :], sg[:, t, :], ALU.mult).then_inc(y_ok, 1)
                dve.wait_ge(rstd_ok, 2)
                for t in range(NT):
                    full(dve, "out", t // 2)
                    dve.tensor_scalar(o_sb[:, t, :], where("out", t // 2)[:, t % 2 * HID:(t % 2 + 1) * HID],
                                      ssq[:, t:t + 1], None, ALU.mult).then_inc(out_ok, 1)
                    dve.wait_ge(out_ok, t + 1)
                    stats(t, o_sb[:, t, :], NT)
                dve.wait_ge(rstd_ok, 3)
                for t in range(NT):
                    dve.tensor_scalar(o_sb[:, t, :], o_sb[:, t, :], mv[:, t, 0:1], rstd[:, t:t + 1],
                                      ALU.subtract, ALU.mult).then_inc(och, 1)
                    dve.wait_ge(och, t + 1)
                    dve.tensor_tensor(x1[:, bass.ds(b * (NT * HID) + t * HID, HID)], o_sb[:, t, :], x_sb[:, t, :],
                                      ALU.add).then_inc(x1_ok, 1)

            @block.gpsimd
            def _(pool):
                pool.wait_ge(act_free, free_no("xT", NT - 1))
                pool.tensor_tensor(xd[:].rearrange("p t (h d) -> p t h d", d=HD),
                                   xtok[:].rearrange("p t (h d) -> p t h d", d=HD),
                                   dsk[:].rearrange("p (o h u) -> p o h u", o=1, u=1).broadcast_to((P, NT, HEADS, HD)),
                                   ALU.mult).then_inc(xd_ok, 1)
                pool.wait_ge(dts, 6)
                pool.wait_ge(xd_ok, 1)
                for q in range(2):
                    for hh in range(2):
                        src = slice(q * CH, (q + 1) * CH)
                        out = xbd[hh * CH:(hh + 1) * CH, :, :, hh * HD:(hh + 1) * HD].rearrange(
                            "p (t q) g d -> p q t g d", q=2)[:, q]
                        xin = xtok[src, :, hh * 256:(hh + 1) * 256].rearrange("p t (g d) -> p t g d", d=HD)
                        din = dt[src, :, hh * HG:(hh + 1) * HG].rearrange("p t (g o) -> p t g o", o=1).broadcast_to(
                            (CH, NT, HG, HD))
                        if q or hh:
                            pool.wait_ge(xbd_ok, 2 * q + hh)
                        pool.tensor_tensor(out, xin, din, ALU.mult).then_inc(xbd_ok, 1)


QH, KVH, D = 16, 4, 128
GRP = QH // KVH
NE, TOPK, EI = 32, 4, 128
NORM_MIN = 1e-12
NEG = -1e30
PAIRS = NT * (NT + 1) // 2


def attention_phase(nc, wq, wk, wv, wo, ln1, cos, sin, ident, x1, x2):
    with ExitStack() as ctx:
        sb, ps, sem = open_tools(nc, ctx)
        wq_sb = sb("wq_sb", [P, NK, QH * D])
        wk_sb = sb("wk_sb", [P, NK, KVH * D])
        wv_sb = sb("wv_sb", [P, NK, KVH * D])
        wo_sb = sb("wo_sb", [P, QH, HID])
        ln1_sb = sb("ln1_sb", [P, NK])
        cos_sb = sb("cos_sb", [P, SEQ])
        sin_sb = sb("sin_sb", [P, SEQ])
        eps_ln = sb("eps_ln", [P, 1])
        eps_rms = sb("eps_rms", [P, 1])
        identb = sb("identb", [P, P], BF16)
        future = sb("future", [P, P], BF16)

        st6 = sb("a_st6", [P, NT, 6])
        mv = sb("a_mv", [P, NT, 2])
        lnv = sb("a_lnv", [P, NT])
        r1 = sb("r1", [P, NT])
        m2 = sb("m2", [P, NT])
        r2 = sb("r2", [P, NT])
        h = sb("h", [P, NT, HID])
        xr = sb("xr", [P, NT, HID])
        xT = sb("xT", [P, NK, SEQ])
        v = sb("v", [P, NT, KVH * D])
        kT = sb("kT", [P, KVH, SEQ])
        rc = sb("rc", [P, 2, SEQ])
        rs = sb("rs", [P, 2, SEQ])
        qT = sb("qT", [P, 2, SEQ])
        nmax_r = sb("nmax_r", [P, 2, NT])
        nmax = sb("nmax", [P, 2, NT])
        rsum = sb("rsum", [P, 2, NT])
        rrec = sb("rrec", [P, 2, NT])
        pr = sb("pr", [P, 2, PAIRS * P])
        pt = sb("pt", [P, 2, PAIRS * P])
        oT = sb("oT", [P, QH, SEQ])
        bank = [ps(f"a_bank{i}", [P, 512]) for i in range(8)]

        su = Sems(sem)
        loaded, masks = su("a_loaded"), su("a_masks")
        with nc.Block() as block:
            @block.sync
            def _(sp):
                n = 0
                for dst, src in ((wq_sb, wq), (wk_sb, wk), (wv_sb, wv)):
                    sp.dma_start(dst[:], src.rearrange("(k p) n -> p k n", p=P)).then_inc(loaded, 16)
                    n += 16
                sp.dma_start(wo_sb[:], wo.rearrange("(h p) n -> p h n", p=P)).then_inc(loaded, 16)
                for dst, src in ((ln1_sb, ln1), (cos_sb, cos), (sin_sb, sin)):
                    sp.dma_start(dst[:], src).then_inc(loaded, 16)
                    n += 16
                sp.wait_ge(loaded, n + 16)

            @block.gpsimd
            def _(pool):
                pool.memset(eps_ln[:], LN_EPS)
                pool.memset(eps_rms[:], RMS_EPS)
                pool.memset(future[:], 0.0)
                pool.memset(identb[:], 0.0).then_inc(masks, 1)
                pool.wait_ge(masks, 1)
                pool.affine_select(out=identb[:], in_=identb[:], compare_op=ALU.not_equal, fill=1.0, base=0,
                                   pattern=[[-1, P]], channel_multiplier=1)
                pool.affine_select(out=future[:], in_=future[:], compare_op=ALU.is_ge, fill=NEG, base=0,
                                   pattern=[[-1, P]], channel_multiplier=1).then_inc(masks, 1)
                pool.wait_ge(masks, 2)
        clear(nc, su)

        s = Sems(sem)
        pe, act_free, dve_free = s("a_pe"), s("a_act_free"), s("a_dve_free")
        stat, mv_ok, lnv_ok, r_ok, m2_ok = s("a_stat"), s("a_mv_ok"), s("a_lnv_ok"), s("r_ok"), s("m2_ok")
        h_ok, xr_ok, xT_ok = s("h_ok"), s("xr_ok"), s("xT_ok")
        rot, qk_ok = s("rot"), s("qk_ok")
        mxr = s("mxr")
        mx_ok, e_ok, rec_ok, p_ok = s("mx_ok"), s("e_ok"), s("rec_ok"), s("p_ok")
        pt_a, pt_v, oT_ok = s("pt_a"), s("pt_v"), s("oT_ok")
        x2_ok = s("x2_ok")

        A, V = (act_free, 1), (dve_free, 1)
        jobs = [("xT", 0, A), ("xT", 1, A)]
        jobs += [("v", t, A) for t in range(NT)]
        jobs += [("k", g, (rot, 3)) for g in range(KVH)]
        steps = []
        for n in range(-2, QH + 1):
            if 0 <= n + 2 < QH:
                steps.append(("q", n + 2))
            if 0 <= n + 1 < QH:
                steps.append(("s", n + 1))
            if 0 <= n < QH:
                steps.append(("p", n))
            if 0 <= n - 1 < QH:
                steps.append(("o", n - 1))
        for what, n in steps:
            if what == "q":
                jobs += [("q", n, (rot, 3))]
            elif what == "s":
                jobs += [("s", (n, g), (e_ok, m)) for g, m in ((3, 1), (2, 2), (1, 1))]
            elif what == "p":
                jobs += [("p", (n, 0), (pt_a, 1)), ("p", (n, 1), (pt_v, 1)), ("p", (n, 2), (pt_a, 1))]
            else:
                jobs += [("o", n, (oT_ok, 1))]
        jobs += [("wo", i, (x2_ok, 2)) for i in range(NT // 2)]
        at = {(n, i): k for k, (n, i, _) in enumerate(jobs)}

        def read_by(k):
            return sum(j[2][1] for j in jobs[:k + 1] if j[2][0] is jobs[k][2][0])

        def where(name, i=0):
            return bank[at[name, i] % 8]

        def fill(eng, name, i=0):
            k = at[name, i] - 8
            if k >= 0:
                eng.wait_ge(jobs[k][2][0], read_by(k))

        def full(eng, name, i=0):
            eng.wait_ge(pe, at[name, i] + 1)

        TILES = (3, 2, 0, 1)

        def score_place(n, i):
            b_ = where("s", (n, i if i else 2))
            c0 = 3 * P if i == 0 else 0
            return b_[:, c0:c0 + (i + 1) * P]

        P_AT = {3: 0, 2: 4 * P, 0: 7 * P, 1: 8 * P}
        T_JOB = {0: (0, 0), 1: (1, 0), 3: (1, 3 * P), 2: (2, 0)}
        T_AT = {0: 0, 1: 4 * P, 3: 7 * P, 2: 8 * P}

        with nc.Fori(0, BATCH) as b, turn(nc, s) as block:
            @block.tensor
            def _(te):
                for k in range(NK):
                    for t in range(NT):
                        te.wait_ge(xr_ok, t + 1)
                        i = te.transpose(where("xT", k)[:, t * P:(t + 1) * P], xr[:, t, k * P:(k + 1) * P], ident[:])
                    i.then_inc(pe, 1)
                te.wait_ge(act_free, 2)
                for t in range(NT):
                    for k in range(NK):
                        i = te.matmul(where("v", t)[:], xT[:, k, t * P:(t + 1) * P], wv_sb[:, k, :],
                                      start=k == 0, stop=k == NK - 1)
                    i.then_inc(pe, 1)

                def project(name, n, w):
                    fill(te, name, n)
                    for k in range(NK):
                        i = te.matmul(where(name, n)[:], w[:, k, n * D:(n + 1) * D], xT[:, k, :],
                                      start=k == 0, stop=k == NK - 1)
                    i.then_inc(pe, 1)

                for g in range(KVH):
                    project("k", g, wk_sb)
                for what, n in steps:
                    if what == "q":
                        project("q", n, wq_sb)
                    elif what == "s":
                        te.wait_ge(qk_ok, KVH + n + 1)
                        for i in TILES:
                            if i:
                                fill(te, "s", (n, i))
                            out = score_place(n, i)
                            te.matmul(out, qT[:, n % 2, i * P:(i + 1) * P], kT[:, n // GRP, 0:(i + 1) * P],
                                      start=True, stop=False)
                            m = te.matmul(out[:, i * P:(i + 1) * P], identb[:], future[:], start=False, stop=True)
                            if i != 2:
                                m.then_inc(pe, 1)
                    elif what == "p":
                        te.wait_ge(p_ok, NT * (n + 1))
                        for job, js in ((0, (0,)), (1, (1, 3)), (2, (2,))):
                            fill(te, "p", (n, job))
                            for j in js:
                                for i in range(j, NT):
                                    c = T_JOB[j][1] + (i - j) * P
                                    m = te.transpose(where("p", (n, job))[:, c:c + P],
                                                     pr[:, n % 2, P_AT[i] + j * P:P_AT[i] + (j + 1) * P], ident[:])
                            m.then_inc(pe, 1)
                    else:
                        fill(te, "o", n)
                        te.wait_ge(pt_a, 2 * (n + 1))
                        te.wait_ge(pt_v, n + 1)
                        for j in range(NT):
                            m = te.matmul(where("o", n)[:, j * P:SEQ], v[:, j, n // GRP * D:(n // GRP + 1) * D],
                                          pt[:, n % 2, T_AT[j]:T_AT[j] + (NT - j) * P],
                                          start=j == 0, stop=j == NT - 1)
                        m.then_inc(pe, 1)
                te.wait_ge(oT_ok, QH)
                for q in range(NT // 2):
                    fill(te, "wo", q)
                    for t in (2 * q, 2 * q + 1):
                        for n in range(QH):
                            m = te.matmul(where("wo", q)[:, t % 2 * HID:(t % 2 + 1) * HID],
                                          oT[:, n, t * P:(t + 1) * P], wo_sb[:, n, :],
                                          start=n == 0, stop=n == QH - 1)
                    m.then_inc(pe, 1)

            @block.scalar
            def _(act):
                logs = [0]

                def rsqrt(out, val, eps):
                    logs[0] += 1
                    act.activation(lnv[:], val, ACT.Ln, bias=eps[:, 0:1]).then_inc(lnv_ok, 1)
                    act.wait_ge(lnv_ok, logs[0])
                    act.activation(out, lnv[:], ACT.Exp, scale=-0.5).then_inc(r_ok, 1)

                act.wait_ge(mv_ok, NT)
                rsqrt(r1[:], mv[:, :, 1], eps_ln)
                act.wait_ge(m2_ok, 2)
                rsqrt(r2[:], m2[:], eps_rms)
                for k in range(NK):
                    full(act, "xT", k)
                    act.activation(xT[:, k, :], where("xT", k)[:], ACT.Copy, scale=ln1_sb[:, k:k + 1]).then_inc(act_free, 1)
                for t in range(NT):
                    full(act, "v", t)
                    act.activation(v[:, t, :], where("v", t)[:], ACT.Copy).then_inc(act_free, 1)

                for what, n in steps:
                    if what == "s":
                        for m, i in enumerate(TILES):
                            act.wait_ge(mx_ok, NT * n + (3 if m == 1 else m + 1))
                            if n >= 2 and m == 0:
                                full(act, "p", (n - 2, 2))
                            act.activation(pr[:, n % 2, P_AT[i]:P_AT[i] + (i + 1) * P], score_place(n, i), ACT.Exp,
                                           bias=nmax[:, n % 2, i:i + 1], scale=D ** -0.5,
                                           accum_out=rsum[:, n % 2, i:i + 1]).then_inc(e_ok, 1)
                    elif what == "p":
                        for job, c in ((0, 4 * P), (2, 2 * P)):
                            full(act, "p", (n, job))
                            if n >= 2 and job == 0:
                                full(act, "o", n - 2)
                            c0 = T_AT[job]
                            act.activation(pt[:, n % 2, c0:c0 + c], where("p", (n, job))[:, 0:c],
                                           ACT.Copy).then_inc(pt_a, 1)
                    elif what == "o":
                        full(act, "o", n)
                        act.activation(oT[:, n, :], where("o", n)[:], ACT.Copy).then_inc(oT_ok, 1)

            @block.vector
            def _(dve):
                for t in range(NT):
                    src = x1[:, bass.ds(b * (NT * HID) + t * HID, HID)]
                    dve.bn_stats(st6[:, t, :], src).then_inc(stat, 1)
                    dve.wait_ge(stat, t + 1)
                    dve.bn_aggr(mv[:, t, :], st6[:, t, :]).then_inc(mv_ok, 1)
                dve.wait_ge(r_ok, 1)
                dve.tensor_tensor(m2[:], mv[:, :, 1], r1[:], ALU.mult).then_inc(m2_ok, 1)
                dve.wait_ge(m2_ok, 1)
                dve.tensor_tensor(m2[:], m2[:], r1[:], ALU.mult).then_inc(m2_ok, 1)
                for t in range(NT):
                    src = x1[:, bass.ds(b * (NT * HID) + t * HID, HID)]
                    dve.tensor_scalar(h[:, t, :], src, mv[:, t, 0:1], r1[:, t:t + 1],
                                      ALU.subtract, ALU.mult).then_inc(h_ok, 1)
                dve.wait_ge(r_ok, 2)
                for t in range(NT):
                    dve.wait_ge(h_ok, t + 1)
                    dve.tensor_scalar(xr[:, t, :], h[:, t, :], r2[:, t:t + 1], None, ALU.mult).then_inc(xr_ok, 1)

                def rotate(name, n, m):
                    full(dve, name, n)
                    if m >= 2:
                        dve.wait_ge(qk_ok, m - 1)
                    src = where(name, n)
                    half = P // 2
                    dve.tensor_tensor(rc[:, m % 2, :], src[:], cos_sb[:], ALU.mult).then_inc(rot, 1)
                    dve.tensor_tensor(rs[0:half, m % 2, :], src[half:P, :], sin_sb[0:half, :], ALU.mult).then_inc(rot, 1)
                    dve.tensor_tensor(rs[half:P, m % 2, :], src[0:half, :], sin_sb[half:P, :], ALU.mult).then_inc(rot, 1)

                for g in range(KVH):
                    rotate("k", g, g)
                for what, n in steps:
                    if what == "q":
                        rotate("q", n, KVH + n)
                    elif what == "s":
                        for m, i in enumerate(TILES):
                            full(dve, "s", (n, i if i else 2))
                            if n >= 2 and m == 0:
                                dve.wait_ge(e_ok, NT * (n - 1))
                            dve.tensor_reduce(nmax_r[:, n % 2, i:i + 1], score_place(n, i), AX_X, ALU.max,
                                              negate=True).then_inc(mxr, 1)
                            dve.wait_ge(mxr, NT * n + m + 1)
                            dve.tensor_scalar(nmax[:, n % 2, i:i + 1], nmax_r[:, n % 2, i:i + 1], D ** -0.5, None,
                                              ALU.mult).then_inc(mx_ok, 1)
                        for m, i in enumerate(TILES):
                            dve.wait_ge(e_ok, NT * n + m + 1)
                            dve.reciprocal(rrec[:, n % 2, i:i + 1], rsum[:, n % 2, i:i + 1]).then_inc(rec_ok, 1)
                            dve.wait_ge(rec_ok, NT * n + m + 1)
                            a = pr[:, n % 2, P_AT[i]:P_AT[i] + (i + 1) * P]
                            dve.tensor_scalar(a, a, rrec[:, n % 2, i:i + 1], None, ALU.mult).then_inc(p_ok, 1)
                    elif what == "p":
                        full(dve, "p", (n, 1))
                        if n >= 2:
                            full(dve, "o", n - 2)
                        dve.tensor_copy(pt[:, n % 2, T_AT[1]:T_AT[1] + 4 * P], where("p", (n, 1))[:]).then_inc(pt_v, 1)
                for t in range(NT):
                    full(dve, "wo", t // 2)
                    dve.tensor_tensor(x2[:, bass.ds(b * (NT * HID) + t * HID, HID)], where("wo", t // 2)[:, t % 2 * HID:(t % 2 + 1) * HID], h[:, t, :],
                                      ALU.add).then_inc(x2_ok, 1)

            @block.gpsimd
            def _(pool):
                for m in range(KVH + QH):
                    pool.wait_ge(rot, 3 * (m + 1))
                    n = m - KVH
                    if n >= 2:
                        full(pool, "s", (n - 2, 1))
                    dst = kT[:, m, :] if n < 0 else qT[:, n % 2, :]
                    pool.tensor_tensor(dst, rc[:, m % 2, :], rs[:, m % 2, :], ALU.add).then_inc(qk_ok, 1)


N16 = BATCH * NT
TILES_MAX = (BATCH * SEQ * TOPK + NE * (P - 1)) // P
TURN = 32
TILES_ALL = -(-TILES_MAX // TURN) * TURN
LOADS = 4


def moe_phase(nc, ln2, gateT, bias_e, weg, weu, wed, wsg, wsu, wsd, ident, x1, x2, xs, ys, filled, n_filled, out):
    with ExitStack() as ctx:
        sb, ps, sem = open_tools(nc, ctx)
        U32, I32 = mybir.dt.uint32, mybir.dt.int32
        wgu = sb("wgu", [P, NK, NE, 2 * EI])
        wd = sb("wd", [P, NE, HID])
        ln2_sb = sb("ln2_sb", [P, NK])
        slot_u = sb("slot_u", [P, N16, TOPK], U32)
        rw = sb("rw", [P, N16, TOPK])
        e_off = sb("e_off", [1, P], I32)
        eps_ln = sb("f_eps_ln", [P, 1])
        bank = [ps(f"f_bank{i}", [P, 512]) for i in range(8)]
        w_s = Sems(sem)
        w_ok = w_s("w_ok")

        route(nc, ctx, sb, sem, bank, ln2_sb, ln2, gateT, bias_e, weg, weu, wed, wsg, wsu, wsd, wgu, wd, w_ok,
              slot_u, rw, e_off, eps_ln, ident, x2, xs, filled, n_filled)
        expert_tiles(nc, sem, bank, wgu, wd, w_ok, ln2_sb, e_off, ident, xs, ys)
        combine(nc, sem, slot_u, rw, eps_ln, x1, x2, ys, out)


def route(nc, ctx, sb, sem, bank, ln2_sb, ln2, gateT, bias_e, weg, weu, wed, wsg, wsu, wsd, wgu, wd, w_ok,
          slot_u, rw, e_off, eps_ln, ident, x2, xs, filled, n_filled):
    I32, U32 = mybir.dt.int32, mybir.dt.uint32
    with ExitStack() as ctx:
        sb, ps, _ = open_tools(nc, ctx)
        xr = sb("r_xr", [P, N16, HID])
        xfT = sb("xfT", [P, NK, BATCH * SEQ])
        gate_sb = sb("gate_sb", [P, NK, NE])
        be_sb = sb("be_sb", [P, NE])
        sg_w = sb("sg_w", [P, NK, EI])
        su_w = sb("su_w", [P, NK, EI])
        sd_w = sb("sd_w", [P, HID])
        eps_rms = sb("f_eps_rms", [P, 1])
        col_i = sb("col_i", [P, NE], I32)
        col_no = sb("col_no", [P, NE])
        row_i = sb("row_i", [P, 1], I32)
        row_no = sb("row_no", [P, 1])
        before = sb("before", [P, P], BF16)
        ones_b = sb("ones_b", [P, P], BF16)
        ones_e = sb("ones_e", [P, NE])
        sq = sb("r_sq", [P, 2, HID])
        ssq = sb("r_ssq", [P, N16])
        lnv = sb("r_lnv", [P, N16])
        rr = sb("r_rr", [P, N16])
        lmax = sb("lmax", [P, N16])
        lsum = sb("lsum", [P, N16])
        lrec = sb("lrec", [P, N16])
        pb = sb("pb", [P, N16, NE])
        pbb = sb("pbb", [P, N16, NE])
        top = sb("top", [P, N16, 8])
        topi = sb("topi", [P, N16, 8], U32)
        topf = sb("topf", [P, N16, TOPK])
        oh = sb("oh", [P, TOPK, N16, NE])
        sel = sb("sel", [P, N16, NE])
        sel_b = sb("sel_b", [P, N16 * NE], BF16)
        tiles = sb("tiles", [P, NE])
        tiles_i = sb("tiles_i", [P, NE], I32)
        upto = sb("upto", [P, NE])
        base = sb("base", [P, NE])
        pos = sb("pos", [P, N16, NE])
        prod = sb("prod", [P, N16, NE])
        slot_f = sb("slot_f", [P, N16, TOPK])
        cmp = sb("cmp", [P, NE])
        e_no = sb("e_no", [P, 1])
        sgl = sb("sgl", [P, 2, SEQ])
        hT = sb("hT", [P, 2, SEQ])

        s = Sems(sem)
        loaded, sh_in, made = s("r_loaded"), s("r_sh_in"), s("r_made")
        pe, sq_ok, lnv_ok, rr_ok, xr_ok, xf_ok = (
            s("r_pe"), s("r_sq_ok"), s("r_lnv_ok"), s("r_rr_ok"), s("r_xr_ok"), s("r_xf_ok"))
        ch, ch_a, sel_ok, slots_ok = s("r_chain"), s("r_chain_a"), s("r_sel_ok"), s("r_slots_ok")
        silu_ok, h_ok, added, scattered, e_col, e_row = (
            s("r_silu"), s("r_h_ok"), s("r_added"), sem("scattered"), s("r_e_col"), s("r_e_row"))
        F = BATCH
        jobs = [("xf", (n, k), (xf_ok, 1)) for n in range(F) for k in range(NK)]
        jobs += [("rt", 0, (ch, 0))]
        jobs += [("pos", 0, (ch, 0)), ("cnt", 0, (ch, 0))]
        at = {(n, i): k for k, (n, i, _) in enumerate(jobs)}

        with nc.Block() as block:
            @block.sync
            def _(sp):
                sp.dma_start(gate_sb[:], gateT.rearrange("(k p) n -> p k n", p=P)).then_inc(loaded, 16)
                sp.dma_start(ln2_sb[:], ln2).then_inc(loaded, 16)
                sp.dma_start(be_sb[:], bias_e.rearrange("(o h) -> o h", o=1).broadcast_to((P, NE))).then_inc(loaded, 16)
                sp.dma_start(sg_w[:], wsg.rearrange("(k p) i -> p k i", p=P)).then_inc(sh_in, 16)
                sp.dma_start(su_w[:], wsu.rearrange("(k p) i -> p k i", p=P)).then_inc(sh_in, 16)
                sp.dma_start(sd_w[:], wsd).then_inc(sh_in, 16)
                for e0 in range(0, NE, 8):
                    for k in range(NK):
                        for j, w in enumerate((weg, weu)):
                            sp.dma_start(wgu[:, k, e0:e0 + 8, j * EI:(j + 1) * EI],
                                         w.rearrange("(e k p) i -> k p e i", k=NK, p=P)[k, :, e0:e0 + 8, :]
                                         ).then_inc(w_ok, 16)
                    sp.dma_start(wd[:, e0:e0 + 8, :],
                                 wed.rearrange("(e p) h -> p e h", p=P)[:, e0:e0 + 8, :]).then_inc(w_ok, 16)
                sp.wait_ge(loaded, 48)
                sp.wait_ge(sh_in, 48)

            @block.gpsimd
            def _(pool):
                pool.memset(eps_ln[:], LN_EPS)
                pool.memset(eps_rms[:], RMS_EPS)
                pool.memset(ones_b[:], 1.0)
                pool.memset(ones_e[:], 1.0)
                pool.memset(before[:], 1.0)
                pool.iota(row_i[:], pattern=[[0, 1]], base=0, channel_multiplier=1)
                pool.iota(col_i[:], pattern=[[1, NE]], base=0, channel_multiplier=0).then_inc(made, 1)
                pool.wait_ge(made, 1)
                pool.tensor_copy(row_no[:], row_i[:])
                pool.tensor_copy(col_no[:], col_i[:])
                pool.affine_select(out=before[:], in_=before[:], compare_op=ALU.is_ge, fill=0.0, base=-1,
                                   pattern=[[1, P]], channel_multiplier=-1).then_inc(made, 1)
                pool.wait_ge(filled, n_filled)
                for k in range(TOPK):
                    pool.wait_ge(slots_ok, k + 1)
                    for t in range(N16):
                        pool.indirect_dma_start(
                            out=xs[:, :], out_offset=bass.IndirectOffsetOnAxis(ap=slot_u[:, t, k:k + 1], axis=0),
                            in_=xr[:, t, :], in_offset=None, bounds_check=None).then_inc(scattered, 16)
                pool.wait_ge(scattered, 16 * TOPK * N16)

            @block.tensor
            def _(te):
                for n in range(F):
                    for k in range(NK):
                        for j in range(NT):
                            t = n * NT + j
                            te.wait_ge(xr_ok, t + 1)
                            m = te.transpose(bank[2 * n + k][:, j * P:(j + 1) * P], xr[:, t, k * P:(k + 1) * P], ident[:])
                        m.then_inc(pe, 1)
                te.wait_ge(loaded, 48)
                for t in range(N16):
                    te.wait_ge(xf_ok, NK * (t // NT + 1))
                    for k in range(NK):
                        m = te.matmul(bank[0][:, t * NE:(t + 1) * NE], xfT[:, k, t * P:(t + 1) * P], gate_sb[:, k, :],
                                      start=k == 0, stop=k == NK - 1)
                m.then_inc(pe, 1)

                def shared(i, gu):
                    if gu:
                        if i >= 2:
                            te.wait_ge(h_ok, i - 1)
                        for bk, w in ((1 + i % 2, sg_w), (3 + i % 2, su_w)):
                            for k in range(NK):
                                m = te.matmul(bank[bk][:], w[:, k, :], xfT[:, k, i * SEQ:(i + 1) * SEQ],
                                              start=k == 0, stop=k == NK - 1)
                            m.then_inc(pe, 1)
                    else:
                        te.wait_ge(h_ok, i + 1)
                        for q in range(NT // 2):
                            if i:
                                te.wait_ge(added, NT * (i - 1) + 2 * q + 2)
                            for t in range(2):
                                c = (2 * q + t) * P
                                m = te.matmul(bank[5 + q][:, t * HID:(t + 1) * HID], hT[:, i % 2, c:c + P], sd_w[:],
                                              start=True, stop=True)
                            m.then_inc(pe, 1)

                te.wait_ge(sh_in, 48)
                shared(0, True)
                shared(1, True)
                te.wait_ge(sel_ok, 1)
                te.matmul(bank[0][:], before[:], sel_b[:], start=True, stop=False)
                for d in range(1, N16):
                    te.matmul(bank[0][:, d * NE:], ones_b[:], sel_b[:, 0:(N16 - d) * NE], start=False,
                              stop=d == N16 - 1)
                for t in range(N16):
                    m = te.matmul(bank[7][:, 0:NE], ones_b[:], sel_b[:, t * NE:(t + 1) * NE], start=t == 0,
                                  stop=t == N16 - 1)
                m.then_inc(pe, 1)
                te.wait_ge(e_col, 1)
                te.transpose(bank[7][0:1, 0:P], e_no[:], ident[:]).then_inc(e_row, 1)
                for i in range(F):
                    if i >= 2:
                        shared(i, True)
                    shared(i, False)



            def gu_at(i):
                return {0: (10, 11), 1: (12, 13), 2: (19, 20), 3: (23, 24)}[i]

            def y_at(i, q):
                return {0: 15, 1: 17, 2: 21, 3: 25}[i] + q

            @block.scalar
            def _(act):
                act.wait_ge(made, 1)
                for t in range(N16):
                    if t >= 2:
                        act.wait_ge(sq_ok, t - 1)
                    act.activation(sq[:, t % 2, :], x2[:, t * HID:(t + 1) * HID], ACT.Square, scale=HID ** -0.5,
                                   accum_out=ssq[:, t:t + 1]).then_inc(sq_ok, 1)
                act.wait_ge(sq_ok, N16)
                act.activation(lnv[:], ssq[:], ACT.Ln, bias=eps_rms[:, 0:1]).then_inc(lnv_ok, 1)
                act.wait_ge(lnv_ok, 1)
                act.activation(rr[:], lnv[:], ACT.Exp, scale=-0.5).then_inc(rr_ok, 1)
                act.wait_ge(loaded, 48)
                for n in range(F):
                    for k in range(NK):
                        act.wait_ge(pe, 2 * n + k + 1)
                        act.activation(xfT[:, k, n * SEQ:(n + 1) * SEQ], bank[2 * n + k][:], ACT.Copy,
                                       scale=ln2_sb[:, k:k + 1]).then_inc(xf_ok, 1)
                act.wait_ge(ch, 2)
                act.activation(pb[:].rearrange("p t e -> p (t e)"), pbb[:].rearrange("p t e -> p (t e)"),
                               ACT.Exp).then_inc(ch_a, 1)
                for i in range(F):
                    act.wait_ge(pe, gu_at(i)[0])
                    if i >= 2:
                        act.wait_ge(h_ok, i - 1)
                    act.activation(sgl[:, i % 2, :], bank[1 + i % 2][:], ACT.Silu).then_inc(silu_ok, 1)

            @block.vector
            def _(dve):
                n_ch = [0]

                def step(i):
                    n_ch[0] += 1
                    i.then_inc(ch, 1)
                    dve.wait_ge(ch, n_ch[0])

                def per_e(ap):
                    return ap.rearrange("p (o e) -> p o e", o=1).broadcast_to((P, N16, NE))

                dve.wait_ge(rr_ok, 1)
                for t in range(N16):
                    dve.tensor_scalar(xr[:, t, :], x2[:, t * HID:(t + 1) * HID], rr[:, t:t + 1], None,
                                      ALU.mult).then_inc(xr_ok, 1)
                dve.wait_ge(pe, 9)
                logits = bank[0][:].rearrange("p (t e) -> p t e", e=NE)
                step(dve.tensor_reduce(lmax[:], logits, AX_X, ALU.max))
                step(dve.tensor_tensor(pbb[:], logits, spread(lmax[:], NE), ALU.subtract))
                dve.wait_ge(ch_a, 1)
                step(dve.tensor_reduce(lsum[:], pb[:], AX_X, ALU.add))
                step(dve.reciprocal(lrec[:], lsum[:]))
                step(dve.tensor_tensor(pb[:], pb[:], spread(lrec[:], NE), ALU.mult))
                dve.wait_ge(made, 2)
                step(dve.tensor_tensor(pbb[:], pb[:], per_e(be_sb[:]), ALU.add))
                for t in range(N16):
                    i = dve.max(top[:, t, :], pbb[:, t, :])
                step(i)
                for t in range(N16):
                    i = dve.max_index(topi[:, t, :], top[:, t, :], pbb[:, t, :])
                step(i)
                step(dve.tensor_copy(topf[:], topi[:, :, 0:TOPK]))
                for k in range(TOPK):
                    i = dve.tensor_tensor(oh[:, k, :, :], per_e(col_no[:]),
                                          topf[:, :, k:k + 1].broadcast_to((P, N16, NE)), ALU.is_equal)
                step(i)
                step(dve.tensor_tensor(sel[:], oh[:, 0, :, :], oh[:, 1, :, :], ALU.add))
                step(dve.tensor_tensor(sel[:], sel[:], oh[:, 2, :, :], ALU.add))
                dve.tensor_tensor(sel_b[:].rearrange("p (t e) -> p t e", e=NE), sel[:], oh[:, 3, :, :],
                                  ALU.add).then_inc(sel_ok, 1)
                dve.wait_ge(pe, 14)
                step(dve.tensor_scalar(tiles[:], bank[7][:, 0:NE], 1.0 / P, (P - 1.0) / P - 0.5 + 1.0 / 512,
                                       ALU.mult, ALU.add))
                step(dve.tensor_copy(tiles_i[:], tiles[:]))
                step(dve.tensor_copy(tiles[:], tiles_i[:]))
                step(dve.tensor_tensor_scan(upto[:], ones_e[:], tiles[:], 0.0, ALU.mult, ALU.add))
                step(dve.tensor_tensor(base[:], upto[:], tiles[:], ALU.subtract))
                step(dve.tensor_scalar(base[:], base[:], float(P), None, ALU.mult))
                step(dve.tensor_tensor(pos[:], bank[0][:].rearrange("p (t e) -> p t e", e=NE), per_e(base[:]), ALU.add))
                for k in range(TOPK):
                    step(dve.tensor_tensor(prod[:], oh[:, k, :, :], pos[:], ALU.mult))
                    step(dve.tensor_reduce(slot_f[:, :, k], prod[:], AX_X, ALU.add))
                    dve.tensor_copy(slot_u[:, :, k], slot_f[:, :, k]).then_inc(slots_ok, 1)
                step(dve.tensor_scalar(cmp[:], upto[:], row_no[:, 0:1], None, ALU.is_le))
                step(dve.tensor_reduce(e_no[:], cmp[:], AX_X, ALU.add))
                dve.tensor_scalar(e_no[:], e_no[:], NE - 1.0, 2.0 * EI, ALU.min, ALU.mult).then_inc(e_col, 1)
                dve.wait_ge(e_row, 1)
                step(dve.tensor_copy(e_off[:], bank[7][0:1, 0:P]))
                for k in range(TOPK):
                    step(dve.tensor_tensor(prod[:], oh[:, k, :, :], pb[:], ALU.mult))
                    step(dve.tensor_reduce(rw[:, :, k], prod[:], AX_X, ALU.add))
                step(dve.tensor_reduce(lsum[:], rw[:], AX_X, ALU.add))
                step(dve.tensor_scalar(lsum[:], lsum[:], NORM_MIN, None, ALU.max))
                step(dve.reciprocal(lrec[:], lsum[:]))
                step(dve.tensor_tensor(rw[:], rw[:], spread(lrec[:], TOPK), ALU.mult))
                for i in range(F):
                    dve.wait_ge(pe, gu_at(i)[1])
                    dve.wait_ge(silu_ok, i + 1)
                    if i >= 2:
                        dve.wait_ge(pe, y_at(i - 2, 1))
                    dve.tensor_tensor(hT[:, i % 2, :], sgl[:, i % 2, :], bank[3 + i % 2][:], ALU.mult).then_inc(h_ok, 1)
                    for t in range(NT):
                        dve.wait_ge(pe, y_at(i, t // 2))
                        acc = x2[:, (i * NT + t) * HID:(i * NT + t + 1) * HID]
                        dve.tensor_tensor(acc, acc, bank[5 + t // 2][:, t % 2 * HID:(t % 2 + 1) * HID],
                                          ALU.add).then_inc(added, 1)
        clear(nc, s)


def expert_tiles(nc, sem, bank, wgu, wd, w_ok, ln2_sb, e_off, ident, xs, ys):
    with ExitStack() as ctx:
        sb, _, _ = open_tools(nc, ctx)
        xin = sb("xin", [P, 2, LOADS, HID])
        xT = sb("e_xT", [P, 2, NK, P])
        sg = sb("e_sg", [P, 2, EI])
        hh = sb("e_h", [P, 2, EI])
        hT = sb("e_hT", [P, 2, P])
        yo = sb("yo", [P, 4, HID])
        s = Sems(sem)
        x_in = [s(f"e_x_in{i}") for i in range(2)]
        xT_pe, xT_a, xT_v, gu_pe, silu_ok, h_ok, hT_pe, hT_ok, y_pe, y_ok = (
            s("e_xT_pe"), s("e_xT_a"), s("e_xT_v"), s("e_gu_pe"), s("e_silu"), s("e_h_ok"), s("e_hT_pe"),
            s("e_hT_ok"), s("e_y_pe"), s("e_y_ok"))
        stored = [s(f"e_stored{i}") for i in range(2)]
        b_x, b_gu, b_h, b_y = bank[0:2], bank[2:4], bank[4:6], bank[6:8]

        with nc.Fori(0, TILES_ALL // TURN) as r, turn(nc, s) as block:
            @block.sync
            def _(sp):
                def store(q):
                    sp.wait_ge(y_ok, 2 * q + 2)
                    sp.dma_start(ys[bass.ds(r * (TURN * P) + q * 2 * P, 2 * P), :].rearrange("(t p) h -> p t h", p=P),
                                 yo[:, q % 2 * 2:q % 2 * 2 + 2, :]).then_inc(stored[q % 2], 16)

                done = 0
                for g in range(TURN // LOADS):
                    if g >= 2:
                        while 2 * done + 5 < LOADS * (g - 1):
                            store(done)
                            done += 1
                        sp.wait_ge(xT_pe, LOADS * (g - 1))
                    sp.dma_start(xin[:, g % 2, :, :], xs[bass.ds(r * (TURN * P) + g * LOADS * P, LOADS * P), :]
                                 .rearrange("(t p) h -> p t h", p=P)).then_inc(x_in[g % 2], 16)
                for q in range(done, TURN // 2):
                    store(q)
                for i in range(2):
                    sp.wait_ge(stored[i], 16 * (TURN // 4))

            @block.tensor
            def _(te):
                te.wait_ge(w_ok, 16 * 5 * (NE // 8))
                off = {}
                for i in range(TURN + 3):
                    if i < TURN:
                        te.wait_ge(x_in[i // LOADS % 2], 16 * (i // LOADS // 2 + 1))
                        if i >= 2:
                            te.wait_ge(xT_a, i - 1)
                            te.wait_ge(xT_v, i - 1)
                        for k in range(NK):
                            m = te.transpose(b_x[i % 2][:, k * P:(k + 1) * P],
                                             xin[:, i // LOADS % 2, i % LOADS, k * P:(k + 1) * P], ident[:])
                        m.then_inc(xT_pe, 1)
                        off[i] = te.value_load(e_off[0:1, bass.ds(r * TURN + i, 1)], min_val=0, max_val=(NE - 1) * 2 * EI)
                    j = i - 1
                    if 0 <= j < TURN:
                        te.wait_ge(xT_a, j + 1)
                        te.wait_ge(xT_v, j + 1)
                        if j >= 2:
                            te.wait_ge(h_ok, j - 1)
                        for k in range(NK):
                            m = te.matmul(b_gu[j % 2][:, 0:2 * EI], xT[:, j % 2, k, :],
                                          wgu[:, k, :, :].rearrange("p e i -> p (e i)")[:, bass.ds(off[j], 2 * EI)],
                                          start=k == 0, stop=k == NK - 1)
                        m.then_inc(gu_pe, 1)
                    j = i - 2
                    if 0 <= j < TURN:
                        te.wait_ge(h_ok, j + 1)
                        if j >= 2:
                            te.wait_ge(hT_ok, j - 1)
                        te.transpose(b_h[j % 2][:, 0:P], hh[:, j % 2, :], ident[:]).then_inc(hT_pe, 1)
                    j = i - 3
                    if 0 <= j < TURN:
                        te.wait_ge(hT_ok, j + 1)
                        if j >= 2:
                            te.wait_ge(y_ok, j - 1)
                        te.matmul(b_y[j % 2][:, 0:HID], hT[:, j % 2, :],
                                  wd[:].rearrange("p e h -> p (e h)")[:, bass.ds(off[j], HID)],
                                  start=True, stop=True).then_inc(y_pe, 1)

            @block.scalar
            def _(act):
                for i in range(TURN + 1):
                    if i < TURN:
                        act.wait_ge(xT_pe, i + 1)
                        if i >= 2:
                            act.wait_ge(gu_pe, i - 1)
                        act.activation(xT[:, i % 2, 0, :], b_x[i % 2][:, 0:P], ACT.Copy,
                                       scale=ln2_sb[:, 0:1]).then_inc(xT_a, 1)
                    j = i - 1
                    if j >= 0:
                        act.wait_ge(gu_pe, j + 1)
                        if j >= 2:
                            act.wait_ge(h_ok, j - 1)
                        act.activation(sg[:, j % 2, :], b_gu[j % 2][:, 0:EI], ACT.Silu).then_inc(silu_ok, 1)

            @block.vector
            def _(dve):
                for i in range(TURN + 3):
                    if i < TURN:
                        dve.wait_ge(xT_a, i + 1)
                        if i >= 2:
                            dve.wait_ge(gu_pe, i - 1)
                        dve.tensor_scalar(xT[:, i % 2, 1, :], b_x[i % 2][:, P:2 * P], ln2_sb[:, 1:2], None,
                                          ALU.mult).then_inc(xT_v, 1)
                    j = i - 1
                    if 0 <= j < TURN:
                        dve.wait_ge(silu_ok, j + 1)
                        if j >= 2:
                            dve.wait_ge(hT_pe, j - 1)
                        dve.tensor_tensor(hh[:, j % 2, :], sg[:, j % 2, :], b_gu[j % 2][:, EI:2 * EI],
                                          ALU.mult).then_inc(h_ok, 1)
                    j = i - 2
                    if 0 <= j < TURN:
                        dve.wait_ge(hT_pe, j + 1)
                        if j >= 2:
                            dve.wait_ge(y_pe, j - 1)
                        dve.tensor_copy(hT[:, j % 2, :], b_h[j % 2][:, 0:P]).then_inc(hT_ok, 1)
                    j = i - 3
                    if 0 <= j < TURN:
                        dve.wait_ge(y_pe, j + 1)
                        if j >= 4:
                            dve.wait_ge(stored[j // 2 % 2], 16 * (j // 4))
                        dve.tensor_copy(yo[:, j % 4, :], b_y[j % 2][:, 0:HID]).then_inc(y_ok, 1)


def combine(nc, sem, slot_u, rw, eps_ln, x1, x2, ys, out):
    with ExitStack() as ctx:
        sb, _, _ = open_tools(nc, ctx)
        RING = 8
        yg = sb("yg", [P, RING, HID])
        st6 = sb("f_st6", [P, N16, 6])
        mv = sb("f_mv", [P, N16, 2])
        lnv = sb("f_lnv", [P, N16])
        r1 = sb("f_r1", [P, N16])
        s = Sems(sem)
        got = [s(f"got{i}") for i in range(RING)]
        used, stat, mv_ok, lnv_ok, r_ok, n_ok, fin_ok, stored = (
            s("used"), s("f_stat"), s("f_mv_ok"), s("f_lnv_ok"), s("f_r_ok"), s("f_n_ok"), s("f_fin"), s("f_stored"))
        with nc.Block() as block:
            @block.gpsimd
            def _(pool):
                for i in range(N16 * TOPK):
                    if i >= RING:
                        pool.wait_ge(used, i - RING + 1)
                    pool.indirect_dma_start(
                        out=yg[:, i % RING, :], out_offset=None, in_=ys[:, :],
                        in_offset=bass.IndirectOffsetOnAxis(ap=slot_u[:, i // TOPK, i % TOPK:i % TOPK + 1], axis=0),
                        bounds_check=None).then_inc(got[i % RING], 16)

            @block.vector
            def _(dve):
                def finish(n):
                    dve.wait_ge(r_ok, n + 1)
                    for t in range(n * NT, (n + 1) * NT):
                        a = x2[:, t * HID:(t + 1) * HID]
                        dve.tensor_scalar(a, a, mv[:, t, 0:1], r1[:, t:t + 1], ALU.subtract, ALU.mult).then_inc(n_ok, 1)
                        dve.wait_ge(n_ok, t + 1)
                        dve.tensor_tensor(a, a, x1[:, t * HID:(t + 1) * HID], ALU.add).then_inc(fin_ok, 1)

                for t in range(N16):
                    acc = x2[:, t * HID:(t + 1) * HID]
                    for k in range(TOPK):
                        i = t * TOPK + k
                        dve.wait_ge(got[i % RING], 16 * (i // RING + 1))
                        if k:
                            dve.wait_ge(used, i)
                        dve.scalar_tensor_tensor(out=acc, in0=yg[:, i % RING, :], scalar=rw[:, t, k:k + 1], in1=acc,
                                                 op0=ALU.mult, op1=ALU.add).then_inc(used, 1)
                    dve.wait_ge(used, (t + 1) * TOPK)
                    dve.bn_stats(st6[:, t, :], acc).then_inc(stat, 1)
                    dve.wait_ge(stat, t + 1)
                    dve.bn_aggr(mv[:, t, :], st6[:, t, :]).then_inc(mv_ok, 1)
                    if t % NT == 0 and t:
                        finish(t // NT - 1)
                finish(BATCH - 1)

            @block.scalar
            def _(act):
                for n in range(BATCH):
                    q = slice(n * NT, (n + 1) * NT)
                    act.wait_ge(mv_ok, NT * (n + 1))
                    act.activation(lnv[:, q], mv[:, q, 1], ACT.Ln, bias=eps_ln[:, 0:1]).then_inc(lnv_ok, 1)
                    act.wait_ge(lnv_ok, n + 1)
                    act.activation(r1[:, q], lnv[:, q], ACT.Exp, scale=-0.5).then_inc(r_ok, 1)

            @block.sync
            def _(sp):
                for n in range(BATCH):
                    sp.wait_ge(fin_ok, NT * (n + 1))
                    sp.dma_start(out[n * SEQ:(n + 1) * SEQ, :].rearrange("(t p) h -> p t h", p=P),
                                 x2[:, n * NT * HID:(n + 1) * NT * HID].rearrange("p (t h) -> p t h", h=HID)
                                 ).then_inc(stored, 16)
                sp.wait_ge(stored, 16 * BATCH)




def mamba_attention_moe(nc, x, winT, conv_w, conv_b, a_log, dt_bias, d_skip, norm_w, woutT, ln1, ln2, wq, wk, wv, wo,
                        cos, sin, gateT, bias_e, weg, weu, wed, wsg, wsu, wsd, out):
    with ExitStack() as ctx:
        sb, _, sem = open_tools(nc, ctx)
        ident = sb("ident", [P, P])
        x1 = sb("x1", [P, BATCH * NT * HID])
        xs = nc.dram_tensor("xs", (TILES_ALL * P, HID), F32, kind="Internal").ap()
        ys = nc.dram_tensor("ys", (TILES_ALL * P, HID), F32, kind="Internal").ap()
        filled, zero_ok = sem("xs_filled"), sem("zero_ok")
        zeros = sb("zeros", [P, 4 * HID])
        n_filled = 16 * (TILES_ALL // 4)
        with nc.Block() as block:
            @block.vector
            def _(dve):
                dve.memset(zeros[:], 0.0).then_inc(zero_ok, 1)

            @block.sync
            def _(sp):
                sp.wait_ge(zero_ok, 1)
                for n in range(TILES_ALL // 4):
                    sp.dma_start(xs[n * 4 * P:(n + 1) * 4 * P, :].rearrange("(p t) h -> p (t h)", p=P),
                                 zeros[:]).then_inc(filled, 16)

        mamba_phase(nc, x, winT, conv_w, conv_b, a_log, dt_bias, d_skip, norm_w, woutT, ident, x1)
        x2 = sb("x2", [P, BATCH * NT * HID])
        attention_phase(nc, wq, wk, wv, wo, ln1, cos, sin, ident, x1, x2)
        moe_phase(nc, ln2, gateT, bias_e, weg, weu, wed, wsg, wsu, wsd, ident, x1, x2, xs, ys, filled, n_filled, out)


def rope_tables(seq, width):
    import numpy as np

    one, theta = np.float32(1.0), np.float32(10000.0)
    freq = one / theta ** (np.arange(0, width, 2, dtype=np.float32) / np.float32(width))
    angle = (np.arange(seq, dtype=np.float32)[:, None] * freq[None, :]).astype(np.float64).T
    c, s = np.cos(angle).astype(np.float32), np.sin(angle).astype(np.float32)
    return np.concatenate([c, c]), np.concatenate([-s, s])


def kernel(**inputs):
    import numpy as np
    import concourse.bacc as bacc
    from concourse.bass_utils import run_bass_kernel_spmd

    a = {k: np.asarray(v) for k, v in inputs.items()}

    def columns(w, n):
        return w.reshape(n, P).T

    def halves(w, heads):
        return w.reshape(HID, heads, D // 2, 2).transpose(0, 1, 3, 2).reshape(HID, heads * D)

    cos, sin = rope_tables(SEQ, D)
    arrays = {
        "x_in": a["L0_attn_hidden_states"].reshape(BATCH * SEQ, HID),
        "winT": a["L0_attn_in_proj_w"].T,
        "conv_w": a["L0_attn_conv_w"].reshape(CONV // P, P, TAPS).transpose(1, 0, 2),
        "conv_b": columns(a["L0_attn_conv_b"], CONV // P),
        "a_log": a["L0_attn_A_log"],
        "dt_bias": a["L0_attn_dt_bias"],
        "d_skip": a["L0_attn_D"],
        "norm_w": columns(a["L0_attn_norm_w"], INTER // P),
        "woutT": a["L0_attn_out_proj_w"].T,
        "ln1": columns(a["L0_ffn_ln1_w"], NK),
        "ln2": columns(a["L0_ffn_ln2_w"], NK),
        "wq": halves(a["L0_ffn_wq"], QH),
        "wk": halves(a["L0_ffn_wk"], KVH),
        "wv": a["L0_ffn_wv"],
        "wo": a["L0_ffn_wo"],
        "cos": cos,
        "sin": sin,
        "gateT": a["L0_ffn_gate_w"].T,
        "bias_e": a["L0_ffn_bias_e"],
        "weg": a["L0_ffn_weg"].reshape(NE * HID, EI),
        "weu": a["L0_ffn_weu"].reshape(NE * HID, EI),
        "wed": a["L0_ffn_wed"].reshape(NE * EI, HID),
        "wsg": a["L0_ffn_wsg"],
        "wsu": a["L0_ffn_wsu"],
        "wsd": a["L0_ffn_wsd"],
    }
    arrays = {f"in_{k}": np.ascontiguousarray(v) for k, v in arrays.items()}
    nc = bacc.Bacc("TRN2", target_bir_lowering=False, num_devices=1)
    args = [nc.dram_tensor(k, v.shape, mybir.dt.from_np(v.dtype), kind="ExternalInput").ap()
            for k, v in arrays.items()]
    args.append(nc.dram_tensor("out", (BATCH * SEQ, HID), F32, kind="ExternalOutput").ap())
    mamba_attention_moe(nc, *args)
    r = run_bass_kernel_spmd(nc, [arrays], core_ids=[0])
    return r.results[0]["out"].reshape(BATCH, SEQ, HID)
```

```python
from contextlib import ExitStack, contextmanager

import concourse.bass as bass
from concourse import mybir

F32 = mybir.dt.float32
BF16 = mybir.dt.bfloat16
F32R = mybir.dt.float32r
ALU = mybir.AluOpType
ACT = mybir.ActivationFunctionType
AX_X = mybir.AxisListType.X
P = 128

BATCH, SEQ, HID = 4, 512, 256
NT = SEQ // P
NK = HID // P
INTER, STATE, HEADS = 512, 128, 32
HD = INTER // HEADS
CONV = INTER + 2 * STATE
TAPS = 4
CH = 64
NCH = SEQ // CH
HG = HEADS // 2
DT0 = INTER + CONV
LN_EPS = 1e-5
RMS_EPS = 1e-6


def open_tools(nc, ctx):
    def sb(name, shape, dt=F32):
        return ctx.enter_context(nc.sbuf_tensor(name, shape, dt))

    def ps(name, shape, dt=F32):
        return ctx.enter_context(nc.psum_tensor(name, shape, dt))

    def sem(name):
        return ctx.enter_context(nc.semaphore(name))

    return sb, ps, sem


def spread(ap, n):
    return ap.rearrange("p (a o) -> p a o", o=1).broadcast_to((ap.shape[0], ap.shape[1], n))


class Sems:

    def __init__(self, sem):
        self.sem, self.all = sem, []

    def __call__(self, name):
        s = self.sem(name)
        self.all.append(s)
        return s


def clear(nc, sems):
    for s in sems.all:
        nc.sync.sem_clear(s)
    nc.all_engine_barrier()


@contextmanager
def turn(nc, sems):
    with nc.Block() as block:
        yield block
    clear(nc, sems)


def mamba_phase(nc, x, winT, conv_w, conv_b, a_log, dt_bias, d_skip, norm_w, woutT, ident, x1):
    with ExitStack() as ctx:
        sb, ps, sem = open_tools(nc, ctx)
        w_in = sb("w_in", [P, NK, DT0 + HEADS])
        w_out = sb("w_out", [P, INTER // P, HID])
        nw = sb("nw", [P, INTER // P])
        cw = sb("cw", [P, CONV // P, TAPS])
        cb = sb("cb", [P, CONV // P])
        alog = sb("alog", [P, HEADS])
        neg_a = sb("neg_a", [P, HEADS])
        dtb = sb("dtb", [P, HEADS])
        dsk = sb("dsk", [P, HEADS])
        tri = sb("tri", [P, P])
        suf = sb("suf", [P, P])
        half = sb("half", [P, 2, P])
        causal = sb("causal", [P, CH])
        segm = sb("segm", [P, CH, P], BF16)
        eps_col = sb("eps_col", [P, 1])
        x_sb = sb("x_sb", [P, NT, HID])
        xn = sb("xn", [P, NT, HID])
        f_st6 = sb("f_st6", [P, NT, 6])
        f_mv = sb("f_mv", [P, NT, 2])
        f_lnv = sb("f_lnv", [P, NT])
        f_rstd = sb("f_rstd", [P, NT])
        xnT = sb("xnT", [P, NK, SEQ])
        bdup = sb("bdup", [P, NCH, 2, CH])
        z = sb("z", [P, NT, HEADS])
        az = sb("az", [P, NT, HEADS])
        et = sb("et", [P, NT, HEADS])
        u = sb("u", [P, NT, HEADS])
        lu = sb("lu", [P, NT, HEADS])
        adl = sb("adl", [P, NT, 2, HG])
        adr = sb("adr", [P, NT, 2, HG])
        xc = sb("xc", [P, CONV // P, SEQ])
        sg = sb("sg", [P, NT, INTER])
        dt = sb("dt", [P, NT, HEADS])
        ad = sb("ad", [P, NT, HEADS])
        adp = sb("adp", [P, 3, NCH * HG], BF16)
        gm = sb("gm", [P, NCH, CH])
        xtok = sb("xtok", [P, NT, INTER])
        btok = sb("btok", [P, NT, STATE])
        c_cur = sb("c_cur", [P, SEQ])
        b_cur = sb("b_cur", [P, NT, STATE])
        dsuf = sb("dsuf", [P, NT, HEADS])
        dec = sb("dec", [P, 4, NT, HEADS])
        es = sb("es", [P, 3, 4, NCH * HG])
        mt = sb("mt", [P, NCH * HG, CH])
        xbd = sb("xbd", [P, NCH, HG, 2 * HD])
        xds = sb("xds", [P, NT, INTER])
        xd = sb("xd", [P, NT, INTER])
        stt = sb("stt", [P, NCH, INTER])
        y = sb("y", [P, NT, INTER])
        dT = xds
        yT = xds
        sq = sb("sq", [P, INTER])
        ssq = sb("ssq", [P, NT])
        o_sb = y[:, :, 0:HID]
        x_res = y[:, :, HID:INTER]
        b_st6 = sb("b_st6", [P, NT, 6])
        b_mv = sb("b_mv", [P, NT, 2])
        b_lnv = sb("b_lnv", [P, NT])
        b_rstd = sb("b_rstd", [P, NT])
        bank = [ps(f"bank{i}", [P, 512]) for i in range(8)]

        s = Sems(sem)
        loaded, w_in_ok, masks, a_ready, folded = s("m_loaded"), s("w_in_ok"), s("m_masks"), s("m_a_ready"), s("m_folded")
        x_in, res_in = s("x_in"), s("res_in")
        pe = s("pe_banks")
        act_free, dve_free = s("act_free"), s("dve_free")
        f_stat, f_mv_ok, f_lnv_ok, f_rstd_ok, xn_ok = s("f_stat"), s("f_mv_ok"), s("f_lnv_ok"), s("f_rstd_ok"), s("xn_ok")
        b_stat, b_mv_ok, b_lnv_ok, b_rstd_ok = s("b_stat"), s("b_mv_ok"), s("b_lnv_ok"), s("b_rstd_ok")
        tap, cid, conv_ok, bdup_ok = s("tap"), s("cid"), s("conv_ok"), s("bdup_ok")
        dts, dts_a, ad_ok, adp_ok = s("dts"), s("dts_a"), s("ad_ok"), s("adp_ok")
        mt_ok = s("mt_ok")
        handed, xbd_ok, xds_ok, xd_ok, dsuf_ok = s("handed"), s("xbd_ok"), s("xds_ok"), s("xd_ok"), s("dsuf_ok")
        carried, state_ok = s("carried"), s("state_ok")
        ych, y_ok, sq_ok = s("ych"), s("y_ok"), s("sq_ok")
        out_ok, och, x1_ok = s("out_ok"), s("och"), s("x1_ok")

        A, V = (act_free, 1), (dve_free, 1)
        CONV_ORDER = (4, 5, 0, 1, 2, 3)
        reader = {"xnT0": A, "xnT1": A, "dt": V, "conv": (tap, TAPS - 1), "gate": A, "bT": A, "g": V, "xT": A,
                  "dec": A, "seg": A, "st": (state_ok, 1), "off": V, "dT": A, "diag": V, "yT": A, "out": (out_ok, 2)}
        FRONT = ("xnT0", "xnT1", "dt", "conv", "gate", "bT", "g", "xT")
        ORDER = [("dec", 0)] + [("seg", i) for i in range(6)] + [("xnT0", 0), ("xnT1", 0), ("seg", 6), ("dt", 0)]
        ORDER += [("seg", 7), ("seg", 8), ("conv", 4), ("seg", 9), ("seg", 10), ("conv", 5)]
        ORDER += [("seg", 11), ("seg", 12), ("conv", 0), ("seg", 13), ("st", 0), ("seg", 14), ("st", 1), ("seg", 15)]
        ORDER += [("st", c) for c in range(2, NCH - 1)] + [("dT", 0), ("off", 0), ("dT", 1), ("diag", 0), ("off", 1)]
        ORDER += [("conv", 1), ("dT", 2), ("diag", 1), ("bT", 0), ("off", 2), ("dT", 3), ("diag", 2), ("conv", 2)]
        ORDER += [("g", 0), ("off", 3), ("diag", 3), ("conv", 3), ("gate", 0), ("gate", 1)]
        ORDER += [("yT", c) for c in range(INTER // P)] + [("gate", 2), ("gate", 3)]
        ORDER += [("out", 0), ("out", 1)] + [("xT", t) for t in range(NT)]

        def stage(back, front, setup=False):
            B, F = back is not None, front is not None
            work = [(n, i) for n, i in ORDER if (F if n in FRONT else B)]
            at = {w: k for k, w in enumerate(work)}

            def read_by(k):
                r = reader[work[k][0]][0]
                return sum(reader[n][1] for n, _ in work[:k + 1] if reader[n][0] is r)

            def where(name, i=0):
                return bank[at[name, i] % 8]

            def fill(eng, name, i=0):
                k = at[name, i] - 8
                if k >= 0:
                    eng.wait_ge(reader[work[k][0]][0], read_by(k))

            def full(eng, name, i=0):
                eng.wait_ge(pe, at[name, i] + 1)

            def free_no(name, i=0):
                return read_by(at[name, i])

            made = {}
            with nc.Block() as block:
                @block.gpsimd
                def _(pool):
                    n = [0]

                    def step(i, name=None):
                        n[0] += 1
                        i.then_inc(masks, 1)
                        pool.wait_ge(masks, n[0])
                        if name:
                            made[name] = n[0]

                    if setup:
                        step(pool.memset(eps_col[:], LN_EPS), "eps")
                        step(pool.memset(ident[:], 0.0))
                        step(pool.affine_select(out=ident[:], in_=ident[:], compare_op=ALU.not_equal, fill=1.0, base=0,
                                                pattern=[[-1, P]], channel_multiplier=1), "ident")
                        step(pool.memset(tri[:], 1.0))
                        step(pool.affine_select(out=tri[:], in_=tri[:], compare_op=ALU.is_ge, fill=0.0, base=0,
                                                pattern=[[1, P]], channel_multiplier=-1))
                        step(pool.memset(tri[0:CH, CH:P], 0.0))
                        for hh in range(2):
                            h = slice(hh * CH, (hh + 1) * CH)
                            step(pool.tensor_copy(causal[h, :], tri[h, h]), "causal")
                        step(pool.memset(suf[:], 1.0))
                        step(pool.affine_select(out=suf[:], in_=suf[:], compare_op=ALU.is_ge, fill=0.0, base=-1,
                                                pattern=[[-1, P]], channel_multiplier=1))
                        step(pool.memset(suf[CH:P, 0:CH], 0.0))
                        step(pool.memset(half[:], 1.0))
                        step(pool.memset(half[0:CH, 1, :], 0.0))
                        step(pool.memset(half[CH:P, 0, :], 0.0))
                        for hh in range(2):
                            v = segm[:, :, hh * CH:(hh + 1) * CH]
                            step(pool.memset(v, 1.0))
                            step(pool.affine_select(out=v, in_=v, compare_op=ALU.is_ge, fill=0.0, base=-1 - CH * hh,
                                                    pattern=[[0, CH], [-1, CH]], channel_multiplier=1))
                            step(pool.affine_select(out=v, in_=v, compare_op=ALU.is_ge, fill=0.0, base=CH * hh,
                                                    pattern=[[1, CH], [0, CH]], channel_multiplier=-1))
                    if B:
                        for q in range(2):
                            for hh in range(2):
                                src = slice(q * CH, (q + 1) * CH)
                                out = xbd[hh * CH:(hh + 1) * CH, :, :, hh * HD:(hh + 1) * HD].rearrange(
                                    "p (t q) g d -> p q t g d", q=2)[:, q]
                                xin = xtok[src, :, hh * 256:(hh + 1) * 256].rearrange("p t (g d) -> p t g d", d=HD)
                                din = dt[src, :, hh * HG:(hh + 1) * HG].rearrange(
                                    "p t (g o) -> p t g o", o=1).broadcast_to((CH, NT, HG, HD))
                                pool.tensor_tensor(out, xin, din, ALU.mult).then_inc(xbd_ok, 1)
                                pool.wait_ge(xbd_ok, 2 * q + hh + 1)
                        pool.wait_ge(dsuf_ok, 1)
                        pool.tensor_tensor(xds[:].rearrange("p t (h d) -> p (t h) d", d=HD),
                                           xtok[:].rearrange("p t (h d) -> p (t h) d", d=HD),
                                           spread(dsuf[:].rearrange("p t h -> p (t h)"), HD), ALU.mult).then_inc(xds_ok, 1)
                        pool.tensor_tensor(xd[:].rearrange("p t (h d) -> p t h d", d=HD),
                                           xtok[:].rearrange("p t (h d) -> p t h d", d=HD),
                                           dsk[:].rearrange("p (o h u) -> p o h u", o=1, u=1).broadcast_to(
                                               (P, NT, HEADS, HD)), ALU.mult).then_inc(xd_ok, 1)

                @block.sync
                def _(sp):
                    if F:
                        sp.dma_start(x_sb[:], x[bass.ds(front * SEQ, SEQ), :].rearrange("(t p) h -> p t h", p=P)
                                     ).then_inc(x_in, 16)
                    if setup:
                        sp.dma_start(w_in[:], winT.rearrange("(k p) n -> p k n", p=P)).then_inc(w_in_ok, 16)
                        sp.dma_start(alog[:], a_log.rearrange("(o h) -> o h", o=1).broadcast_to((P, HEADS))
                                     ).then_inc(loaded, 16)
                        sp.dma_start(cw[:], conv_w).then_inc(loaded, 16)
                        sp.dma_start(cb[:], conv_b).then_inc(loaded, 16)
                        sp.dma_start(nw[:], norm_w).then_inc(loaded, 16)
                        for dst, src in ((dtb, dt_bias), (dsk, d_skip)):
                            sp.dma_start(dst[:], src.rearrange("(o h) -> o h", o=1).broadcast_to((P, HEADS))
                                         ).then_inc(loaded, 16)
                        sp.dma_start(w_out[:], woutT.rearrange("(k p) n -> p k n", p=P)).then_inc(loaded, 16)
                        sp.wait_ge(loaded, 7 * 16)
                    if B:
                        sp.wait_ge(sq_ok, NT)
                        full(sp, "yT", INTER // P - 1)
                        sp.dma_start(x_res, x[bass.ds(back * SEQ, SEQ), :].rearrange("(t p) h -> p t h", p=P)
                                     ).then_inc(res_in, 16)

                @block.tensor
                def _(te):
                    for name, i in work:
                        if name == "xnT0" and setup:
                            te.wait_ge(masks, made["ident"])
                        elif name == "st":
                            te.wait_ge(xds_ok, 1)
                            te.wait_ge(handed, 1)
                        elif name == "dt":
                            te.wait_ge(act_free, free_no("xnT0"))
                            te.wait_ge(act_free, free_no("xnT1"))
                            if setup:
                                te.wait_ge(w_in_ok, 16)
                        elif name == "bT":
                            te.wait_ge(conv_ok, 1)
                        elif name == "g":
                            te.wait_ge(conv_ok, 2)
                            te.wait_ge(bdup_ok, 1)
                        elif name == "xT":
                            te.wait_ge(conv_ok, CONV // P)
                        elif name == "off":
                            te.wait_ge(handed, 2)
                        elif name == "diag":
                            te.wait_ge(act_free, free_no("dT", i))
                        elif name == "dT" and i == 0:
                            te.wait_ge(xbd_ok, 4)
                            te.wait_ge(mt_ok, CH // 4)
                        elif name == "out":
                            te.wait_ge(act_free, free_no("yT", INTER // P - 1))
                        fill(te, name, i)
                        to = where(name, i)

                        if name in ("xnT0", "xnT1"):
                            k = int(name == "xnT1")
                            for t in range(NT):
                                te.wait_ge(xn_ok, t + 1)
                                m = te.transpose(to[:, t * P:(t + 1) * P], xn[:, t, k * P:(k + 1) * P], ident[:])
                        elif name == "dt":
                            for t in range(NT):
                                for k in range(NK):
                                    m = te.matmul(to[:, t * HEADS:(t + 1) * HEADS], xnT[:, k, t * P:(t + 1) * P],
                                                  w_in[:, k, DT0:DT0 + HEADS], start=k == 0, stop=k == NK - 1)
                        elif name == "conv":
                            for k in range(NK):
                                m = te.matmul(to[:], w_in[:, k, INTER + i * P:INTER + (i + 1) * P], xnT[:, k, :],
                                              start=k == 0, stop=k == NK - 1)
                        elif name == "gate":
                            for k in range(NK):
                                m = te.matmul(to[:], xnT[:, k, i * P:(i + 1) * P], w_in[:, k, 0:INTER],
                                              start=k == 0, stop=k == NK - 1)
                        elif name == "bT":
                            for t in range(NT):
                                m = te.transpose(to[:, t * P:(t + 1) * P], xc[:, 4, t * P:(t + 1) * P], ident[:])
                        elif name == "g":
                            for c in range(NCH):
                                m = te.matmul(to[:, c * CH:(c + 1) * CH],
                                              bdup[:, c, :, :].rearrange("p a s -> p (a s)"),
                                              xc[:, 5, c * CH:(c + 1) * CH], start=True, stop=True)
                        elif name == "xT":
                            for c in range(NT):
                                m = te.transpose(to[:, c * P:(c + 1) * P], xc[:, c, i * P:(i + 1) * P], ident[:])
                        elif name == "dec":
                            rhs = ad[:].rearrange("p t h -> p (t h)")
                            te.matmul(to[:, 0:P], tri[:], rhs, start=True, stop=True)
                            te.matmul(to[:, P:2 * P], suf[:], rhs, start=True, stop=True)
                            for q in range(2):
                                m = te.matmul(to[:, (2 + q) * P:(3 + q) * P], half[:, q, :], rhs, start=True, stop=True)
                        elif name == "seg":
                            for j in range(4):
                                for part in range(3):
                                    m = te.matmul(to[:, j * P:(j + 1) * P], segm[:, 4 * i + j, :], adp[:, part, :],
                                                  start=part == 0, stop=part == 2)
                        elif name == "st":
                            h = slice(i % 2 * CH, (i % 2 + 1) * CH)
                            m = te.matmul(to[:], b_cur[h, i // 2, :], xds[h, i // 2, :], start=True, stop=True)
                        elif name == "off":
                            for q in range(2):
                                c = 2 * i + q
                                if c:
                                    te.wait_ge(state_ok, c)
                                m = te.matmul(to[q * CH:(q + 1) * CH, :], c_cur[:, c * CH:(c + 1) * CH],
                                              stt[:, c, :], start=True, stop=True)
                        elif name == "dT":
                            for q in range(2):
                                for g in range(HG):
                                    m = te.matmul(to[g % 4 * 2 * HD:(g % 4 + 1) * 2 * HD,
                                                     g // 4 * P + q * CH:g // 4 * P + (q + 1) * CH],
                                                  xbd[:, 2 * i + q, g, :], mt[:, (2 * i + q) * HG + g, :],
                                                  start=True, stop=True)
                        elif name == "diag":
                            for gg in range(HG // 4):
                                out = to[:].rearrange("p (a g d) -> p g a d", a=2, g=HG)[:, 4 * gg:4 * gg + 4, :, :]
                                m = te.transpose(out, dT[:, i, gg * P:(gg + 1) * P], ident[:])
                        elif name == "yT":
                            for t in range(NT):
                                te.wait_ge(y_ok, t + 1)
                                m = te.transpose(to[:, t * P:(t + 1) * P], y[:, t, i * P:(i + 1) * P], ident[:])
                        elif name == "out":
                            for t in (2 * i, 2 * i + 1):
                                for c in range(INTER // P):
                                    m = te.matmul(to[:, t % 2 * HID:(t % 2 + 1) * HID], yT[:, c, t * P:(t + 1) * P],
                                                  w_out[:, c, :], start=c == 0, stop=c == INTER // P - 1)
                        m.then_inc(pe, 1)

                @block.scalar
                def _(act):
                    def rsqrt(out, v, lnv, logs, ready):
                        act.activation(lnv[:], v, ACT.Ln, bias=eps_col[:, 0:1]).then_inc(logs[0], 1)
                        act.wait_ge(*logs)
                        act.activation(out, lnv[:], ACT.Exp, scale=-0.5).then_inc(ready, 1)

                    def seg(g):
                        full(act, "seg", g)
                        if g >= 3:
                            act.wait_ge(mt_ok, g - 2)
                        act.activation(es[:, g % 3, :, :].rearrange("p l c -> p (l c)"), where("seg", g)[:],
                                       ACT.Exp).then_inc(act_free, 1)

                    def conv(c):
                        full(act, "conv", c)
                        if B and c == 5:
                            act.wait_ge(handed, 2)
                        act.activation(xc[:, c, :], where("conv", c)[:], ACT.Identity, bias=cb[:, c:c + 1],
                                       scale=cw[:, c, TAPS - 1:TAPS]).then_inc(cid, 1)

                    def silu_conv(c):
                        n = CONV_ORDER.index(c)
                        act.wait_ge(tap, 3 * (n + 1))
                        if c == 4:
                            act.activation(bdup[:], xc[:, c, :].rearrange("p (c o s) -> p c o s", c=NCH, o=1)
                                           .broadcast_to((P, NCH, 2, CH)), ACT.Silu).then_inc(bdup_ok, 1)
                            act.wait_ge(bdup_ok, 1)
                        act.activation(xc[:, c, :], xc[:, c, :], ACT.Silu).then_inc(conv_ok, 1)

                    def gate(t):
                        full(act, "gate", t)
                        if B:
                            act.wait_ge(y_ok, t + 1)
                        act.activation(sg[:, t, :], where("gate", t)[:], ACT.Silu).then_inc(act_free, 1)

                    def xT(t):
                        full(act, "xT", t)
                        if B and t == 0:
                            act.wait_ge(xds_ok, 1)
                            act.wait_ge(xbd_ok, 4)
                            act.wait_ge(xd_ok, 1)
                        act.activation(xtok[:, t, :], where("xT", t)[:], ACT.Copy).then_inc(act_free, 1)

                    def within(t):
                        full(act, "dT", t)
                        act.activation(dT[:, t, :], where("dT", t)[:], ACT.Copy).then_inc(act_free, 1)

                    def square(t):
                        act.wait_ge(y_ok, t + 1)
                        if t:
                            act.wait_ge(sq_ok, t)
                        act.activation(sq[:], y[:, t, :], ACT.Square, scale=INTER ** -0.5,
                                       accum_out=ssq[:, t:t + 1]).then_inc(sq_ok, 1)

                    logs_and_exps = "natural_log_exp_and_others"
                    act.preload_act_table_set(logs_and_exps)
                    if B:
                        act.activation(b_cur[:], btok[:], ACT.Copy).then_inc(handed, 1)
                        act.activation(c_cur[:], xc[:, 5, :], ACT.Copy).then_inc(handed, 1)
                        full(act, "dec")
                        act.activation(dec[:].rearrange("p k t h -> p (k t h)"), where("dec")[:],
                                       ACT.Exp).then_inc(act_free, 1)
                        for g in range(3):
                            seg(g)
                    if setup:
                        act.wait_ge(masks, made["eps"])
                    if F:
                        act.wait_ge(f_mv_ok, NT)
                        rsqrt(f_rstd[:], f_mv[:, :, 1], f_lnv, (f_lnv_ok, 1), f_rstd_ok)
                    if B:
                        for g in range(3, 6):
                            seg(g)
                    if F:
                        full(act, "xnT0")
                        act.activation(xnT[:, 0, :], where("xnT0")[:], ACT.Copy).then_inc(act_free, 1)
                        full(act, "xnT1")
                        act.activation(xnT[:, 1, :], where("xnT1")[:], ACT.Copy).then_inc(act_free, 1)
                    if B:
                        for g in range(6, 9):
                            seg(g)
                    if setup:
                        act.wait_ge(loaded, 7 * 16)
                        act.activation(neg_a[:], alog[:], ACT.Exp).then_inc(a_ready, 1)
                    if F:
                        act.wait_ge(dts, 1)
                        act.activation(et[:], az[:], ACT.Exp, scale=-1.0).then_inc(dts_a, 1)
                        conv(4)
                    if B:
                        seg(9)
                        seg(10)
                    if F:
                        conv(5)
                    if B:
                        seg(11)
                        seg(12)
                    if F:
                        conv(0)
                    if B:
                        for g in range(13, 16):
                            seg(g)
                        full(act, "st", NCH - 2)
                        within(0)
                    if F:
                        silu_conv(4)
                        silu_conv(5)
                    if B:
                        within(1)
                    if F:
                        silu_conv(0)
                        conv(1)
                    if B:
                        within(2)
                        square(0)
                    if F:
                        full(act, "bT")
                        if B:
                            act.wait_ge(handed, 1)
                        act.activation(btok[:].rearrange("p t n -> p (t n)"), where("bT")[:],
                                       ACT.Copy).then_inc(act_free, 1)
                    if B:
                        within(3)
                        square(1)
                    if F:
                        silu_conv(1)
                        conv(2)
                    if B:
                        square(2)
                    if F:
                        silu_conv(2)
                        conv(3)
                        gate(0)
                        gate(1)
                    if B:
                        square(3)
                    if F:
                        silu_conv(3)
                    if B:
                        for c in range(INTER // P):
                            full(act, "yT", c)
                            act.activation(yT[:, c, :], where("yT", c)[:], ACT.Copy).then_inc(act_free, 1)
                    if F:
                        gate(2)
                        gate(3)
                    act.preload_act_table_set(logs_and_exps)
                    if B:
                        act.wait_ge(sq_ok, NT)
                        rsqrt(ssq[:], ssq[:], b_lnv, (b_lnv_ok, 1), b_rstd_ok)
                    if F:
                        act.wait_ge(dts, 2)
                        act.activation(lu[:], u[:], ACT.Ln).then_inc(dts_a, 1)
                        for t in range(NT):
                            xT(t)
                    if B:
                        act.wait_ge(b_mv_ok, NT)
                        rsqrt(b_rstd[:], b_mv[:, :, 1], b_lnv, (b_lnv_ok, 2), b_rstd_ok)

                @block.vector
                def _(dve):
                    def mt_part(g):
                        dve.wait_ge(act_free, free_no("seg", g))
                        out = mt[:, :, 4 * g:4 * g + 4].rearrange("p (c g) l -> p c g l", c=NCH)
                        e_ap = es[:, g % 3, :, :].rearrange("p l (c g) -> p c g l", c=NCH)
                        g_ap = gm[:, :, 4 * g:4 * g + 4].rearrange("p c (o l) -> p c o l", o=1).broadcast_to(
                            (P, NCH, HG, 4))
                        dve.tensor_tensor(out, e_ap, g_ap, ALU.mult).then_inc(mt_ok, 1)

                    def taps(c):
                        n = CONV_ORDER.index(c)
                        dve.wait_ge(cid, n + 1)
                        for j in range(1, TAPS):
                            if j > 1:
                                dve.wait_ge(tap, 3 * n + j - 1)
                            dve.scalar_tensor_tensor(out=xc[:, c, j:SEQ], in0=where("conv", c)[:, 0:SEQ - j],
                                                     scalar=cw[:, c, TAPS - 1 - j:TAPS - j], in1=xc[:, c, j:SEQ],
                                                     op0=ALU.mult, op1=ALU.add).then_inc(tap, 1)

                    def state(c):
                        full(dve, "st", c)
                        if c == 0:
                            dve.tensor_copy(stt[:, 1, :], where("st", 0)[:]).then_inc(state_ok, 1)
                        else:
                            dve.wait_ge(state_ok, c)
                            dve.tensor_tensor(stt[:, c + 1, :].rearrange("p (h d) -> p h d", d=HD),
                                              stt[:, c, :].rearrange("p (h d) -> p h d", d=HD),
                                              spread(dec[:, 2 + c % 2, c // 2, :], HD), ALU.mult).then_inc(carried, 1)
                            dve.wait_ge(carried, c)
                            dve.tensor_tensor(stt[:, c + 1, :], stt[:, c + 1, :], where("st", c)[:],
                                              ALU.add).then_inc(state_ok, 1)

                    def gated(t):
                        full(dve, "off", t)
                        if t == 0:
                            dve.wait_ge(xd_ok, 1)
                        dve.tensor_tensor(y[:, t, :].rearrange("p (h d) -> p h d", d=HD),
                                          where("off", t)[:].rearrange("p (h d) -> p h d", d=HD),
                                          spread(dec[:, 0, t, :], HD), ALU.mult).then_inc(dve_free, 1)
                        dve.wait_ge(dve_free, free_no("off", t))
                        dve.tensor_tensor(y[:, t, :], y[:, t, :], xd[:, t, :], ALU.add).then_inc(ych, 1)
                        full(dve, "diag", t)
                        dve.wait_ge(ych, t + 1)
                        dve.tensor_tensor(y[:, t, :], y[:, t, :], where("diag", t)[:], ALU.add).then_inc(dve_free, 1)
                        dve.wait_ge(dve_free, free_no("diag", t))
                        dve.tensor_tensor(y[:, t, :], y[:, t, :], sg[:, t, :], ALU.mult).then_inc(y_ok, 1)

                    if F:
                        dve.wait_ge(x_in, 16)
                        for t in range(NT):
                            dve.bn_stats(f_st6[:, t, :], x_sb[:, t, :]).then_inc(f_stat, 1)
                        for t in range(NT):
                            dve.wait_ge(f_stat, t + 1)
                            dve.bn_aggr(f_mv[:, t, :], f_st6[:, t, :]).then_inc(f_mv_ok, 1)
                    if B:
                        dve.wait_ge(act_free, free_no("dec"))
                        dve.tensor_tensor(dsuf[:], dt[:], dec[:, 1, :, :], ALU.mult).then_inc(dsuf_ok, 1)
                        mt_part(0)
                    if setup:
                        dve.memset(stt[:, 0, :], 0.0)
                    if B:
                        for g in range(1, 4):
                            mt_part(g)
                    if F:
                        dve.wait_ge(f_rstd_ok, 1)
                        for t in range(NT):
                            dve.tensor_scalar(xn[:, t, :], x_sb[:, t, :], f_mv[:, t, 0:1], f_rstd[:, t:t + 1],
                                              ALU.subtract, ALU.mult).then_inc(xn_ok, 1)
                    if B:
                        mt_part(4)
                        mt_part(5)
                        mt_part(6)
                    if setup:
                        dve.wait_ge(loaded, 7 * 16)
                    if F:
                        full(dve, "dt")
                        dve.tensor_tensor(z[:], where("dt")[:, 0:NT * HEADS].rearrange("p (t h) -> p t h", t=NT),
                                          dtb[:].rearrange("p (o h) -> p o h", o=1).broadcast_to((P, NT, HEADS)),
                                          ALU.add).then_inc(dve_free, 1)
                        dve.wait_ge(dve_free, free_no("dt"))
                        dve.scalar_tensor_tensor(out=az[:], in0=z[:], scalar=-1.0, in1=z[:], op0=ALU.mult,
                                                 op1=ALU.max).then_inc(dts, 1)
                    if setup:
                        dve.memset(xbd[:], 0.0)
                    if B:
                        for g in range(7, 11):
                            mt_part(g)
                    if F:
                        taps(4)
                        dve.wait_ge(dts_a, 1)
                        dve.tensor_scalar(u[:], et[:], 1.0, None, ALU.add).then_inc(dts, 1)
                    if B:
                        for g in range(11, 13):
                            mt_part(g)
                    if F:
                        taps(5)
                    if B:
                        for g in range(13, 16):
                            mt_part(g)
                    if F:
                        taps(0)
                    if B:
                        for c in range(NCH - 1):
                            state(c)
                        gated(0)
                        gated(1)
                    if F:
                        taps(1)
                    if B:
                        gated(2)
                    if F:
                        taps(2)
                        dve.wait_ge(dts, 2)
                        dve.scalar_tensor_tensor(out=et[:], in0=u[:], scalar=1.0, in1=et[:], op0=ALU.subtract,
                                                 op1=ALU.subtract)
                        dve.reciprocal(az[:], u[:]).then_inc(dts, 1)
                        dve.wait_ge(dts, 3)
                        dve.tensor_tensor(et[:], et[:], az[:], ALU.mult)
                        full(dve, "g")
                        if B:
                            dve.wait_ge(mt_ok, CH // 4)
                        if setup:
                            dve.wait_ge(masks, made["causal"])
                        dve.tensor_tensor(gm[:], where("g")[:].rearrange("p (c l) -> p c l", c=NCH),
                                          causal[:].rearrange("p (o l) -> p o l", o=1).broadcast_to((P, NCH, CH)),
                                          ALU.mult).then_inc(dve_free, 1)
                    if B:
                        gated(3)
                    if F:
                        taps(3)
                    if setup:
                        dve.wait_ge(a_ready, 1)
                        dve.tensor_scalar(neg_a[:], neg_a[:], -1.0, None, ALU.mult).then_inc(folded, 1)
                        dve.wait_ge(folded, 1)
                    if F:
                        dve.wait_ge(dts_a, 2)
                        if B:
                            dve.wait_ge(dsuf_ok, 1)
                            dve.wait_ge(xbd_ok, 4)
                        dve.scalar_tensor_tensor(out=dt[:], in0=z[:], scalar=0.0, in1=lu[:], op0=ALU.max,
                                                 op1=ALU.add).then_inc(dts, 1)
                        dve.wait_ge(dts, 4)
                        dve.tensor_tensor(dt[:], dt[:], et[:], ALU.subtract).then_inc(dts, 1)
                        dve.wait_ge(dts, 5)
                        dve.tensor_scalar(dt[:], dt[:], 0.0, 100.0, ALU.max, ALU.min).then_inc(dts, 1)
                        dve.wait_ge(dts, 6)
                        if B:
                            full(dve, "dec")
                        dve.tensor_tensor(ad[:], dt[:], neg_a[:].rearrange("p (o h) -> p o h", o=1).broadcast_to(
                            (P, NT, HEADS)), ALU.mult).then_inc(ad_ok, 1)
                        dve.wait_ge(ad_ok, 1)
                        for hh in range(2):
                            for q in range(2):
                                i = dve.tensor_copy(adl[hh * CH:(hh + 1) * CH, :, q, :],
                                                    ad[q * CH:(q + 1) * CH, :, hh * HG:(hh + 1) * HG])
                        i.then_inc(dts, 1)
                        dve.wait_ge(dts, 7)
                        flat = "p t q g -> p (t q g)"
                        if B:
                            full(dve, "seg", CH // 4 - 1)
                        dve.tensor_copy(adp[:, 0, :], adl[:].rearrange(flat)).then_inc(adp_ok, 1)
                        dve.wait_ge(adp_ok, 1)
                        dve.tensor_tensor(adr[:].rearrange(flat), adl[:].rearrange(flat), adp[:, 0, :],
                                          ALU.subtract).then_inc(dts, 1)
                        dve.wait_ge(dts, 8)
                        dve.tensor_copy(adp[:, 1, :], adr[:].rearrange(flat)).then_inc(adp_ok, 1)
                        dve.wait_ge(adp_ok, 2)
                        dve.tensor_tensor(adp[:, 2, :], adr[:].rearrange(flat), adp[:, 1, :],
                                          ALU.subtract).then_inc(adp_ok, 1)
                    if setup:
                        for k in range(INTER // P):
                            dve.tensor_scalar(w_out[:, k, :], w_out[:, k, :], nw[:, k:k + 1], None, ALU.mult)
                    if B:
                        dve.wait_ge(b_rstd_ok, 1)
                        for t in range(NT):
                            full(dve, "out", t // 2)
                            dve.tensor_scalar(o_sb[:, t, :], where("out", t // 2)[:, t % 2 * HID:(t % 2 + 1) * HID],
                                              ssq[:, t:t + 1], None, ALU.mult).then_inc(out_ok, 1)
                        for t in range(NT):
                            dve.wait_ge(out_ok, t + 1)
                            dve.bn_stats(b_st6[:, t, :], o_sb[:, t, :]).then_inc(b_stat, 1)
                        for t in range(NT):
                            dve.wait_ge(b_stat, t + 1)
                            dve.bn_aggr(b_mv[:, t, :], b_st6[:, t, :]).then_inc(b_mv_ok, 1)
                        dve.wait_ge(b_rstd_ok, 2)
                        for t in range(NT):
                            dve.tensor_scalar(o_sb[:, t, :], o_sb[:, t, :], b_mv[:, t, 0:1], b_rstd[:, t:t + 1],
                                              ALU.subtract, ALU.mult).then_inc(och, 1)
                        dve.wait_ge(res_in, 16)
                        for t in range(NT):
                            dve.wait_ge(och, t + 1)
                            dve.tensor_tensor(x1[:, bass.ds(back * (NT * HID) + t * HID, HID)], o_sb[:, t, :],
                                              x_res[:, t, :], ALU.add).then_inc(x1_ok, 1)
            clear(nc, s)

        stage(None, 0, setup=True)
        with nc.Fori(0, BATCH - 1) as b:
            stage(b, b + 1)
        stage(BATCH - 1, None)


QH, KVH, D = 16, 4, 128
GRP = QH // KVH
NE, TOPK, EI = 32, 4, 128
NORM_MIN = 1e-12
NEG = -1e30
PAIRS = NT * (NT + 1) // 2


def attention_phase(nc, wq, wk, wv, wo, ln1, cos, sin, ident, x1, x2, zeros, zero_ok, fill_xs):
    with ExitStack() as ctx:
        sb, ps, sem = open_tools(nc, ctx)
        wq_hl = sb("wq_hl", [P, 2, NK, QH * D], F32R)
        wk_hl = sb("wk_hl", [P, 2, NK, KVH * D], F32R)
        wv_hl = sb("wv_hl", [P, 2, NK, KVH * D], F32R)
        wo_hl = sb("wo_hl", [P, 2, QH, HID], F32R)
        ln1_sb = sb("ln1_sb", [P, NK])
        cos_sb = sb("cos_sb", [P, SEQ])
        sin_sb = sb("sin_sb", [P, SEQ])
        eps_ln = sb("eps_ln", [P, 1])
        eps_rms = sb("eps_rms", [P, 1])
        identb = sb("identb", [P, P], BF16)
        future = sb("future", [P, P], BF16)

        N16 = BATCH * NT
        st6 = sb("a_st6", [P, N16, 6])
        mv = sb("a_mv", [P, N16, 2])
        lnv = sb("a_lnv", [P, N16])
        r1 = sb("r1", [P, N16])
        m2 = sb("m2", [P, N16])
        r2 = sb("r2", [P, N16 + NT])
        xr = sb("xr", [P, NT, HID])
        xT = sb("xT", [P, 2, NK, SEQ], F32R)
        bank = [ps(f"a_bank{i}", [P, 512]) for i in range(8)]

        su = Sems(sem)
        ln1_in, small_in, wkv_in, wq_in, wo_in, masks = (
            su("a_ln1_in"), su("a_small_in"), su("a_wkv_in"), su("a_wq_in"), su("a_wo_in"), su("a_masks"))
        stat, mv_ok, lnv_ok, r_ok, m2_ok = su("a_stat"), su("a_mv_ok"), su("a_lnv_ok"), su("r_ok"), su("m2_ok")
        half_ok = su("a_half_ok")
        hi_ok, h_ok, xr0_ok, xT0_pe, xT0_hi = su("a_hi_ok"), su("h_ok"), su("xr0_ok"), su("xT0_pe"), su("xT0_hi")
        raw_ctx = ctx.enter_context(ExitStack())
        raws = [raw_ctx.enter_context(nc.sbuf_tensor(f"raw{i}", [P, *w.shape[2:]], F32))
                for i, w in enumerate((wk_hl, wv_hl, wq_hl, wo_hl))]
        parts = [(wk_hl, wk, wkv_in, "(k p) n -> p k n"), (wv_hl, wv, wkv_in, "(k p) n -> p k n"),
                 (wq_hl, wq, wq_in, "(k p) n -> p k n"), (wo_hl, wo, wo_in, "(h p) n -> p h n")]
        arrived = {0: 32, 1: 32, 2: 16, 3: 16}
        with nc.Block() as block:
            @block.sync
            def _(sp):
                sp.dma_start(ln1_sb[:], ln1).then_inc(ln1_in, 16)
                for raw, (w, src, arrive, order) in zip(raws, parts):
                    sp.dma_start(raw[:], src.rearrange(order, p=P)).then_inc(arrive, 16)
                for dst, src in ((cos_sb, cos), (sin_sb, sin)):
                    sp.dma_start(dst[:], src).then_inc(small_in, 16)
                sp.wait_ge(small_in, 32)
                fill_xs(sp)

            @block.gpsimd
            def _(pool):
                pool.memset(zeros[:], 0.0).then_inc(zero_ok, 1)
                pool.memset(eps_ln[:], LN_EPS)
                pool.memset(r2[:, N16:], 0.0)
                pool.memset(x2[:, N16 * HID:], 0.0)
                pool.memset(eps_rms[:], RMS_EPS)
                pool.memset(future[:], 0.0)
                pool.memset(identb[:], 0.0).then_inc(masks, 1)
                pool.wait_ge(masks, 1)
                pool.affine_select(out=identb[:], in_=identb[:], compare_op=ALU.not_equal, fill=1.0, base=0,
                                   pattern=[[-1, P]], channel_multiplier=1)
                pool.affine_select(out=future[:], in_=future[:], compare_op=ALU.is_ge, fill=NEG, base=0,
                                   pattern=[[-1, P]], channel_multiplier=1).then_inc(masks, 1)
                pool.wait_ge(masks, 2)
                for i in range(2):
                    pool.wait_ge(hi_ok, i + 1)
                    pool.tensor_tensor(parts[i][0][:, 1, :, :], raws[i][:], parts[i][0][:, 0, :, :].bitcast(F32),
                                       ALU.subtract)
                pool.wait_ge(hi_ok, 3)
                pool.tensor_tensor(wq_hl[:, 1, 0, :], raws[2][:, 0, :], wq_hl[:, 0, 0, :].bitcast(F32), ALU.subtract)
                pool.wait_ge(hi_ok, 5)
                q = slice(0, QH // 4)
                pool.tensor_tensor(wo_hl[:, 1, q, :], raws[3][:, q, :], wo_hl[:, 0, q, :].bitcast(F32), ALU.subtract)

            @block.scalar
            def _(act):
                act.wait_ge(masks, 1)
                for i, (w, _, arrive, _) in enumerate(parts):
                    if i == 1:
                        act.wait_ge(mv_ok, N16)
                        act.activation(lnv[:], mv[:, :, 1], ACT.Ln, bias=eps_ln[:, 0:1]).then_inc(lnv_ok, 1)
                        act.wait_ge(lnv_ok, 1)
                        act.activation(r1[:], lnv[:], ACT.Exp, scale=-0.5).then_inc(r_ok, 1)
                    if i == 2:
                        act.wait_ge(m2_ok, 2)
                        act.activation(lnv[:], m2[:], ACT.Ln, bias=eps_rms[:, 0:1]).then_inc(lnv_ok, 1)
                        act.wait_ge(lnv_ok, 2)
                        act.activation(r2[:, 0:N16], lnv[:], ACT.Exp, scale=-0.5).then_inc(r_ok, 1)
                    if i == 3:
                        act.wait_ge(ln1_in, 16)
                        for k in range(NK):
                            act.wait_ge(xT0_pe, k + 1)
                            act.activation(xT[:, 0, k, :], bank[k][:], ACT.Copy,
                                           scale=ln1_sb[:, k:k + 1]).then_inc(xT0_hi, 1)
                    act.wait_ge(arrive, arrived[i])
                    q = slice(0, QH // 2 if i == 3 else w.shape[2])
                    if i == 2:
                        for k in range(NK):
                            act.activation(w[:, 0, k, :], raws[i][:, k, :], ACT.Copy).then_inc(hi_ok, 1)
                    else:
                        act.activation(w[:, 0, q, :], raws[i][:, q, :], ACT.Copy).then_inc(hi_ok, 1)

            @block.tensor
            def _(te):
                te.wait_ge(xr0_ok, NT)
                for k in range(NK):
                    for t in range(NT):
                        m = te.transpose(bank[k][:, t * P:(t + 1) * P], xr[:, t, k * P:(k + 1) * P], ident[:])
                    m.then_inc(xT0_pe, 1)

            @block.vector
            def _(dve):
                for t in range(N16):
                    dve.bn_stats(st6[:, t, :], x1[:, t * HID:(t + 1) * HID]).then_inc(stat, 1)
                for t in range(N16):
                    dve.wait_ge(stat, t + 1)
                    dve.bn_aggr(mv[:, t, :], st6[:, t, :]).then_inc(mv_ok, 1)
                dve.wait_ge(r_ok, 1)
                dve.tensor_tensor(m2[:], mv[:, :, 1], r1[:], ALU.mult).then_inc(m2_ok, 1)
                dve.wait_ge(m2_ok, 1)
                dve.tensor_tensor(m2[:], m2[:], r1[:], ALU.mult).then_inc(m2_ok, 1)
                for t in range(N16):
                    dve.tensor_scalar(x2[:, t * HID:(t + 1) * HID], x1[:, t * HID:(t + 1) * HID], mv[:, t, 0:1],
                                      r1[:, t:t + 1], ALU.subtract, ALU.mult).then_inc(h_ok, 1)
                dve.wait_ge(r_ok, 2)
                dve.wait_ge(h_ok, NT)
                for t in range(NT):
                    dve.tensor_scalar(xr[:, t, :], x2[:, t * HID:(t + 1) * HID], r2[:, t:t + 1], None,
                                      ALU.mult).then_inc(xr0_ok, 1)
                dve.wait_ge(hi_ok, 4)
                dve.tensor_tensor(wq_hl[:, 1, 1, :], raws[2][:, 1, :], wq_hl[:, 0, 1, :].bitcast(F32), ALU.subtract)
                for k in range(NK):
                    dve.wait_ge(xT0_hi, k + 1)
                    dve.scalar_tensor_tensor(out=xT[:, 1, k, :], in0=bank[k][:], scalar=ln1_sb[:, k:k + 1],
                                             in1=xT[:, 0, k, :].bitcast(F32), op0=ALU.mult, op1=ALU.subtract)
                dve.wait_ge(wo_in, 16)
                q = slice(QH // 2, QH)
                dve.tensor_copy(wo_hl[:, 0, q, :], raws[3][:, q, :]).then_inc(half_ok, 1)
                dve.wait_ge(half_ok, 1)
                dve.tensor_tensor(wo_hl[:, 1, q, :], raws[3][:, q, :], wo_hl[:, 0, q, :].bitcast(F32), ALU.subtract)
                dve.wait_ge(hi_ok, 5)
                q = slice(QH // 4, QH // 2)
                dve.tensor_tensor(wo_hl[:, 1, q, :], raws[3][:, q, :], wo_hl[:, 0, q, :].bitcast(F32), ALU.subtract)
        clear(nc, su)
        raw_ctx.close()

        v = sb("v", [P, NT - 1, KVH * D])
        v0_hl = sb("v0_hl", [P, 2, KVH * D], F32R)
        kT = sb("kT", [P, KVH, SEQ])
        k_hl = sb("k_hl", [P, 2, 2, SEQ], F32R)
        q_hl = sb("q_hl", [P, 2, 2, P], F32R)
        rc = sb("rc", [P, 2, SEQ])
        rs = sb("rs", [P, 2, SEQ])
        qT = sb("qT", [P, 2, SEQ])
        nmax_r = sb("nmax_r", [P, 2, NT])
        nmax = sb("nmax", [P, 2, NT])
        rsum = sb("rsum", [P, 2, NT])
        rrec = sb("rrec", [P, 2, NT])
        pr = sb("pr", [P, 2, PAIRS * P])
        pt = sb("pt", [P, 2, (PAIRS - NT) * P])
        pt0_hl = sb("pt0_hl", [P, 2, 2, SEQ], F32R)
        oT = sb("oT", [P, 2, 2, SEQ], F32R)
        woT = xr[:].rearrange("p t h -> p (t h)").rearrange("p (k s) -> p k s", k=NK)

        s = Sems(sem)
        pe, act_free = s("a_pe"), s("a_act_free")
        xr_ok, hi_ok, lo_ok = s("xr_ok"), s("t_hi_ok"), s("lo_ok")
        k_hi, k_lo, q_part, v_hi, v_lo, pt_hi, pt_lo = (
            s("k_hi"), s("k_lo"), s("q_part"), s("v_hi"), s("v_lo"), s("pt_hi"), s("pt_lo"))
        rot, qk_ok = s("rot"), s("qk_ok")
        mxr = s("mxr")
        mx_ok, e_ok, rec_ok, p_ok = s("mx_ok"), s("e_ok"), s("rec_ok"), s("p_ok")
        pt_a, o_hi, o_lo = s("pt_a"), s("o_hi"), s("o_lo")
        wo_ok, woT_a, woT_v, x2_ok = s("wo_ok"), s("woT_a"), s("woT_v"), s("x2_ok")

        steps = [("k", 0), ("q", 0), ("v", 0), ("kx", 0), ("v", 1), ("q", 1), ("v", 2), ("s", 0), ("k", 1), ("v", 3)]
        for n in range(QH + 2):
            if 2 <= n + 2 < QH:
                steps.append(("q", n + 2))
            if n + 1 < QH:
                steps.append(("s", n + 1))
            if n == 2:
                steps.append(("k", 2))
            if n == 4:
                steps.append(("k", 3))
            if n + 1 == 2:
                steps.append(("kx", 1))
            if n + 1 in (GRP, 2 * GRP):
                steps.append(("kx", (n + 1) // GRP + 1))
            if n + 1 == QH:
                steps += [("x", k) for k in range(NK)]
            if 0 <= n - 1 < QH:
                steps.append(("o", n - 1))
            if n < QH:
                steps.append(("p", n))
            if 0 <= n - 2:
                steps.append(("wo", n - 2))
        jobs = []
        heads = []
        for what, n in steps:
            if what in ("k", "q"):
                jobs += [(what, n, (rot, 3))]
                heads.append((what, n))
            elif what == "x":
                jobs += [("x", n, (lo_ok, 1))]
            elif what == "v":
                jobs += [("v", n, (act_free, 1) if n else (v_lo, 1))]
            elif what == "s":
                jobs += [("s", (n, g), (e_ok, m)) for g, m in ((3, 1), (2, 2), (1, 1))]
            elif what == "p":
                jobs += [("p", (n, 0), (pt_lo, 1)), ("p", (n, 1), (pt_a, 1)), ("p", (n, 2), (pt_a, 1))]
            elif what == "o":
                jobs += [("o", n, (o_lo, 1))]
        jobs += [("wt", i, (x2_ok, 1)) for i in range(NT // 2)]
        RING = 6
        at = {(n, i): k for k, (n, i, _) in enumerate(jobs)}

        def read_by(k):
            return sum(j[2][1] for j in jobs[:k + 1] if j[2][0] is jobs[k][2][0])

        def where(name, i=0):
            return bank[at[name, i] % RING]

        def fill(eng, name, i=0):
            k = at[name, i] - RING
            if k >= 0:
                eng.wait_ge(jobs[k][2][0], read_by(k))

        def full(eng, name, i=0):
            eng.wait_ge(pe, at[name, i] + 1)

        TILES = (3, 2, 0, 1)

        def score_place(n, i):
            b_ = where("s", (n, i if i else 2))
            c0 = 3 * P if i == 0 else 0
            return b_[:, c0:c0 + (i + 1) * P]

        P_AT = {3: 0, 2: 4 * P, 0: 7 * P, 1: 8 * P}
        T_JOB = {0: (0, 0), 1: (1, 0), 3: (1, 3 * P), 2: (2, 0)}
        T_AT = {1: 0, 3: 3 * P, 2: 4 * P}

        with nc.Fori(0, BATCH) as b, turn(nc, s) as block:
            @block.tensor
            def _(te):
                def product(out, stationary, moving, first, last):
                    te.matmul(out, stationary(0), moving(0), start=first, stop=False)
                    te.matmul(out, stationary(0), moving(1), start=False, stop=False)
                    return te.matmul(out, stationary(1), moving(0), start=False, stop=last)

                for what, n in steps:
                    if what == "kx":
                        continue
                    if what in ("k", "q", "v"):
                        fill(te, what, n)
                        w = {"k": wk_hl, "q": wq_hl, "v": wv_hl}[what]
                        for k in range(NK):
                            if what == "v":
                                m = product(where(what, n)[:], lambda a: xT[:, a, k, n * P:(n + 1) * P],
                                            lambda a: w[:, a, k, :], k == 0, k == NK - 1)
                            else:
                                m = product(where(what, n)[:], lambda a: w[:, a, k, n * D:(n + 1) * D],
                                            lambda a: xT[:, a, k, :], k == 0, k == NK - 1)
                        m.then_inc(pe, 1)
                    elif what == "x":
                        fill(te, "x", n)
                        te.wait_ge(xr_ok, NT)
                        for t in range(NT):
                            m = te.transpose(where("x", n)[:, t * P:(t + 1) * P], xr[:, t, n * P:(n + 1) * P], ident[:])
                        m.then_inc(pe, 1)
                    elif what == "s":
                        te.wait_ge(qk_ok, heads.index(("q", n)) + 1)
                        te.wait_ge(qk_ok, heads.index(("k", n // GRP)) + 1)
                        for i in TILES:
                            if i:
                                fill(te, "s", (n, i))
                            out = score_place(n, i)
                            if i == NT - 1:
                                te.wait_ge(k_lo, n // GRP + 1)
                                product(out, lambda a: q_hl[:, n % 2, a, :], lambda a: k_hl[:, n // GRP % 2, a, :], True,
                                        False)
                            else:
                                te.matmul(out, qT[:, n % 2, i * P:(i + 1) * P], kT[:, n // GRP, 0:(i + 1) * P],
                                          start=True, stop=False)
                            m = te.matmul(out[:, i * P:(i + 1) * P], identb[:], future[:], start=False, stop=True)
                            if i != 2:
                                m.then_inc(pe, 1)
                    elif what == "p":
                        te.wait_ge(p_ok, NT * (n + 1))
                        for job, js in ((0, (0,)), (1, (1, 3)), (2, (2,))):
                            fill(te, "p", (n, job))
                            for j in js:
                                for i in range(j, NT):
                                    c = T_JOB[j][1] + (i - j) * P
                                    m = te.transpose(where("p", (n, job))[:, c:c + P],
                                                     pr[:, n % 2, P_AT[i] + j * P:P_AT[i] + (j + 1) * P], ident[:])
                            m.then_inc(pe, 1)
                    elif what == "o":
                        fill(te, "o", n)
                        te.wait_ge(act_free, NT - 1)
                        te.wait_ge(v_lo, 1)
                        te.wait_ge(pt_lo, n + 1)
                        product(where("o", n)[:], lambda a: v0_hl[:, a, n // GRP * D:(n // GRP + 1) * D],
                                lambda a: pt0_hl[:, n % 2, a, :], True, False)
                        te.wait_ge(pt_a, 2 * (n + 1))
                        for j in range(1, NT):
                            m = te.matmul(where("o", n)[:, j * P:SEQ], v[:, j - 1, n // GRP * D:(n // GRP + 1) * D],
                                          pt[:, n % 2, T_AT[j]:T_AT[j] + (NT - j) * P],
                                          start=False, stop=j == NT - 1)
                        m.then_inc(pe, 1)
                    else:
                        te.wait_ge(o_lo, n + 1)
                        for k in range(NK):
                            m = product(bank[RING + k][:], lambda a: wo_hl[:, a, n, k * P:(k + 1) * P],
                                        lambda a: oT[:, n % 2, a, :], n == 0, n == QH - 1)
                        m.then_inc(wo_ok, 1)
                te.wait_ge(woT_a, 1)
                te.wait_ge(woT_v, 1)
                for q in range(NT // 2):
                    fill(te, "wt", q)
                    for t in (2 * q, 2 * q + 1):
                        for k in range(NK):
                            m = te.transpose(where("wt", q)[:, t % 2 * HID + k * P:t % 2 * HID + (k + 1) * P],
                                             woT[:, k, t * P:(t + 1) * P], ident[:])
                    m.then_inc(pe, 1)

            @block.scalar
            def _(act):
                for what, n in steps:
                    if what == "x":
                        full(act, "x", n)
                        act.activation(xT[:, 0, n, :], where("x", n)[:], ACT.Copy,
                                       scale=ln1_sb[:, n:n + 1]).then_inc(hi_ok, 1)
                    elif what == "v":
                        full(act, "v", n)
                        if n:
                            act.activation(v[:, n - 1, :], where("v", n)[:], ACT.Copy).then_inc(act_free, 1)
                        else:
                            act.activation(v0_hl[:, 0, :], where("v", 0)[:], ACT.Copy).then_inc(v_hi, 1)
                    elif what == "kx":
                        act.wait_ge(qk_ok, heads.index(("k", n)) + 1)
                        if n >= 2:
                            full(act, "s", (GRP * (n - 1) - 1, 3))
                        act.activation(k_hl[:, n % 2, 0, :], kT[:, n, :], ACT.Copy).then_inc(k_hi, 1)
                    elif what == "s":
                        for m, i in enumerate(TILES):
                            act.wait_ge(mx_ok, NT * n + (3 if m == 1 else m + 1))
                            if n >= 2 and m == 0:
                                full(act, "p", (n - 2, 2))
                            act.activation(pr[:, n % 2, P_AT[i]:P_AT[i] + (i + 1) * P], score_place(n, i), ACT.Exp,
                                           bias=nmax[:, n % 2, i:i + 1], scale=D ** -0.5,
                                           accum_out=rsum[:, n % 2, i:i + 1]).then_inc(e_ok, 1)
                    elif what == "p":
                        full(act, "p", (n, 0))
                        if n >= 2:
                            full(act, "o", n - 2)
                        act.activation(pt0_hl[:, n % 2, 0, :], where("p", (n, 0))[:], ACT.Copy).then_inc(pt_hi, 1)
                        full(act, "p", (n, 1))
                        act.activation(pt[:, n % 2, T_AT[1]:T_AT[1] + 4 * P], where("p", (n, 1))[:],
                                       ACT.Copy).then_inc(pt_a, 1)
                        full(act, "p", (n, 2))
                        act.activation(pt[:, n % 2, T_AT[2]:T_AT[2] + 2 * P], where("p", (n, 2))[:, 0:2 * P],
                                       ACT.Copy).then_inc(pt_a, 1)
                    elif what == "o":
                        full(act, "o", n)
                        if n >= 2:
                            act.wait_ge(wo_ok, n - 1)
                        act.activation(oT[:, n % 2, 0, :], where("o", n)[:], ACT.Copy).then_inc(o_hi, 1)
                act.wait_ge(wo_ok, QH)
                full(act, "x", NK - 1)
                act.activation(woT[:, 0, :], bank[RING][:], ACT.Copy).then_inc(woT_a, 1)

            @block.vector
            def _(dve):
                def rotate(name, n, m):
                    full(dve, name, n)
                    if m >= 2:
                        dve.wait_ge(qk_ok, m - 1)
                    src = where(name, n)
                    half = P // 2
                    dve.tensor_tensor(rc[:, m % 2, :], src[:], cos_sb[:], ALU.mult).then_inc(rot, 1)
                    dve.tensor_tensor(rs[0:half, m % 2, :], src[half:P, :], sin_sb[0:half, :], ALU.mult).then_inc(rot, 1)
                    dve.tensor_tensor(rs[half:P, m % 2, :], src[0:half, :], sin_sb[half:P, :], ALU.mult).then_inc(rot, 1)

                for what, n in steps:
                    if what == "kx":
                        dve.wait_ge(k_hi, n + 1)
                        if n >= 2:
                            full(dve, "s", (GRP * (n - 1) - 1, 3))
                        dve.tensor_tensor(k_hl[:, n % 2, 1, :], kT[:, n, :], k_hl[:, n % 2, 0, :].bitcast(F32),
                                          ALU.subtract).then_inc(k_lo, 1)
                    elif (what, n) == ("v", 0):
                        dve.wait_ge(v_hi, 1)
                        dve.tensor_tensor(v0_hl[:, 1, :], where("v", 0)[:], v0_hl[:, 0, :].bitcast(F32),
                                          ALU.subtract).then_inc(v_lo, 1)
                    elif what in ("k", "q"):
                        rotate(what, n, heads.index((what, n)))
                        if (what, n) == ("q", QH - 1):
                            for t in range(NT):
                                dve.tensor_scalar(xr[:, t, :], x2[:, bass.ds(b * (NT * HID) + (NT + t) * HID, HID)],
                                                  r2[:, bass.ds(b * NT + NT + t, 1)], None, ALU.mult).then_inc(xr_ok, 1)
                    elif what == "x":
                        dve.wait_ge(hi_ok, n + 1)
                        dve.scalar_tensor_tensor(out=xT[:, 1, n, :], in0=where("x", n)[:], scalar=ln1_sb[:, n:n + 1],
                                                 in1=xT[:, 0, n, :].bitcast(F32), op0=ALU.mult,
                                                 op1=ALU.subtract).then_inc(lo_ok, 1)
                    elif what == "s":
                        for m, i in enumerate(TILES):
                            full(dve, "s", (n, i if i else 2))
                            if n >= 2 and m == 0:
                                dve.wait_ge(e_ok, NT * (n - 1))
                            dve.tensor_reduce(nmax_r[:, n % 2, i:i + 1], score_place(n, i), AX_X, ALU.max,
                                              negate=True).then_inc(mxr, 1)
                            dve.wait_ge(mxr, NT * n + m + 1)
                            dve.tensor_scalar(nmax[:, n % 2, i:i + 1], nmax_r[:, n % 2, i:i + 1], D ** -0.5, None,
                                              ALU.mult).then_inc(mx_ok, 1)
                        for m, i in enumerate(TILES):
                            dve.wait_ge(e_ok, NT * n + m + 1)
                            dve.reciprocal(rrec[:, n % 2, i:i + 1], rsum[:, n % 2, i:i + 1]).then_inc(rec_ok, 1)
                            dve.wait_ge(rec_ok, NT * n + m + 1)
                            a = pr[:, n % 2, P_AT[i]:P_AT[i] + (i + 1) * P]
                            dve.tensor_scalar(a, a, rrec[:, n % 2, i:i + 1], None, ALU.mult).then_inc(p_ok, 1)
                    elif what == "p":
                        dve.wait_ge(pt_hi, n + 1)
                        if n >= 2:
                            full(dve, "o", n - 2)
                        dve.tensor_tensor(pt0_hl[:, n % 2, 1, :], where("p", (n, 0))[:],
                                          pt0_hl[:, n % 2, 0, :].bitcast(F32), ALU.subtract).then_inc(pt_lo, 1)
                    elif what == "o":
                        dve.wait_ge(o_hi, n + 1)
                        if n >= 2:
                            dve.wait_ge(wo_ok, n - 1)
                        dve.tensor_tensor(oT[:, n % 2, 1, :], where("o", n)[:], oT[:, n % 2, 0, :].bitcast(F32),
                                          ALU.subtract).then_inc(o_lo, 1)
                dve.wait_ge(wo_ok, QH)
                full(dve, "x", NK - 1)
                dve.tensor_copy(woT[:, 1, :], bank[RING + 1][:]).then_inc(woT_v, 1)
                for q in range(NT // 2):
                    full(dve, "wt", q)
                    acc = x2[:, bass.ds(b * (NT * HID) + q * 2 * HID, 2 * HID)]
                    dve.tensor_tensor(acc, acc, where("wt", q)[:], ALU.add).then_inc(x2_ok, 1)

            @block.gpsimd
            def _(pool):
                for m, (what, n) in enumerate(heads):
                    pool.wait_ge(rot, 3 * (m + 1))
                    if what == "q" and n >= 2:
                        full(pool, "s", (n - 2, 1))
                    dst = kT[:, n, :] if what == "k" else qT[:, n % 2, :]
                    i = pool.tensor_tensor(dst, rc[:, m % 2, :], rs[:, m % 2, :], ALU.add)
                    if what == "k":
                        i.then_inc(qk_ok, 1)
                        continue
                    i.then_inc(q_part, 1)
                    pool.wait_ge(q_part, 2 * n + 1)
                    last, parts_of = qT[:, n % 2, SEQ - P:], q_hl[:, n % 2, :, :]
                    pool.tensor_copy(parts_of[:, 0, :], last).then_inc(q_part, 1)
                    pool.wait_ge(q_part, 2 * n + 2)
                    pool.tensor_tensor(parts_of[:, 1, :], last, parts_of[:, 0, :].bitcast(F32),
                                       ALU.subtract).then_inc(qk_ok, 1)


N16 = BATCH * NT
TILES_MAX = (BATCH * SEQ * TOPK + NE * (P - 1)) // P
TURN = 48
TILES_ALL = -(-TILES_MAX // TURN) * TURN
LOADS = 4
OUTS = 8
ROW = HID + 1
TOKENS = BATCH * SEQ
YS_ROWS = 1 + TOPK * TOKENS + TILES_ALL * P


def moe_phase(nc, ln2, gateT, bias_e, weg, weu, wed, wsg, wsu, wsd, ident, x1, x2, xs, ys, filled, n_filled, out):
    with ExitStack() as ctx:
        sb, ps, sem = open_tools(nc, ctx)
        U32, I32 = mybir.dt.uint32, mybir.dt.int32
        wgu = sb("wgu", [P, NK, NE, 2 * EI])
        wd = sb("wd", [P, NE, HID])
        ln2_sb = sb("ln2_sb", [P, NK])
        slot_u = sb("slot_u", [P, N16, TOPK], U32)
        spare = sb("spare", [P, TILES_ALL])
        rw = sb("rw", [P, N16, TOPK])
        e_off = sb("e_off", [1, P], I32)
        eps_ln = sb("f_eps_ln", [P, 1])
        bank = [ps(f"f_bank{i}", [P, 512]) for i in range(8)]
        w_s = Sems(sem)
        w_ok = w_s("w_ok")

        route(nc, ctx, sb, sem, bank, ln2_sb, ln2, gateT, bias_e, weg, weu, wed, wsg, wsu, wsd, wgu, wd, w_ok,
              slot_u, spare, rw, e_off, eps_ln, ident, x2, xs, filled, n_filled)
        expert_tiles(nc, sem, bank, wgu, wd, w_ok, ln2_sb, e_off, spare, ident, xs, ys)
        yg = wgu[:].rearrange("p k e i -> p (k e i)").rearrange("p (n k t h) -> p n k t h", n=BATCH, k=TOPK, t=NT)
        combine(nc, sem, yg, rw, eps_ln, x1, x2, ys, out)


def route(nc, ctx, sb, sem, bank, ln2_sb, ln2, gateT, bias_e, weg, weu, wed, wsg, wsu, wsd, wgu, wd, w_ok,
          slot_u, spare, rw, e_off, eps_ln, ident, x2, xs, filled, n_filled):
    I32, U32 = mybir.dt.int32, mybir.dt.uint32
    with ExitStack() as ctx:
        sb, ps, _ = open_tools(nc, ctx)
        xr = sb("r_xr", [P, N16, ROW])
        spare_i = sb("spare_i", [P, TILES_ALL], I32)
        goal_i = sb("goal_i", [P, N16], I32)
        xfT = sb("xfT", [P, NK, BATCH * SEQ])
        gate_sb = sb("gate_sb", [P, NK, NE])
        be_sb = sb("be_sb", [P, NE])
        sg_w = sb("sg_w", [P, NK, EI])
        su_w = sb("su_w", [P, NK, EI])
        sd_w = sb("sd_w", [P, HID])
        eps_rms = sb("f_eps_rms", [P, 1])
        col_i = sb("col_i", [P, NE], I32)
        col_no = sb("col_no", [P, NE])
        row_i = sb("row_i", [P, 1], I32)
        row_no = sb("row_no", [P, 1])
        before = sb("before", [P, P], BF16)
        ones_b = sb("ones_b", [P, P], BF16)
        ones_e = sb("ones_e", [P, NE])
        sq = sb("r_sq", [P, 2, HID])
        ssq = sb("r_ssq", [P, N16])
        lnv = sb("r_lnv", [P, N16])
        st6 = sb("r_st6", [P, N16 // 2, 6])
        mv = sb("r_mv", [P, N16 // 2, 2])
        stat, stat2, ms_ok = sem("r_stat"), sem("r_stat2"), sem("r_ms_ok")
        rr = sb("r_rr", [P, N16])
        lmax = sb("lmax", [P, N16])
        lsum = sb("lsum", [P, N16])
        lrec = sb("lrec", [P, N16])
        lgT_ok, xf_v = sem("lgT_ok"), sem("xf_v")
        pb = sb("pb", [P, N16, NE])
        pbb = sb("pbb", [P, N16, NE])
        top = sb("top", [P, N16, 8])
        topi = sb("topi", [P, N16, 8], U32)
        topf = sb("topf", [P, N16, TOPK])
        oh = sb("oh", [P, TOPK, N16, NE])
        sel = sb("sel", [P, N16, NE])
        sel_b = sb("sel_b", [P, N16 * NE], BF16)
        tiles = sb("tiles", [P, NE])
        tiles_i = sb("tiles_i", [P, NE], I32)
        upto = sb("upto", [P, NE])
        base = sb("base", [P, NE])
        pos = sb("pos", [P, N16, NE])
        prod = sb("prod", [P, N16, NE])
        slot_f = sb("slot_f", [P, N16, TOPK])
        cmp = sb("cmp", [P, NE])
        e_no = sb("e_no", [P, 1])
        sgl = sb("sgl", [P, 2, SEQ])
        hT = sb("hT", [P, 2, SEQ])
        lgT = hT[:, 0, :]

        s = Sems(sem)
        loaded, sh_in, made = s("r_loaded"), s("r_sh_in"), s("r_made")
        pe, sq_ok, lnv_ok, rr_ok, xr_ok, xf_ok = (
            s("r_pe"), s("r_sq_ok"), s("r_lnv_ok"), s("r_rr_ok"), s("r_xr_ok"), s("r_xf_ok"))
        ch, ch_a, sel_ok, slots_ok = s("r_chain"), s("r_chain_a"), s("r_sel_ok"), s("r_slots_ok")
        silu_ok, h_ok, added, scattered, e_col, e_row, goal_ok = (
            s("r_silu"), s("r_h_ok"), s("r_added"), [sem(f"scattered{i}") for i in range(BATCH)], s("r_e_col"), s("r_e_row"),
            s("goal_ok"))
        F = BATCH
        jobs = [("xf", (n, k), (xf_ok, 1)) for n in range(F) for k in range(NK)]
        jobs += [("rt", 0, (ch, 0))]
        jobs += [("pos", 0, (ch, 0)), ("cnt", 0, (ch, 0))]
        at = {(n, i): k for k, (n, i, _) in enumerate(jobs)}

        with nc.Block() as block:
            @block.sync
            def _(sp):
                sp.dma_start(gate_sb[:], gateT.rearrange("(k p) n -> p k n", p=P)).then_inc(loaded, 16)
                sp.dma_start(ln2_sb[:], ln2).then_inc(loaded, 16)
                sp.dma_start(be_sb[:], bias_e.rearrange("(o h) -> o h", o=1).broadcast_to((P, NE))).then_inc(loaded, 16)
                sp.dma_start(sg_w[:], wsg.rearrange("(k p) i -> p k i", p=P)).then_inc(sh_in, 16)
                sp.dma_start(su_w[:], wsu.rearrange("(k p) i -> p k i", p=P)).then_inc(sh_in, 16)
                sp.dma_start(sd_w[:], wsd).then_inc(sh_in, 16)
                for e0 in range(0, NE, 8):
                    for k in range(NK):
                        for j, w in enumerate((weg, weu)):
                            sp.dma_start(wgu[:, k, e0:e0 + 8, j * EI:(j + 1) * EI],
                                         w.rearrange("(e k p) i -> k p e i", k=NK, p=P)[k, :, e0:e0 + 8, :]
                                         ).then_inc(w_ok, 16)
                    sp.dma_start(wd[:, e0:e0 + 8, :],
                                 wed.rearrange("(e p) h -> p e h", p=P)[:, e0:e0 + 8, :]).then_inc(w_ok, 16)
                sp.wait_ge(loaded, 48)
                sp.wait_ge(sh_in, 48)

            @block.gpsimd
            def _(pool):
                pool.memset(eps_ln[:], LN_EPS)
                pool.memset(eps_rms[:], RMS_EPS)
                pool.memset(ones_b[:], 1.0)
                pool.memset(ones_e[:], 1.0)
                pool.memset(before[:], 1.0)
                pool.iota(spare_i[:], pattern=[[P, TILES_ALL]], base=1 + TOPK * TOKENS, channel_multiplier=1)
                pool.iota(goal_i[:], pattern=[[P, N16]], base=1, channel_multiplier=1)
                pool.iota(row_i[:], pattern=[[0, 1]], base=0, channel_multiplier=1)
                pool.iota(col_i[:], pattern=[[1, NE]], base=0, channel_multiplier=0).then_inc(made, 1)
                pool.wait_ge(made, 1)
                pool.tensor_copy(row_no[:], row_i[:])
                pool.tensor_copy(col_no[:], col_i[:])
                pool.tensor_copy(spare[:], spare_i[:])
                pool.tensor_copy(xr[:, :, HID], goal_i[:])
                pool.affine_select(out=before[:], in_=before[:], compare_op=ALU.is_ge, fill=0.0, base=-1,
                                   pattern=[[1, P]], channel_multiplier=-1).then_inc(made, 1)
                pool.wait_ge(filled, n_filled)
                for k in range(TOPK):
                    pool.wait_ge(slots_ok, k + 1)
                    for t in range(N16):
                        if k and t % NT == 0:
                            pool.wait_ge(goal_ok, BATCH * (k - 1) + t // NT + 1)
                        pool.indirect_dma_start(
                            out=xs[:, :], out_offset=bass.IndirectOffsetOnAxis(ap=slot_u[:, t, k:k + 1], axis=0),
                            in_=xr[:, t, :], in_offset=None, bounds_check=None).then_inc(scattered[t // NT], 16)
                for i in range(BATCH):
                    pool.wait_ge(scattered[i], 16 * TOPK * NT)

            @block.tensor
            def _(te):
                for n in range(F):
                    for k in range(NK):
                        for j in range(NT):
                            t = n * NT + j
                            te.wait_ge(xr_ok, t + 1)
                            m = te.transpose(bank[2 * n + k][:, j * P:(j + 1) * P], xr[:, t, k * P:(k + 1) * P], ident[:])
                        m.then_inc(pe, 1)
                te.wait_ge(loaded, 48)
                for n in range(F):
                    te.wait_ge(xf_ok, n + 1)
                    te.wait_ge(xf_v, n + 1)
                    for k in range(NK):
                        m = te.matmul(bank[0][n * NE:(n + 1) * NE, :], gate_sb[:, k, :], xfT[:, k, n * SEQ:(n + 1) * SEQ],
                                      start=k == 0, stop=k == NK - 1)
                m.then_inc(pe, 1)
                te.wait_ge(lgT_ok, 1)
                for t in range(NT):
                    m = te.transpose(bank[1][:, t * P:(t + 1) * P], lgT[:, t * P:(t + 1) * P], ident[:])
                m.then_inc(pe, 1)

                def shared(i, gu):
                    if gu:
                        if i >= 2:
                            te.wait_ge(h_ok, i - 1)
                        for bk, w in ((1 + i % 2, sg_w), (3 + i % 2, su_w)):
                            for k in range(NK):
                                m = te.matmul(bank[bk][:], w[:, k, :], xfT[:, k, i * SEQ:(i + 1) * SEQ],
                                              start=k == 0, stop=k == NK - 1)
                            m.then_inc(pe, 1)
                    else:
                        te.wait_ge(h_ok, i + 1)
                        for q in range(NT // 2):
                            if i:
                                te.wait_ge(added, NT * (i - 1) + 2 * q + 2)
                            for t in range(2):
                                c = (2 * q + t) * P
                                m = te.matmul(bank[5 + q][:, t * HID:(t + 1) * HID], hT[:, i % 2, c:c + P], sd_w[:],
                                              start=True, stop=True)
                            m.then_inc(pe, 1)

                te.wait_ge(sh_in, 48)
                te.wait_ge(ch, 2)
                shared(0, True)
                shared(1, True)
                te.wait_ge(sel_ok, 1)
                te.matmul(bank[0][:], before[:], sel_b[:], start=True, stop=False)
                for d in range(1, N16):
                    te.matmul(bank[0][:, d * NE:], ones_b[:], sel_b[:, 0:(N16 - d) * NE], start=False,
                              stop=d == N16 - 1)
                for t in range(N16):
                    m = te.matmul(bank[7][:, 0:NE], ones_b[:], sel_b[:, t * NE:(t + 1) * NE], start=t == 0,
                                  stop=t == N16 - 1)
                m.then_inc(pe, 1)
                te.wait_ge(e_col, 1)
                te.transpose(bank[7][0:1, 0:P], e_no[:], ident[:]).then_inc(e_row, 1)
                for i in range(F):
                    if i >= 2:
                        shared(i, True)
                    shared(i, False)



            def gu_at(i):
                return {0: (11, 12), 1: (13, 14), 2: (20, 21), 3: (24, 25)}[i]

            def y_at(i, q):
                return {0: 16, 1: 18, 2: 22, 3: 26}[i] + q

            @block.scalar
            def _(act):
                act.wait_ge(made, 1)
                for t in range(N16 // 2):
                    if t >= 2:
                        act.wait_ge(sq_ok, t - 1)
                    act.activation(sq[:, t % 2, :], x2[:, t * HID:(t + 1) * HID], ACT.Square, scale=HID ** -0.5,
                                   accum_out=ssq[:, t:t + 1]).then_inc(sq_ok, 1)
                act.wait_ge(sq_ok, N16 // 2)
                act.wait_ge(ms_ok, 2)
                act.activation(lnv[:], ssq[:], ACT.Ln, bias=eps_rms[:, 0:1]).then_inc(lnv_ok, 1)
                act.wait_ge(lnv_ok, 1)
                act.activation(rr[:], lnv[:], ACT.Exp, scale=-0.5).then_inc(rr_ok, 1)
                act.wait_ge(loaded, 48)
                for n in range(F):
                    for k in range(NK):
                        if k:
                            continue
                        act.wait_ge(pe, 2 * n + k + 1)
                        act.activation(xfT[:, k, n * SEQ:(n + 1) * SEQ], bank[2 * n + k][:], ACT.Copy,
                                       scale=ln2_sb[:, k:k + 1]).then_inc(xf_ok, 1)
                act.wait_ge(pe, 9)
                act.activation(lgT, bank[0][:], ACT.Copy).then_inc(lgT_ok, 1)
                act.wait_ge(ch, 2)
                act.activation(pb[:].rearrange("p t e -> p (t e)"), pbb[:].rearrange("p t e -> p (t e)"),
                               ACT.Exp).then_inc(ch_a, 1)
                for i in range(F):
                    act.wait_ge(pe, gu_at(i)[0])
                    if i >= 2:
                        act.wait_ge(h_ok, i - 1)
                    act.activation(sgl[:, i % 2, :], bank[1 + i % 2][:], ACT.Silu).then_inc(silu_ok, 1)

            @block.vector
            def _(dve):
                n_ch = [0]

                def step(i):
                    n_ch[0] += 1
                    i.then_inc(ch, 1)
                    dve.wait_ge(ch, n_ch[0])

                def per_e(ap):
                    return ap.rearrange("p (o e) -> p o e", o=1).broadcast_to((P, N16, NE))

                for t in range(N16 // 2):
                    dve.bn_stats(st6[:, t, :], x2[:, (N16 // 2 + t) * HID:(N16 // 2 + t + 1) * HID]).then_inc(stat, 1)
                for t in range(N16 // 2):
                    dve.wait_ge(stat, t + 1)
                    dve.bn_aggr(mv[:, t, :], st6[:, t, :]).then_inc(stat2, 1)
                rest = ssq[:, N16 // 2:]
                dve.wait_ge(stat2, N16 // 2)
                dve.tensor_tensor(rest, mv[:, :, 0], mv[:, :, 0], ALU.mult).then_inc(ms_ok, 1)
                dve.wait_ge(ms_ok, 1)
                dve.tensor_tensor(rest, rest, mv[:, :, 1], ALU.add).then_inc(ms_ok, 1)
                dve.wait_ge(rr_ok, 1)
                for t in range(N16):
                    dve.tensor_scalar(xr[:, t, 0:HID], x2[:, t * HID:(t + 1) * HID], rr[:, t:t + 1], None,
                                      ALU.mult).then_inc(xr_ok, 1)
                dve.wait_ge(loaded, 48)
                for n in range(F):
                    dve.wait_ge(pe, 2 * n + 2)
                    dve.tensor_scalar(xfT[:, 1, n * SEQ:(n + 1) * SEQ], bank[2 * n + 1][:], ln2_sb[:, 1:2], None,
                                      ALU.mult).then_inc(xf_v, 1)
                dve.wait_ge(pe, 10)
                logits = bank[1][:].rearrange("p (t n e) -> p n t e", n=BATCH, e=NE)
                by_seq = "p (n t) -> p n t"
                step(dve.tensor_reduce(lmax[:].rearrange(by_seq, n=BATCH), logits, AX_X, ALU.max))
                step(dve.tensor_tensor(pbb[:].rearrange("p (n t) e -> p n t e", n=BATCH), logits,
                                       lmax[:].rearrange("p (n t o) -> p n t o", n=BATCH, o=1).broadcast_to(
                                           (P, BATCH, NT, NE)), ALU.subtract))
                dve.wait_ge(ch_a, 1)
                step(dve.tensor_reduce(lsum[:], pb[:], AX_X, ALU.add))
                step(dve.reciprocal(lrec[:], lsum[:]))
                step(dve.tensor_tensor(pb[:], pb[:], spread(lrec[:], NE), ALU.mult))
                dve.wait_ge(made, 2)
                step(dve.tensor_tensor(pbb[:], pb[:], per_e(be_sb[:]), ALU.add))
                for t in range(N16):
                    i = dve.max(top[:, t, :], pbb[:, t, :])
                step(i)
                for t in range(N16):
                    i = dve.max_index(topi[:, t, :], top[:, t, :], pbb[:, t, :])
                step(i)
                step(dve.tensor_copy(topf[:], topi[:, :, 0:TOPK]))
                for k in range(TOPK):
                    i = dve.tensor_tensor(oh[:, k, :, :], per_e(col_no[:]),
                                          topf[:, :, k:k + 1].broadcast_to((P, N16, NE)), ALU.is_equal)
                step(i)
                step(dve.tensor_tensor(sel[:], oh[:, 0, :, :], oh[:, 1, :, :], ALU.add))
                step(dve.tensor_tensor(sel[:], sel[:], oh[:, 2, :, :], ALU.add))
                dve.tensor_tensor(sel_b[:].rearrange("p (t e) -> p t e", e=NE), sel[:], oh[:, 3, :, :],
                                  ALU.add).then_inc(sel_ok, 1)
                dve.wait_ge(pe, 15)
                step(dve.tensor_scalar(tiles[:], bank[7][:, 0:NE], 1.0 / P, (P - 1.0) / P - 0.5 + 1.0 / 512,
                                       ALU.mult, ALU.add))
                step(dve.tensor_copy(tiles_i[:], tiles[:]))
                step(dve.tensor_copy(tiles[:], tiles_i[:]))
                step(dve.tensor_tensor_scan(upto[:], ones_e[:], tiles[:], 0.0, ALU.mult, ALU.add))
                step(dve.tensor_tensor(base[:], upto[:], tiles[:], ALU.subtract))
                step(dve.tensor_scalar(base[:], base[:], float(P), None, ALU.mult))
                step(dve.tensor_tensor(pos[:], bank[0][:].rearrange("p (t e) -> p t e", e=NE), per_e(base[:]), ALU.add))
                for k in range(TOPK):
                    step(dve.tensor_tensor(prod[:], oh[:, k, :, :], pos[:], ALU.mult))
                    step(dve.tensor_reduce(slot_f[:, :, k], prod[:], AX_X, ALU.add))
                    dve.tensor_copy(slot_u[:, :, k], slot_f[:, :, k]).then_inc(slots_ok, 1)
                step(dve.tensor_scalar(cmp[:], upto[:], row_no[:, 0:1], None, ALU.is_le))
                step(dve.tensor_reduce(e_no[:], cmp[:], AX_X, ALU.add))
                dve.tensor_scalar(e_no[:], e_no[:], NE - 1.0, 2.0 * EI, ALU.min, ALU.mult).then_inc(e_col, 1)
                dve.wait_ge(e_row, 1)
                step(dve.tensor_copy(e_off[:], bank[7][0:1, 0:P]))
                for k in range(TOPK):
                    step(dve.tensor_tensor(prod[:], oh[:, k, :, :], pb[:], ALU.mult))
                    step(dve.tensor_reduce(rw[:, :, k], prod[:], AX_X, ALU.add))
                step(dve.tensor_reduce(lsum[:], rw[:], AX_X, ALU.add))
                step(dve.tensor_scalar(lsum[:], lsum[:], NORM_MIN, None, ALU.max))
                step(dve.reciprocal(lrec[:], lsum[:]))
                step(dve.tensor_tensor(rw[:], rw[:], spread(lrec[:], TOPK), ALU.mult))
                def next_goals(k):
                    for i in range(BATCH):
                        dve.wait_ge(scattered[i], 16 * NT * k)
                        goal = xr[:, i * NT:(i + 1) * NT, HID]
                        dve.tensor_scalar(goal, goal, float(TOKENS), None, ALU.add).then_inc(goal_ok, 1)

                for i in range(F):
                    if i:
                        next_goals(i)
                    dve.wait_ge(pe, gu_at(i)[1])
                    dve.wait_ge(silu_ok, i + 1)
                    if i >= 2:
                        dve.wait_ge(pe, y_at(i - 2, 1))
                    dve.tensor_tensor(hT[:, i % 2, :], sgl[:, i % 2, :], bank[3 + i % 2][:], ALU.mult).then_inc(h_ok, 1)
                    for t in range(NT):
                        dve.wait_ge(pe, y_at(i, t // 2))
                        acc = x2[:, (i * NT + t) * HID:(i * NT + t + 1) * HID]
                        dve.tensor_tensor(acc, acc, bank[5 + t // 2][:, t % 2 * HID:(t % 2 + 1) * HID],
                                          ALU.add).then_inc(added, 1)
        clear(nc, s)


def expert_tiles(nc, sem, bank, wgu, wd, w_ok, ln2_sb, e_off, spare, ident, xs, ys):
    with ExitStack() as ctx:
        sb, _, _ = open_tools(nc, ctx)
        U32 = mybir.dt.uint32
        xin = sb("xin", [P, 2, LOADS, ROW])
        goal_f = sb("goal_f", [P, 2, LOADS])
        goal_u = sb("goal_u", [P, 4, LOADS], U32)
        xT = sb("e_xT", [P, 2, NK, P])
        sg = sb("e_sg", [P, 2, EI])
        hh = sb("e_h", [P, 2, EI])
        hT = sb("e_hT", [P, 2, P])
        yo = sb("yo", [P, OUTS, HID])
        s = Sems(sem)
        x_in = [s(f"e_x_in{i}") for i in range(2)]
        xT_pe, xT_a, xT_v, gu_pe, silu_ok, h_ok, hT_pe, hT_ok, y_pe, y_ok = (
            s("e_xT_pe"), s("e_xT_a"), s("e_xT_v"), s("e_gu_pe"), s("e_silu"), s("e_h_ok"), s("e_hT_pe"),
            s("e_hT_ok"), s("e_y_pe"), s("e_y_ok"))
        goal_t, goal_ok = s("e_goal_t"), s("e_goal_ok")
        stored = [sem(f"e_stored{i}") for i in range(OUTS)]
        b_x, b_gu, b_h, b_y = bank[0:2], bank[2:4], bank[4:6], bank[6:8]

        with nc.Fori(0, TILES_ALL // TURN) as r, turn(nc, s) as block:
            @block.sync
            def _(sp):
                for g in range(TURN // LOADS):
                    if g >= 2:
                        sp.wait_ge(xT_pe, LOADS * (g - 1))
                        sp.wait_ge(goal_ok, g - 1)
                    sp.dma_start(xin[:, g % 2, :, :], xs[bass.ds(r * (TURN * P) + g * LOADS * P, LOADS * P), :]
                                 .rearrange("(t p) h -> p t h", p=P)).then_inc(x_in[g % 2], 16)

            @block.gpsimd
            def _(pool):
                for i in range(TURN):
                    pool.wait_ge(goal_ok, i // LOADS + 1)
                    pool.wait_ge(y_ok, i + 1)
                    pool.indirect_dma_start(
                        out=ys[:, :], out_offset=bass.IndirectOffsetOnAxis(
                            ap=goal_u[:, i // LOADS % 4, i % LOADS:i % LOADS + 1], axis=0),
                        in_=yo[:, i % OUTS, :], in_offset=None, bounds_check=None).then_inc(stored[i % OUTS], 16)
                for i in range(OUTS):
                    pool.wait_ge(stored[i], r * (16 * TURN // OUTS) + 16 * TURN // OUTS)

            @block.tensor
            def _(te):
                te.wait_ge(w_ok, 16 * 5 * (NE // 8))
                off = {}
                for i in range(TURN + 3):
                    if i < TURN:
                        te.wait_ge(x_in[i // LOADS % 2], 16 * (i // LOADS // 2 + 1))
                        if i >= 2:
                            te.wait_ge(xT_a, i - 1)
                            te.wait_ge(xT_v, i - 1)
                        for k in range(NK):
                            m = te.transpose(b_x[i % 2][:, k * P:(k + 1) * P],
                                             xin[:, i // LOADS % 2, i % LOADS, k * P:(k + 1) * P], ident[:])
                        m.then_inc(xT_pe, 1)
                        off[i] = te.value_load(e_off[0:1, bass.ds(r * TURN + i, 1)], min_val=0, max_val=(NE - 1) * 2 * EI)
                    j = i - 1
                    if 0 <= j < TURN:
                        te.wait_ge(xT_a, j + 1)
                        te.wait_ge(xT_v, j + 1)
                        if j >= 2:
                            te.wait_ge(h_ok, j - 1)
                        for k in range(NK):
                            m = te.matmul(b_gu[j % 2][:, 0:2 * EI], xT[:, j % 2, k, :],
                                          wgu[:, k, :, :].rearrange("p e i -> p (e i)")[:, bass.ds(off[j], 2 * EI)],
                                          start=k == 0, stop=k == NK - 1)
                        m.then_inc(gu_pe, 1)
                    j = i - 2
                    if 0 <= j < TURN:
                        te.wait_ge(h_ok, j + 1)
                        if j >= 2:
                            te.wait_ge(hT_ok, j - 1)
                        te.transpose(b_h[j % 2][:, 0:P], hh[:, j % 2, :], ident[:]).then_inc(hT_pe, 1)
                    j = i - 3
                    if 0 <= j < TURN:
                        te.wait_ge(hT_ok, j + 1)
                        if j >= 2:
                            te.wait_ge(y_ok, j - 1)
                        te.matmul(b_y[j % 2][:, 0:HID], hT[:, j % 2, :],
                                  wd[:].rearrange("p e h -> p (e h)")[:, bass.ds(off[j], HID)],
                                  start=True, stop=True).then_inc(y_pe, 1)

            @block.scalar
            def _(act):
                for i in range(TURN + 1):
                    if i < TURN:
                        act.wait_ge(xT_pe, i + 1)
                        if i >= 2:
                            act.wait_ge(gu_pe, i - 1)
                        act.activation(xT[:, i % 2, 0, :], b_x[i % 2][:, 0:P], ACT.Copy,
                                       scale=ln2_sb[:, 0:1]).then_inc(xT_a, 1)
                    j = i - 1
                    if j >= 0:
                        act.wait_ge(gu_pe, j + 1)
                        if j >= 2:
                            act.wait_ge(h_ok, j - 1)
                        act.activation(sg[:, j % 2, :], b_gu[j % 2][:, 0:EI], ACT.Silu).then_inc(silu_ok, 1)

            @block.vector
            def _(dve):
                for i in range(TURN + 3):
                    if i < TURN:
                        if i % LOADS == 0:
                            g = i // LOADS
                            dve.wait_ge(x_in[g % 2], 16 * (g // 2 + 1))
                            if g >= 4:
                                for q in range(LOADS):
                                    n = (g - 4) * LOADS + q
                                    dve.wait_ge(stored[n % OUTS], r * (16 * TURN // OUTS) + 16 * (n // OUTS + 1))
                            goal = xin[:, g % 2, :, HID]
                            dve.tensor_scalar(goal_f[:, g % 2, :], goal, 0.0, None, ALU.is_equal).then_inc(goal_t, 1)
                            dve.wait_ge(goal_t, 3 * g + 1)
                            dve.tensor_tensor(goal_f[:, g % 2, :], goal_f[:, g % 2, :],
                                              spare[:, bass.ds(r * TURN + i, LOADS)], ALU.mult).then_inc(goal_t, 1)
                            dve.wait_ge(goal_t, 3 * g + 2)
                            dve.tensor_tensor(goal_f[:, g % 2, :], goal_f[:, g % 2, :], goal,
                                              ALU.add).then_inc(goal_t, 1)
                            dve.wait_ge(goal_t, 3 * g + 3)
                            dve.tensor_copy(goal_u[:, g % 4, :], goal_f[:, g % 2, :]).then_inc(goal_ok, 1)
                        dve.wait_ge(xT_a, i + 1)
                        if i >= 2:
                            dve.wait_ge(gu_pe, i - 1)
                        dve.tensor_scalar(xT[:, i % 2, 1, :], b_x[i % 2][:, P:2 * P], ln2_sb[:, 1:2], None,
                                          ALU.mult).then_inc(xT_v, 1)
                    j = i - 1
                    if 0 <= j < TURN:
                        dve.wait_ge(silu_ok, j + 1)
                        if j >= 2:
                            dve.wait_ge(hT_pe, j - 1)
                        dve.tensor_tensor(hh[:, j % 2, :], sg[:, j % 2, :], b_gu[j % 2][:, EI:2 * EI],
                                          ALU.mult).then_inc(h_ok, 1)
                    j = i - 2
                    if 0 <= j < TURN:
                        dve.wait_ge(hT_pe, j + 1)
                        if j >= 2:
                            dve.wait_ge(y_pe, j - 1)
                        dve.tensor_copy(hT[:, j % 2, :], b_h[j % 2][:, 0:P]).then_inc(hT_ok, 1)
                    j = i - 3
                    if 0 <= j < TURN:
                        dve.wait_ge(y_pe, j + 1)
                        if j >= OUTS:
                            dve.wait_ge(stored[j % OUTS], r * (16 * TURN // OUTS) + 16 * (j // OUTS))
                        dve.tensor_copy(yo[:, j % OUTS, :], b_y[j % 2][:, 0:HID]).then_inc(y_ok, 1)


def combine(nc, sem, yg, rw, eps_ln, x1, x2, ys, out):
    with ExitStack() as ctx:
        sb, _, _ = open_tools(nc, ctx)
        st6 = sb("c_st6", [P, N16, 6])
        mv = sb("c_mv", [P, N16, 2])
        lnv = sb("c_lnv", [P, N16])
        r1 = sb("c_r1", [P, N16])
        off = sb("c_off", [P, N16])
        off_ok, weighed, fourth = sem("c_off_ok"), sem("weighed"), sem("fourth")
        LAST = TOPK - 1
        s = Sems(sem)
        got = [[s(f"got{i}{k}") for k in range(TOPK)] for i in range(BATCH)]
        used, stat, mv_ok, lnv_ok, r_ok, n_ok, fin_ok, stored = (
            s("used"), s("c_stat"), s("c_mv_ok"), s("c_lnv_ok"), s("c_r_ok"), s("c_n_ok"), s("c_fin"), s("c_stored"))
        with nc.Block() as block:
            @block.vector
            def _(dve):
                def stats(n):
                    for t in range(n * NT, (n + 1) * NT):
                        dve.wait_ge(used, NT * (LAST * n + LAST - 1) + t % NT + 1)
                        dve.bn_stats(st6[:, t, :], x2[:, t * HID:(t + 1) * HID]).then_inc(stat, 1)
                    for t in range(n * NT, (n + 1) * NT):
                        dve.wait_ge(stat, t + 1)
                        dve.bn_aggr(mv[:, t, :], st6[:, t, :]).then_inc(mv_ok, 1)

                def shift(n):
                    q = slice(n * NT, (n + 1) * NT)
                    dve.wait_ge(r_ok, n + 1)
                    dve.scalar_tensor_tensor(out=off[:, q], in0=mv[:, q, 0], scalar=-1.0, in1=r1[:, q], op0=ALU.mult,
                                             op1=ALU.mult).then_inc(off_ok, 1)

                for n in range(BATCH):
                    for k in range(LAST):
                        dve.wait_ge(got[n][k], 16)
                        for t in range(n * NT, (n + 1) * NT):
                            if k == 0:
                                dve.wait_ge(fourth, t + 1)
                            else:
                                dve.wait_ge(used, NT * (LAST * n + k - 1) + t % NT + 1)
                            acc = x2[:, t * HID:(t + 1) * HID]
                            dve.scalar_tensor_tensor(out=acc, in0=yg[:, n, k, t % NT, :], scalar=rw[:, t, k:k + 1],
                                                     in1=acc, op0=ALU.mult, op1=ALU.add).then_inc(used, 1)
                    stats(n)
                    if n:
                        shift(n - 1)
                shift(BATCH - 1)

            @block.scalar
            def _(act):
                def weigh(n):
                    act.wait_ge(got[n][LAST], 16)
                    for t in range(n * NT, (n + 1) * NT):
                        a = yg[:, n, LAST, t % NT, :]
                        act.activation(a, a, ACT.Copy, scale=rw[:, t, LAST:LAST + 1]).then_inc(weighed, 1)

                def norm(n):
                    q = slice(n * NT, (n + 1) * NT)
                    act.wait_ge(mv_ok, NT * (n + 1))
                    act.activation(lnv[:, q], mv[:, q, 1], ACT.Ln, bias=eps_ln[:, 0:1]).then_inc(lnv_ok, 1)
                    act.wait_ge(lnv_ok, n + 1)
                    act.activation(r1[:, q], lnv[:, q], ACT.Exp, scale=-0.5).then_inc(r_ok, 1)
                    act.wait_ge(off_ok, n + 1)
                    for t in range(n * NT, (n + 1) * NT):
                        a = x2[:, t * HID:(t + 1) * HID]
                        act.activation(a, a, ACT.Identity, bias=off[:, t:t + 1], scale=r1[:, t:t + 1]).then_inc(n_ok, 1)

                act.preload_act_table_set("natural_log_exp_and_others")
                weigh(0)
                weigh(1)
                for n in range(BATCH):
                    if n + 2 < BATCH:
                        weigh(n + 2)
                    norm(n)

            @block.gpsimd
            def _(pool):
                def add_last(n):
                    for t in range(n * NT, (n + 1) * NT):
                        pool.wait_ge(weighed, t + 1)
                        a = x2[:, t * HID:(t + 1) * HID]
                        pool.tensor_tensor(a, a, yg[:, n, LAST, t % NT, :], ALU.add).then_inc(fourth, 1)

                add_last(0)
                add_last(1)
                for n in range(BATCH):
                    if n + 2 < BATCH:
                        add_last(n + 2)
                    for t in range(n * NT, (n + 1) * NT):
                        a = x2[:, t * HID:(t + 1) * HID]
                        pool.wait_ge(n_ok, t + 1)
                        pool.tensor_tensor(a, a, x1[:, t * HID:(t + 1) * HID], ALU.add).then_inc(fin_ok, 1)

            @block.sync
            def _(sp):
                for n in range(BATCH):
                    for k in (LAST, *range(LAST)):
                        first = 1 + k * TOKENS + n * SEQ
                        sp.dma_start(yg[:, n, k, :, :], ys[first:first + SEQ, :].rearrange("(t p) h -> p t h", p=P)
                                     ).then_inc(got[n][k], 16)
                for n in range(BATCH):
                    sp.wait_ge(fin_ok, NT * (n + 1))
                    sp.dma_start(out[n * SEQ:(n + 1) * SEQ, :].rearrange("(t p) h -> p t h", p=P),
                                 x2[:, n * NT * HID:(n + 1) * NT * HID].rearrange("p (t h) -> p t h", h=HID)
                                 ).then_inc(stored, 16)
                sp.wait_ge(stored, 16 * BATCH)




def mamba_attention_moe(nc, x, winT, conv_w, conv_b, a_log, dt_bias, d_skip, norm_w, woutT, ln1, ln2, wq, wk, wv, wo,
                        cos, sin, gateT, bias_e, weg, weu, wed, wsg, wsu, wsd, out):
    with ExitStack() as ctx:
        sb, _, sem = open_tools(nc, ctx)
        ident = sb("ident", [P, P])
        x1 = sb("x1", [P, BATCH * NT * HID])
        xs = nc.dram_tensor("xs", (TILES_ALL * P, ROW), F32, kind="Internal").ap()
        ys = nc.dram_tensor("ys", (YS_ROWS, HID), F32, kind="Internal").ap()
        filled, zero_ok = sem("xs_filled"), sem("zero_ok")
        n_filled = 2 * 16
        mamba_phase(nc, x, winT, conv_w, conv_b, a_log, dt_bias, d_skip, norm_w, woutT, ident, x1)
        zeros = sb("zeros", [P, ROW])

        def fill_xs(sp):
            sp.wait_ge(zero_ok, 1)
            for n in range(2):
                rows = TILES_ALL * P // 2
                sp.dma_start(xs[n * rows:(n + 1) * rows, :].rearrange("(p q) h -> p q h", p=P),
                             zeros[:].rearrange("p (o f) -> p o f", o=1).broadcast_to((P, rows // P, ROW))
                             ).then_inc(filled, 16)

        x2 = sb("x2", [P, (BATCH + 1) * NT * HID])
        attention_phase(nc, wq, wk, wv, wo, ln1, cos, sin, ident, x1, x2, zeros, zero_ok, fill_xs)
        moe_phase(nc, ln2, gateT, bias_e, weg, weu, wed, wsg, wsu, wsd, ident, x1, x2, xs, ys, filled, n_filled, out)


def rope_tables(seq, width):
    import numpy as np

    one, theta = np.float32(1.0), np.float32(10000.0)
    freq = one / theta ** (np.arange(0, width, 2, dtype=np.float32) / np.float32(width))
    angle = (np.arange(seq, dtype=np.float32)[:, None] * freq[None, :]).astype(np.float64).T
    c, s = np.cos(angle).astype(np.float32), np.sin(angle).astype(np.float32)
    return np.concatenate([c, c]), np.concatenate([-s, s])


def kernel(**inputs):
    import numpy as np
    import concourse.bacc as bacc
    from concourse.bass_utils import run_bass_kernel_spmd

    a = {k: np.asarray(v) for k, v in inputs.items()}

    def columns(w, n):
        return w.reshape(n, P).T

    def halves(w, heads):
        return w.reshape(HID, heads, D // 2, 2).transpose(0, 1, 3, 2).reshape(HID, heads * D)

    cos, sin = rope_tables(SEQ, D)
    arrays = {
        "x_in": a["L0_attn_hidden_states"].reshape(BATCH * SEQ, HID),
        "winT": a["L0_attn_in_proj_w"].T,
        "conv_w": a["L0_attn_conv_w"].reshape(CONV // P, P, TAPS).transpose(1, 0, 2),
        "conv_b": columns(a["L0_attn_conv_b"], CONV // P),
        "a_log": a["L0_attn_A_log"],
        "dt_bias": a["L0_attn_dt_bias"],
        "d_skip": a["L0_attn_D"],
        "norm_w": columns(a["L0_attn_norm_w"], INTER // P),
        "woutT": a["L0_attn_out_proj_w"].T,
        "ln1": columns(a["L0_ffn_ln1_w"], NK),
        "ln2": columns(a["L0_ffn_ln2_w"], NK),
        "wq": halves(a["L0_ffn_wq"], QH),
        "wk": halves(a["L0_ffn_wk"], KVH),
        "wv": a["L0_ffn_wv"],
        "wo": a["L0_ffn_wo"],
        "cos": cos,
        "sin": sin,
        "gateT": a["L0_ffn_gate_w"].T,
        "bias_e": a["L0_ffn_bias_e"],
        "weg": a["L0_ffn_weg"].reshape(NE * HID, EI),
        "weu": a["L0_ffn_weu"].reshape(NE * HID, EI),
        "wed": a["L0_ffn_wed"].reshape(NE * EI, HID),
        "wsg": a["L0_ffn_wsg"],
        "wsu": a["L0_ffn_wsu"],
        "wsd": a["L0_ffn_wsd"],
    }
    arrays = {f"in_{k}": np.ascontiguousarray(v) for k, v in arrays.items()}
    nc = bacc.Bacc("TRN2", target_bir_lowering=False, num_devices=1)
    args = [nc.dram_tensor(k, v.shape, mybir.dt.from_np(v.dtype), kind="ExternalInput").ap()
            for k, v in arrays.items()]
    args.append(nc.dram_tensor("out", (BATCH * SEQ, HID), F32, kind="ExternalOutput").ap())
    mamba_attention_moe(nc, *args)
    r = run_bass_kernel_spmd(nc, [arrays], core_ids=[0])
    return r.results[0]["out"].reshape(BATCH, SEQ, HID)
```
